# Optimizing a Trainium2 kernel written in Bass

```python
import numpy as np
import jax
import jax.numpy as jnp

def _softmax(x, axis=-1):
    return jax.nn.softmax(x, axis=axis)

def _gelu(x):
    return jax.nn.gelu(x, approximate=True)

def _silu(x):
    return jax.nn.silu(x)

def _sigmoid(x):
    return jax.nn.sigmoid(x)

def _layernorm(x, axis=-1, eps=1e-05):
    m = jnp.mean(x, axis=axis, keepdims=True)
    v = jnp.var(x, axis=axis, keepdims=True)
    return (x - m) / jnp.sqrt(v + eps)

def _scatter_add(tgt, idx, src, axis=0):
    return tgt.at[idx].add(src)

def _segment_sum(src, seg, n):
    return jax.ops.segment_sum(src, seg, n)
kernel_name = 'mk_decoder_postln_d2_seqx_r8_d13cbc'

def setup_inputs(seed: int=0):
    np.random.seed(seed)
    _w = jnp.asarray

    def _rec_inputs():
        import jax
        import jax.numpy as jnp
        _rk = jax.random.key(seed)
        x = 0.0003765 + 1 * jax.random.normal(jax.random.fold_in(_rk, 1), (16, 128, 256), jnp.float32)
        _lenS = 128 - jax.random.randint(jax.random.fold_in(_rk, 7), (16,), 0, max(1, 128 // 4) + 1, jnp.int32)
        _lenS2 = 128 - jax.random.randint(jax.random.fold_in(_rk, 8), (16,), 0, max(1, 128 // 4) + 1, jnp.int32)
        _ctx_2048P = jax.random.normal(jax.random.fold_in(_rk, 11), (16, 16, 256), jnp.float32)
        _ctx_2048c = jax.random.dirichlet(jax.random.fold_in(_rk, 511), 0.3 * jnp.ones((16,), jnp.float32), (16, 128))
        _ctx_2048t = jnp.einsum('bsk,bkd->bsd', _ctx_2048c, _ctx_2048P)
        _ctx_2048t = _ctx_2048t * jax.lax.rsqrt(jnp.mean(jnp.square(_ctx_2048t)) + 1e-12) * 0.953939
        ctx_2048 = -0.000292821 + 1.00034 * (_ctx_2048t + 0.3 * jax.random.normal(jax.random.fold_in(_rk, 611), (16, 128, 256), jnp.float32))
        return (x, ctx_2048)
    x, ctx_2048 = _rec_inputs()

    def _L0_attn_setup():
        import jax, jax.numpy as jnp
        import numpy as np
        import math
        D = 256
        H = 16
        KV = 4
        DH = D // H
        REP = H // KV
        LAMBDA_INIT = 0.8 - 0.6 * math.exp(-0.3 * 0)
        ROPE_BASE = 10000.0
        EPS = 1e-05

        def _rope(x, cos, sin):
            x1, x2 = (x[..., ::2], x[..., 1::2])
            c = cos[None, None]
            s = sin[None, None]
            o1 = x1 * c - x2 * s
            o2 = x1 * s + x2 * c
            return jnp.stack([o1, o2], axis=-1).reshape(x.shape)

        def _forward(x, Wq, Wk, Wv, Wo, lambda_q1, lambda_k1, lambda_q2, lambda_k2, gn_w, gn_b):
            B, T, _ = x.shape
            q = (x @ Wq).reshape(B, T, H, 2 * DH).transpose(0, 2, 1, 3)
            k = (x @ Wk).reshape(B, T, KV, 2 * DH).transpose(0, 2, 1, 3)
            v = (x @ Wv).reshape(B, T, KV, 2 * DH).transpose(0, 2, 1, 3)
            q1, q2 = (q[..., :DH], q[..., DH:])
            k1, k2 = (k[..., :DH], k[..., DH:])
            inv = 1.0 / ROPE_BASE ** (jnp.arange(0, DH, 2, dtype=jnp.float32) / DH)
            freqs = jnp.arange(T, dtype=jnp.float32)[:, None] * inv[None, :]
            cos, sin = (jnp.cos(freqs), jnp.sin(freqs))
            q1, q2 = (_rope(q1, cos, sin), _rope(q2, cos, sin))
            k1, k2 = (_rope(k1, cos, sin), _rope(k2, cos, sin))
            k1 = jnp.repeat(k1, REP, axis=1)
            k2 = jnp.repeat(k2, REP, axis=1)
            v = jnp.repeat(v, REP, axis=1)
            mask = jnp.triu(jnp.full((T, T), -jnp.inf, dtype=x.dtype), k=1)[None, None]
            scale = 1.0 / math.sqrt(DH)
            s1 = jnp.einsum('bhtd,bhsd->bhts', q1, k1) * scale + mask
            s2 = jnp.einsum('bhtd,bhsd->bhts', q2, k2) * scale + mask
            a1 = jax.nn.softmax(s1, axis=-1)
            a2 = jax.nn.softmax(s2, axis=-1)
            lam = jnp.exp(jnp.sum(lambda_q1 * lambda_k1)) - jnp.exp(jnp.sum(lambda_q2 * lambda_k2)) + LAMBDA_INIT
            diff = a1 - lam * a2
            out = jnp.einsum('bhts,bhsd->bhtd', diff, v)
            out = out.transpose(0, 2, 1, 3)
            mean = jnp.mean(out, axis=(1, 3), keepdims=True)
            var = jnp.var(out, axis=(1, 3), keepdims=True)
            out = (out - mean) * jax.lax.rsqrt(var + EPS)
            out = out * gn_w.reshape(1, 1, H, 2 * DH) + gn_b.reshape(1, 1, H, 2 * DH)
            out = out.reshape(B, T, 2 * H * DH) * (1.0 - LAMBDA_INIT)
            return out @ Wo
        key = jax.random.key(seed)
        ks = jax.random.split(key, 12)
        B, T = (1, 256)
        s = 0.02
        return {'x': jax.random.normal(ks[0], (B, T, D), jnp.float32), 'Wq': jax.random.normal(ks[1], (D, 2 * H * DH), jnp.float32) * s, 'Wk': jax.random.normal(ks[2], (D, 2 * KV * DH), jnp.float32) * s, 'Wv': jax.random.normal(ks[3], (D, 2 * KV * DH), jnp.float32) * s, 'Wo': jax.random.normal(ks[4], (2 * H * DH, D), jnp.float32) * s, 'lambda_q1': jax.random.normal(ks[5], (DH,), jnp.float32) * 0.1, 'lambda_k1': jax.random.normal(ks[6], (DH,), jnp.float32) * 0.1, 'lambda_q2': jax.random.normal(ks[7], (DH,), jnp.float32) * 0.1, 'lambda_k2': jax.random.normal(ks[8], (DH,), jnp.float32) * 0.1, 'gn_w': jnp.ones((2 * H * DH,), jnp.float32), 'gn_b': jnp.zeros((2 * H * DH,), jnp.float32)}
    _L0_attn_all = _L0_attn_setup()
    _L0_attn_in = {k: v for k, v in _L0_attn_all.items() if k in ('Wq', 'Wk', 'Wv', 'Wo', 'lambda_q1', 'lambda_k1', 'lambda_q2', 'lambda_k2', 'gn_w', 'gn_b')}
    del _L0_attn_all

    def _L0_xattn_setup():
        import jax, jax.numpy as jnp
        import numpy as np
        key = jax.random.key(seed)
        k1, k2, k3, k4, k5 = jax.random.split(key, 5)
        B, D_MODEL, L = (2, 128, 256)
        HEAD_DIM = 8
        H = D_MODEL // HEAD_DIM
        return {'k': jax.random.normal(k1, (B, D_MODEL, L), dtype=jnp.float32), 'v': jax.random.normal(k2, (B, D_MODEL, L), dtype=jnp.float32), 'q': jax.random.normal(k3, (B, D_MODEL, L), dtype=jnp.float32), 'ssm_kernel': jax.random.normal(k4, (H, L), dtype=jnp.float32), 'D': jax.random.normal(k5, (H,), dtype=jnp.float32), 'head_dim': HEAD_DIM}
    _L0_xattn_all = _L0_xattn_setup()
    _L0_xattn_in = {k: v for k, v in _L0_xattn_all.items() if k in ('ssm_kernel', 'D')}
    del _L0_xattn_all

    def _L0_ffn_setup():
        import jax, jax.numpy as jnp
        import numpy as np
        TOP_K = 2
        key = jax.random.key(seed)
        ks = jax.random.split(key, 4)
        G, S, F, E, H = (4, 256, 256, 8, 256)
        return {'x': jax.random.normal(ks[0], (G, S, F), dtype=jnp.float32), 'router_logits': jax.random.normal(ks[1], (F, E), dtype=jnp.float32) * 0.02, 'gating_einsum': jax.random.normal(ks[2], (E, 2, H, F), dtype=jnp.float32) * 0.02, 'linear': jax.random.normal(ks[3], (E, H, F), dtype=jnp.float32) * 0.02, 'per_expert_scale': jnp.ones((E,), dtype=jnp.float32), 'router_scale': jnp.ones((F,), dtype=jnp.float32)}
    _L0_ffn_all = _L0_ffn_setup()
    _L0_ffn_in = {k: v for k, v in _L0_ffn_all.items() if k in ('router_logits', 'gating_einsum', 'linear', 'per_expert_scale', 'router_scale')}
    del _L0_ffn_all

    def _L1_attn_setup():
        import jax, jax.numpy as jnp
        import numpy as np
        BLOCK = 32
        NUM_HEADS = 16
        HEAD_DIM = 128
        FP4_GRID = jnp.array([0.0, 0.5, 1.0, 1.5, 2.0, 3.0, 4.0, 6.0], dtype=jnp.float32)

        def quantize_to_mxfp4(w, block_size=BLOCK):
            D, F = w.shape
            blocks = w.reshape(D // block_size, block_size, F)
            amax = jnp.max(jnp.abs(blocks), axis=1)
            e = jnp.floor(jnp.log2(jnp.maximum(amax, 1e-12) / 6.0))
            scale = jnp.exp2(e)
            v = blocks / scale[:, None, :]
            idx = jnp.argmin(jnp.abs(jnp.abs(v)[..., None] - FP4_GRID), axis=-1)
            codes = jnp.sign(v) * FP4_GRID[idx]
            return (codes.reshape(D, F).astype(jnp.float32), scale.astype(jnp.float32))

        def _mxfp4_matmul(x, codes, scales, block_size=BLOCK):
            w = codes * jnp.repeat(scales, block_size, axis=0)
            return x @ w
        key = jax.random.key(seed)
        ks = jax.random.split(key, 9)
        B, S, D = (2, 256, 256)
        feat = NUM_HEADS * HEAD_DIM
        x = jax.random.normal(ks[0], (B, S, D), dtype=jnp.float32)

        def make_w(k, din, dout):
            w = jax.random.normal(k, (din, dout), dtype=jnp.float32) * (1.0 / np.sqrt(din))
            return quantize_to_mxfp4(w, BLOCK)
        wq_codes, wq_scales = make_w(ks[1], D, feat)
        wk_codes, wk_scales = make_w(ks[2], D, feat)
        wv_codes, wv_scales = make_w(ks[3], D, feat)
        wo_codes, wo_scales = make_w(ks[4], feat, D)
        bq = jnp.zeros((feat,), jnp.float32)
        bk = jnp.zeros((feat,), jnp.float32)
        bv = jnp.zeros((feat,), jnp.float32)
        bo = jnp.zeros((D,), jnp.float32)
        return {'x': x, 'wq_codes': wq_codes, 'wq_scales': wq_scales, 'bq': bq, 'wk_codes': wk_codes, 'wk_scales': wk_scales, 'bk': bk, 'wv_codes': wv_codes, 'wv_scales': wv_scales, 'bv': bv, 'wo_codes': wo_codes, 'wo_scales': wo_scales, 'bo': bo}
    _L1_attn_all = _L1_attn_setup()
    _L1_attn_in = {k: v for k, v in _L1_attn_all.items() if k in ('wq_codes', 'wq_scales', 'bq', 'wk_codes', 'wk_scales', 'bk', 'wv_codes', 'wv_scales', 'bv', 'wo_codes', 'wo_scales', 'bo')}
    del _L1_attn_all

    def _L1_xattn_setup():
        import jax, jax.numpy as jnp
        import numpy as np

        def _wkv(time_decay, time_first, k, v):
            w = -jnp.exp(time_decay)
            u = time_first
            B, T, C = k.shape
            aa = jnp.zeros((B, C), dtype=k.dtype)
            bb = jnp.zeros((B, C), dtype=k.dtype)
            pp = jnp.full((B, C), -1e+38, dtype=k.dtype)

            def step(carry, kv_t):
                aa, bb, pp = carry
                kt, vt = kv_t
                ww = u + kt
                q = jnp.maximum(pp, ww)
                e1 = jnp.exp(pp - q)
                e2 = jnp.exp(ww - q)
                y_t = (e1 * aa + e2 * vt) / (e1 * bb + e2)
                ww2 = pp + w
                q2 = jnp.maximum(ww2, kt)
                e1b = jnp.exp(ww2 - q2)
                e2b = jnp.exp(kt - q2)
                new_carry = (e1b * aa + e2b * vt, e1b * bb + e2b, q2)
                return (new_carry, y_t)
            ks = jnp.transpose(k, (1, 0, 2))
            vs = jnp.transpose(v, (1, 0, 2))
            _, ys = jax.lax.scan(step, (aa, bb, pp), (ks, vs))
            return jnp.transpose(ys, (1, 0, 2))
        key = jax.random.key(seed)
        k1, k2, k3, k4 = jax.random.split(key, 4)
        B, T, C = (8, 128, 256)
        return {'batch_size': B, 'seq_len': T, 'embedding_dim': C, 'time_decay': jax.random.normal(k1, (C,), dtype=jnp.float32), 'time_first': jax.random.normal(k2, (C,), dtype=jnp.float32), 'k': jax.random.normal(k3, (B, T, C), dtype=jnp.float32), 'v': jax.random.normal(k4, (B, T, C), dtype=jnp.float32)}
    _L1_xattn_all = _L1_xattn_setup()
    _L1_xattn_in = {k: v for k, v in _L1_xattn_all.items() if k in ('time_decay', 'time_first')}
    del _L1_xattn_all

    def _L1_ffn_setup():
        import jax, jax.numpy as jnp
        import numpy as np
        B_, S, D = (4, 512, 256)
        OUT = 256
        E, R = (8, 16)
        ALPHA = 32.0
        SCALING = ALPHA / R
        key = jax.random.key(seed)
        ks = jax.random.split(key, 6)
        x = jax.random.normal(ks[0], (B_, S, D), dtype=jnp.float32)
        W_base = jax.random.normal(ks[1], (OUT, D), dtype=jnp.float32) * D ** (-0.5)
        b_base = jax.random.normal(ks[2], (OUT,), dtype=jnp.float32) * 0.01
        router_W = jax.random.normal(ks[3], (E, D), dtype=jnp.float32) * D ** (-0.5)
        A = jax.random.normal(ks[4], (E, R, D), dtype=jnp.float32) * D ** (-0.5)
        Bw = jax.random.normal(ks[5], (E, OUT, R), dtype=jnp.float32) * 0.02
        return {'x': x, 'W_base': W_base, 'b_base': b_base, 'router_W': router_W, 'A': A, 'Bw': Bw}
    _L1_ffn_all = _L1_ffn_setup()
    _L1_ffn_in = {k: v for k, v in _L1_ffn_all.items() if k in ('W_base', 'b_base', 'router_W', 'A', 'Bw')}
    del _L1_ffn_all
    return {'x': x, 'ctx_2048': ctx_2048, 'L0_attn_Wq': _L0_attn_in['Wq'], 'L0_attn_Wk': _L0_attn_in['Wk'], 'L0_attn_Wv': _L0_attn_in['Wv'], 'L0_attn_Wo': _L0_attn_in['Wo'], 'L0_attn_lambda_q1': _L0_attn_in['lambda_q1'], 'L0_attn_lambda_k1': _L0_attn_in['lambda_k1'], 'L0_attn_lambda_q2': _L0_attn_in['lambda_q2'], 'L0_attn_lambda_k2': _L0_attn_in['lambda_k2'], 'L0_attn_gn_w': _L0_attn_in['gn_w'], 'L0_attn_gn_b': _L0_attn_in['gn_b'], 'L0_xattn_ssm_kernel': _L0_xattn_in['ssm_kernel'], 'L0_xattn_D': _L0_xattn_in['D'], 'L0_ffn_router_logits': _L0_ffn_in['router_logits'], 'L0_ffn_gating_einsum': _L0_ffn_in['gating_einsum'], 'L0_ffn_linear': _L0_ffn_in['linear'], 'L0_ffn_per_expert_scale': _L0_ffn_in['per_expert_scale'], 'L0_ffn_router_scale': _L0_ffn_in['router_scale'], 'L1_attn_wq_codes': _L1_attn_in['wq_codes'], 'L1_attn_wq_scales': _L1_attn_in['wq_scales'], 'L1_attn_bq': _L1_attn_in['bq'], 'L1_attn_wk_codes': _L1_attn_in['wk_codes'], 'L1_attn_wk_scales': _L1_attn_in['wk_scales'], 'L1_attn_bk': _L1_attn_in['bk'], 'L1_attn_wv_codes': _L1_attn_in['wv_codes'], 'L1_attn_wv_scales': _L1_attn_in['wv_scales'], 'L1_attn_bv': _L1_attn_in['bv'], 'L1_attn_wo_codes': _L1_attn_in['wo_codes'], 'L1_attn_wo_scales': _L1_attn_in['wo_scales'], 'L1_attn_bo': _L1_attn_in['bo'], 'L1_xattn_time_decay': _L1_xattn_in['time_decay'], 'L1_xattn_time_first': _L1_xattn_in['time_first'], 'L1_ffn_W_base': _L1_ffn_in['W_base'], 'L1_ffn_b_base': _L1_ffn_in['b_base'], 'L1_ffn_router_W': _L1_ffn_in['router_W'], 'L1_ffn_A': _L1_ffn_in['A'], 'L1_ffn_Bw': _L1_ffn_in['Bw']}

def reference(x, ctx_2048, L0_attn_Wq, L0_attn_Wk, L0_attn_Wv, L0_attn_Wo, L0_attn_lambda_q1, L0_attn_lambda_k1, L0_attn_lambda_q2, L0_attn_lambda_k2, L0_attn_gn_w, L0_attn_gn_b, L0_xattn_ssm_kernel, L0_xattn_D, L0_ffn_router_logits, L0_ffn_gating_einsum, L0_ffn_linear, L0_ffn_per_expert_scale, L0_ffn_router_scale, L1_attn_wq_codes, L1_attn_wq_scales, L1_attn_bq, L1_attn_wk_codes, L1_attn_wk_scales, L1_attn_bk, L1_attn_wv_codes, L1_attn_wv_scales, L1_attn_bv, L1_attn_wo_codes, L1_attn_wo_scales, L1_attn_bo, L1_xattn_time_decay, L1_xattn_time_first, L1_ffn_W_base, L1_ffn_b_base, L1_ffn_router_W, L1_ffn_A, L1_ffn_Bw):
    import jax
    import jax.numpy as jnp

    def _L0_attn_ref(x, Wq, Wk, Wv, Wo, lambda_q1, lambda_k1, lambda_q2, lambda_k2, gn_w, gn_b):
        import jax, jax.numpy as jnp
        import numpy as np
        import math
        D = 256
        H = 16
        KV = 4
        DH = D // H
        REP = H // KV
        LAMBDA_INIT = 0.8 - 0.6 * math.exp(-0.3 * 0)
        ROPE_BASE = 10000.0
        EPS = 1e-05

        def _rope(x, cos, sin):
            x1, x2 = (x[..., ::2], x[..., 1::2])
            c = cos[None, None]
            s = sin[None, None]
            o1 = x1 * c - x2 * s
            o2 = x1 * s + x2 * c
            return jnp.stack([o1, o2], axis=-1).reshape(x.shape)

        def _forward(x, Wq, Wk, Wv, Wo, lambda_q1, lambda_k1, lambda_q2, lambda_k2, gn_w, gn_b):
            B, T, _ = x.shape
            q = (x @ Wq).reshape(B, T, H, 2 * DH).transpose(0, 2, 1, 3)
            k = (x @ Wk).reshape(B, T, KV, 2 * DH).transpose(0, 2, 1, 3)
            v = (x @ Wv).reshape(B, T, KV, 2 * DH).transpose(0, 2, 1, 3)
            q1, q2 = (q[..., :DH], q[..., DH:])
            k1, k2 = (k[..., :DH], k[..., DH:])
            inv = 1.0 / ROPE_BASE ** (jnp.arange(0, DH, 2, dtype=jnp.float32) / DH)
            freqs = jnp.arange(T, dtype=jnp.float32)[:, None] * inv[None, :]
            cos, sin = (jnp.cos(freqs), jnp.sin(freqs))
            q1, q2 = (_rope(q1, cos, sin), _rope(q2, cos, sin))
            k1, k2 = (_rope(k1, cos, sin), _rope(k2, cos, sin))
            k1 = jnp.repeat(k1, REP, axis=1)
            k2 = jnp.repeat(k2, REP, axis=1)
            v = jnp.repeat(v, REP, axis=1)
            mask = jnp.triu(jnp.full((T, T), -jnp.inf, dtype=x.dtype), k=1)[None, None]
            scale = 1.0 / math.sqrt(DH)
            s1 = jnp.einsum('bhtd,bhsd->bhts', q1, k1) * scale + mask
            s2 = jnp.einsum('bhtd,bhsd->bhts', q2, k2) * scale + mask
            a1 = jax.nn.softmax(s1, axis=-1)
            a2 = jax.nn.softmax(s2, axis=-1)
            lam = jnp.exp(jnp.sum(lambda_q1 * lambda_k1)) - jnp.exp(jnp.sum(lambda_q2 * lambda_k2)) + LAMBDA_INIT
            diff = a1 - lam * a2
            out = jnp.einsum('bhts,bhsd->bhtd', diff, v)
            out = out.transpose(0, 2, 1, 3)
            mean = jnp.mean(out, axis=(1, 3), keepdims=True)
            var = jnp.var(out, axis=(1, 3), keepdims=True)
            out = (out - mean) * jax.lax.rsqrt(var + EPS)
            out = out * gn_w.reshape(1, 1, H, 2 * DH) + gn_b.reshape(1, 1, H, 2 * DH)
            out = out.reshape(B, T, 2 * H * DH) * (1.0 - LAMBDA_INIT)
            return out @ Wo
        return _forward(x, Wq, Wk, Wv, Wo, lambda_q1, lambda_k1, lambda_q2, lambda_k2, gn_w, gn_b)

    def _L0_xattn_ref(k, v, q, ssm_kernel, D, head_dim):
        import jax, jax.numpy as jnp
        import numpy as np
        B, HD, L = k.shape
        H = HD // head_dim
        fft_size = 2 * L
        k_ = k.reshape(B, H, head_dim, L)
        v_ = v.reshape(B, H, head_dim, L)
        q_ = q.reshape(B, H, head_dim, L)
        kv = jnp.einsum('bhil,bhjl->bijhl', k_, v_)
        kv_f = jnp.fft.rfft(kv, n=fft_size)
        kernel_f = jnp.fft.rfft(ssm_kernel, n=fft_size)
        y = jnp.fft.irfft(kv_f * kernel_f, n=fft_size)[..., :L]
        out = y + kv * D[None, None, None, :, None]
        out = jnp.einsum('bijhl,bhil->bjhl', out, q_)
        out = jnp.transpose(out, (0, 2, 1, 3)).reshape(B, H * head_dim, L)
        return out.astype(k.dtype)

    def _L0_ffn_ref(x, router_logits, gating_einsum, linear, per_expert_scale, router_scale):
        import jax, jax.numpy as jnp
        import numpy as np
        TOP_K = 2
        G, S, F = x.shape
        E = router_logits.shape[-1]
        H = linear.shape[1]
        k = TOP_K
        dtype = x.dtype
        var = jnp.mean(jnp.square(x.astype(jnp.float32)), axis=-1, keepdims=True)
        router_input = x * jax.lax.rsqrt(var + 1e-06).astype(dtype)
        root_size = jax.lax.rsqrt(jnp.array(F, dtype=dtype))
        router_input = router_input * root_size * router_scale.astype(dtype)
        logits = jnp.einsum('gsd,de->gse', router_input, router_logits.astype(dtype))
        logits32 = logits.astype(jnp.float32)
        probs = jax.nn.softmax(logits32, axis=-1)
        _, choices = jax.lax.approx_max_k(logits32, k=k)
        indicator = jax.nn.one_hot(choices, E, dtype=probs.dtype).sum(axis=-2)
        renorm = jnp.sum(indicator * probs, axis=-1, keepdims=True)
        renorm = jnp.where(renorm > 0.0, renorm, 1.0)
        weights = probs / renorm
        x_flat = x.reshape((-1, F))
        batch_size = G * S
        choices_flat = choices.ravel()
        xs_order = choices_flat.argsort()
        xs_reverse_argsort = xs_order.argsort()
        xs_indices = jnp.repeat(jnp.arange(batch_size), k)[xs_order]
        sorted_xs = x_flat[xs_indices, :]
        choices_oh = jax.nn.one_hot(choices, num_classes=E, dtype=jnp.int32)
        tokens_per_expert = jnp.sum(choices_oh, axis=(0, 1, 2))
        combine_weights = (choices_oh.astype(jnp.float32) * jnp.expand_dims(weights, axis=2)).sum(axis=-1).astype(weights.dtype)
        w_gate = jnp.transpose(gating_einsum, (0, 3, 1, 2)).reshape(E, F, 2 * H)
        gate_out = jax.lax.ragged_dot(sorted_xs, w_gate.astype(dtype), group_sizes=tokens_per_expert)
        gate_out = gate_out.reshape(gate_out.shape[0], 2, H)
        activation = jax.nn.gelu(gate_out[:, 0, :]) * gate_out[:, 1, :]
        expert_outputs = jax.lax.ragged_dot(activation, linear.astype(dtype), group_sizes=tokens_per_expert)
        expert_indices = jnp.repeat(jnp.arange(E), tokens_per_expert, total_repeat_length=expert_outputs.shape[0])
        expert_outputs = expert_outputs * per_expert_scale.astype(expert_outputs.dtype)[expert_indices, None]
        out = expert_outputs[xs_reverse_argsort].reshape((G, S, k, -1))
        out = jnp.einsum('blkd,blk->bld', out, combine_weights, preferred_element_type=out.dtype)
        return out

    def _L1_attn_ref(x, wq_codes, wq_scales, bq, wk_codes, wk_scales, bk, wv_codes, wv_scales, bv, wo_codes, wo_scales, bo):
        import jax, jax.numpy as jnp
        import numpy as np
        BLOCK = 32
        NUM_HEADS = 16
        HEAD_DIM = 128
        FP4_GRID = jnp.array([0.0, 0.5, 1.0, 1.5, 2.0, 3.0, 4.0, 6.0], dtype=jnp.float32)

        def quantize_to_mxfp4(w, block_size=BLOCK):
            D, F = w.shape
            blocks = w.reshape(D // block_size, block_size, F)
            amax = jnp.max(jnp.abs(blocks), axis=1)
            e = jnp.floor(jnp.log2(jnp.maximum(amax, 1e-12) / 6.0))
            scale = jnp.exp2(e)
            v = blocks / scale[:, None, :]
            idx = jnp.argmin(jnp.abs(jnp.abs(v)[..., None] - FP4_GRID), axis=-1)
            codes = jnp.sign(v) * FP4_GRID[idx]
            return (codes.reshape(D, F).astype(jnp.float32), scale.astype(jnp.float32))

        def _mxfp4_matmul(x, codes, scales, block_size=BLOCK):
            w = codes * jnp.repeat(scales, block_size, axis=0)
            return x @ w
        B, S, D = x.shape
        q = _mxfp4_matmul(x, wq_codes, wq_scales) + bq
        k = _mxfp4_matmul(x, wk_codes, wk_scales) + bk
        v = _mxfp4_matmul(x, wv_codes, wv_scales) + bv
        q = q.reshape(B, S, NUM_HEADS, HEAD_DIM)
        k = k.reshape(B, S, NUM_HEADS, HEAD_DIM)
        v = v.reshape(B, S, NUM_HEADS, HEAD_DIM)
        scores = jnp.einsum('bqhd,bkhd->bhqk', q, k) / jnp.sqrt(jnp.float32(HEAD_DIM))
        attn = jax.nn.softmax(scores, axis=-1)
        out = jnp.einsum('bhqk,bkhd->bqhd', attn, v).reshape(B, S, NUM_HEADS * HEAD_DIM)
        return _mxfp4_matmul(out, wo_codes, wo_scales) + bo

    def _L1_xattn_ref(batch_size, seq_len, embedding_dim, time_decay, time_first, k, v):
        import jax, jax.numpy as jnp
        import numpy as np

        def _wkv(time_decay, time_first, k, v):
            w = -jnp.exp(time_decay)
            u = time_first
            B, T, C = k.shape
            aa = jnp.zeros((B, C), dtype=k.dtype)
            bb = jnp.zeros((B, C), dtype=k.dtype)
            pp = jnp.full((B, C), -1e+38, dtype=k.dtype)

            def step(carry, kv_t):
                aa, bb, pp = carry
                kt, vt = kv_t
                ww = u + kt
                q = jnp.maximum(pp, ww)
                e1 = jnp.exp(pp - q)
                e2 = jnp.exp(ww - q)
                y_t = (e1 * aa + e2 * vt) / (e1 * bb + e2)
                ww2 = pp + w
                q2 = jnp.maximum(ww2, kt)
                e1b = jnp.exp(ww2 - q2)
                e2b = jnp.exp(kt - q2)
                new_carry = (e1b * aa + e2b * vt, e1b * bb + e2b, q2)
                return (new_carry, y_t)
            ks = jnp.transpose(k, (1, 0, 2))
            vs = jnp.transpose(v, (1, 0, 2))
            _, ys = jax.lax.scan(step, (aa, bb, pp), (ks, vs))
            return jnp.transpose(ys, (1, 0, 2))
        assert seq_len <= 128
        return _wkv(time_decay, time_first, k, v)

    def _L1_ffn_ref(x, W_base, b_base, router_W, A, Bw):
        import jax, jax.numpy as jnp
        import numpy as np
        B_, S, D = (4, 512, 256)
        OUT = 256
        E, R = (8, 16)
        ALPHA = 32.0
        SCALING = ALPHA / R
        base_out = jnp.einsum('bsd,od->bso', x, W_base) + b_base
        logits = jnp.einsum('bsd,ed->bse', jax.lax.stop_gradient(x), router_W)
        routing_probs = jax.nn.softmax(logits, axis=-1)
        expert_idx = jnp.argmax(routing_probs, axis=-1)
        onehot = jax.nn.one_hot(expert_idx, E, dtype=x.dtype)
        h = jnp.einsum('bsd,erd->bser', x, A)
        h = h * onehot[..., None]
        delta = jnp.einsum('bser,eor->bso', h, Bw)
        return base_out + delta * SCALING
    x = _layernorm(x + _L0_attn_ref(x, L0_attn_Wq, L0_attn_Wk, L0_attn_Wv, L0_attn_Wo, L0_attn_lambda_q1, L0_attn_lambda_k1, L0_attn_lambda_q2, L0_attn_lambda_k2, L0_attn_gn_w, L0_attn_gn_b), axis=-1)
    x = _layernorm(x + _L0_xattn_ref(ctx_2048, ctx_2048, x, L0_xattn_ssm_kernel, L0_xattn_D, 8), axis=-1)
    x = _layernorm(x + _L0_ffn_ref(x, L0_ffn_router_logits, L0_ffn_gating_einsum, L0_ffn_linear, L0_ffn_per_expert_scale, L0_ffn_router_scale), axis=-1)
    x = _layernorm(x + _L1_attn_ref(x, L1_attn_wq_codes, L1_attn_wq_scales, L1_attn_bq, L1_attn_wk_codes, L1_attn_wk_scales, L1_attn_bk, L1_attn_wv_codes, L1_attn_wv_scales, L1_attn_bv, L1_attn_wo_codes, L1_attn_wo_scales, L1_attn_bo), axis=-1)
    x = _layernorm(x + _L1_xattn_ref(16, 128, 256, L1_xattn_time_decay, L1_xattn_time_first, x, ctx_2048), axis=-1)
    x = _layernorm(x + _L1_ffn_ref(x, L1_ffn_W_base, L1_ffn_b_base, L1_ffn_router_W, L1_ffn_A, L1_ffn_Bw), axis=-1)
    return x

_drawn_inputs = setup_inputs


def setup_inputs(seed=0):
    import zlib

    import numpy as np

    out = dict(_drawn_inputs(seed))
    spreads = {'L0_attn_gn_w': (1.0, 0.2),
     'L0_attn_gn_b': (0.0, 0.1),
     'L0_ffn_per_expert_scale': (1.0, 0.6),
     'L0_ffn_router_scale': (1.0, 0.6),
     'L1_attn_bq': (0.0, 0.567),
     'L1_attn_bk': (0.0, 0.8),
     'L1_attn_bv': (0.0, 0.1),
     'L1_attn_bo': (0.0, 0.1)}
    factors = {'L0_attn_lambda_q1': 8.0,
     'L0_attn_lambda_k1': 6.178,
     'L0_attn_lambda_q2': 8.0,
     'L0_attn_lambda_k2': 8.0,
     'L0_ffn_router_logits': 3.775,
     'L0_ffn_gating_einsum': 3.767,
     'L0_ffn_linear': 3.393,
     'L1_ffn_b_base': 7.934}
    for name, (base, spread) in spreads.items():
        noise = np.random.default_rng([zlib.crc32(name.encode()), seed]).standard_normal(out[name].shape)
        drawn = base * np.exp(spread * noise) if base else spread * noise
        out[name] = jnp.asarray(drawn.astype(out[name].dtype))
    for name, factor in factors.items():
        out[name] = (out[name] * factor).astype(out[name].dtype)
    return out
```

```python
import math
from contextlib import ExitStack

import concourse.bass as bass
from concourse import mybir
from concourse.alu_op_type import AluOpType as ALU

F32 = mybir.dt.float32
F32R = mybir.dt.float32r
BF16 = mybir.dt.bfloat16
ACT = mybir.ActivationFunctionType
AX_X = mybir.AxisListType.X

P = 128
B = 16
T = 128
D = 256
DT = D // P
G = 4
NG = B // G
GT = G * T
BANK = 512
LN_EPS = 1e-5

H0, KV0, DH0 = 16, 4, 16
REP0 = H0 // KV0
LAMBDA_INIT = 0.8 - 0.6 * math.exp(-0.3 * 0)


def one(ap_3d, i):
    return ap_3d[:, bass.ds(i, 1), :].rearrange("p o n -> p (o n)")


def hold(eng):
    eng.nop(nofuse=True)


class Mem:

    def __init__(self, nc, ctx):
        self.nc, self.ctx, self.sems = nc, ctx, []

    def recycle(self):
        self.nc.clear_and_free_semaphores(self.sems)
        self.nc.all_engine_barrier()

    def sb(self, name, shape, dt=F32):
        return self.ctx.enter_context(self.nc.sbuf_tensor(name, shape, dt))

    def ps(self, name, shape, dt=F32):
        return self.ctx.enter_context(self.nc.psum_tensor(name, shape, dt))

    def sem(self, name):
        if not self.sems:
            self.ctx.callback(self.recycle)
        self.sems.append(self.nc.alloc_semaphore(name=name))
        return self.sems[-1]


def stage_load(nc, env, inp):
    with ExitStack() as ctx:
        m = Mem(nc, ctx)
        raw = m.sb("ld_raw", [P, DT, B * T])
        x_in = m.sem("ld_x_in")
        raw_in = m.sem("ld_raw_in")
        hi_done = m.sem("ld_hi_done")
        lo_done = m.sem("ld_lo_done")
        pool_done = m.sem("ld_pool_done")
        block = ctx.enter_context(nc.Block())
        XTh, XTl = env["XTh"], env["XTl"]

        @block.sync
        def _(sp):
            for dt in range(DT):
                sp.dma_start(raw[:, dt, :], inp["xT"][dt]).then_inc(raw_in, 16)
            sp.dma_start(env["X"][:, :, :], inp["x"].rearrange("b t d -> t b d")).then_inc(x_in, 16)
            sp.dma_start(env["ident"][:, :], inp["ident"]).then_inc(x_in, 16)
            sp.wait_ge(x_in, 32)
            hold(sp)

        @block.scalar
        def _(act):
            for dt in range(DT):
                act.wait_ge(raw_in, 16 * DT)
                nc.scalar.activation(XTh[:, dt, :], raw[:, dt, :], ACT.Copy).then_inc(hi_done, 1)

        @block.vector
        def _(dve):
            for dt in range(DT):
                dve.wait_ge(hi_done, dt + 1)
                nc.vector.tensor_tensor(XTl[:, dt, :], raw[:, dt, :], XTh[:, dt, :].bitcast(F32),
                                        ALU.subtract).then_inc(lo_done, 1)

        @block.gpsimd
        def _(pool):
            nc.gpsimd.memset(env["minus_half"][:, :], -0.5).then_inc(pool_done, 1)
            nc.gpsimd.memset(env["ones"][:, :], 1.0).then_inc(pool_done, 1)


def stage_norm(nc, env, tag, turn=None, out=None):
    X, XTh, XTl, ident = env["X"], env["XTh"], env["XTl"], env["ident"]
    split = turn == "halves"
    with ExitStack() as ctx:
        m = Mem(nc, ctx)
        stats = m.sb(f"{tag}_stats", [P, B, 6])
        moments = m.sb(f"{tag}_moments", [P, B, 2])
        var_eps = m.sb(f"{tag}_var_eps", [P, B])
        rstd = m.sb(f"{tag}_rstd", [P, B])
        scaled = m.sb(f"{tag}_scaled", [P, B])
        shift = m.sb(f"{tag}_shift", [P, B])
        xT_ps = [m.ps(f"{tag}_xT_ps{i}", [P, DT, GT]) for i in range(2)]
        stats_done = m.sem(f"{tag}_stats_done")
        moments_done = m.sem(f"{tag}_moments_done")
        eps_done = m.sem(f"{tag}_eps_done")
        rstd_done = m.sem(f"{tag}_rstd_done")
        shift_done = m.sem(f"{tag}_shift_done")
        normed_dve = m.sem(f"{tag}_normed_dve")
        normed_act = m.sem(f"{tag}_normed_act")
        turned = m.sem(f"{tag}_turned")
        hi_done = m.sem(f"{tag}_hi_done")
        lo_done = m.sem(f"{tag}_lo_done")
        out_done = m.sem(f"{tag}_out_done")
        block = ctx.enter_context(nc.Block())
        half = G // 2

        @block.vector
        def _(dve):
            def normalise(g):
                dve.wait_ge(rstd_done, g + 1)
                for b in range(g * G, g * G + half):
                    last = nc.vector.tensor_scalar(X[:, b, :], X[:, b, :], moments[:, b, 0:1], rstd[:, b:b + 1],
                                                   ALU.subtract, ALU.mult)
                last.then_inc(normed_dve, 1)

            def low(g):
                for dt in range(DT):
                    cols = slice(g * GT, (g + 1) * GT)
                    dve.wait_ge(hi_done, g * DT + (dt + 1))
                    nc.vector.tensor_tensor(XTl[:, dt, cols], xT_ps[g % 2][:, dt, :],
                                            XTh[:, dt, cols].bitcast(F32), ALU.subtract).then_inc(lo_done, 1)

            for g in range(NG):
                for b in range(g * G, (g + 1) * G):
                    nc.vector.bn_stats(stats[:, b, :], X[:, b, :]).then_inc(stats_done, 1)
                for b in range(g * G, (g + 1) * G):
                    dve.wait_ge(stats_done, b + 1)
                    nc.vector.bn_aggr(moments[:, b, :], stats[:, b, :]).then_inc(moments_done, 1)
                if g >= 1:
                    normalise(g - 1)
                if g >= 2 and split:
                    low(g - 2)
            if split:
                low(NG - 2)
            normalise(NG - 1)
            if split:
                low(NG - 1)

        @block.gpsimd
        def _(pool):
            for g in range(NG):
                bs = slice(g * G, (g + 1) * G)
                pool.wait_ge(moments_done, g * G + G)
                nc.gpsimd.tensor_scalar(var_eps[:, bs], moments[:, bs, 1], 1.0, LN_EPS, ALU.mult, ALU.add).then_inc(eps_done, 1)
                pool.wait_ge(eps_done, 2 * g + 1)
                nc.gpsimd.tensor_tensor(rstd[:, bs], var_eps[:, bs], env["minus_half"][:, 0:G], ALU.pow).then_inc(rstd_done, 1)
                pool.wait_ge(rstd_done, g + 1)
                nc.gpsimd.tensor_tensor(scaled[:, bs], moments[:, bs, 0], rstd[:, bs], ALU.mult).then_inc(eps_done, 1)
                pool.wait_ge(eps_done, 2 * g + 2)
                nc.gpsimd.tensor_scalar(shift[:, bs], scaled[:, bs], -1.0, None, ALU.mult).then_inc(shift_done, 1)

        @block.scalar
        def _(act):
            for g in range(NG + 1):
                if g < NG:
                    act.wait_ge(shift_done, g + 1)
                    for b in range(g * G + half, (g + 1) * G):
                        last = nc.scalar.activation(X[:, b, :], X[:, b, :], ACT.Identity, scale=rstd[:, b:b + 1],
                                                    bias=shift[:, b:b + 1])
                    last.then_inc(normed_act, 1)
                if g >= 1 and turn is not None:
                    act.wait_ge(turned, g)
                    for dt in range(DT):
                        src = xT_ps[(g - 1) % 2][:, dt, :]
                        if turn == "spaced":
                            src = src.rearrange("p (b t) -> p b t", b=G)
                            dst = env["XTk"][:, dt, (g - 1) * G:g * G, 1:T + 1]
                        else:
                            dst = (XTh if split else env["XTf"])[:, dt, (g - 1) * GT:g * GT]
                        nc.scalar.activation(dst, src, ACT.Copy).then_inc(hi_done, 1)

        if turn is not None:
            @block.tensor
            def _(pe):
                for g in range(NG):
                    pe.wait_ge(normed_dve, g + 1)
                    pe.wait_ge(normed_act, g + 1)
                    if g >= 2:
                        pe.wait_ge(lo_done if split else hi_done, (g - 1) * DT)
                    for dt in range(DT):
                        for j in range(G):
                            last = nc.tensor.transpose(xT_ps[g % 2][:, dt, j * T:(j + 1) * T],
                                                       X[:, g * G + j, dt * P:(dt + 1) * P], ident[:, :])
                    last.then_inc(turned, 1)

        if out is not None:
            @block.sync
            def _(sp):
                for g in range(NG):
                    sp.wait_ge(normed_dve, g + 1)
                    sp.wait_ge(normed_act, g + 1)
                    sp.dma_start(out[g * G:(g + 1) * G, :, :].rearrange("b t d -> t b d"), X[:, g * G:(g + 1) * G, :])\
                        .then_inc(out_done, 16)
                sp.wait_ge(out_done, 16 * NG)


def halves(nc, out, lhs, rhs, tiles):
    terms = [(lhs[i], rhs[k], n) for n in range(tiles) for i, k in ((0, 0), (0, 1), (1, 0))]
    for at, (lh, rh, n) in enumerate(terms):
        last = nc.tensor.matmul(out, lh(n), rh(n), start=(at == 0), stop=(at == len(terms) - 1))
    return last


def stage_attn0_heads(nc, env, inp):
    XTh, XTl, OT = env["XTh"], env["XTl"], env["OT"]
    NT = REP0
    NK = 2 * (NT + 1)
    U = G * REP0
    R = 2 * KV0
    V = 2 * DH0
    LAST = U + 8
    with ExitStack() as ctx:
        m = Mem(nc, ctx)
        w_raw = m.sb("a0_w_raw", [P, DT, NK * P + P])
        w_hi = m.sb("a0_w_hi", [P, DT, NK * P + P], F32R)
        w_lo = m.sb("a0_w_lo", [P, DT, NK * P + P], F32R)
        cos = m.sb("a0_cos", [P, T])
        sin = m.sb("a0_sin", [P, T])
        row_mask = m.sb("a0_row_mask", [P, R])
        lam_in = m.sb("a0_lam_in", [P, 4, DH0])
        lam_prod = m.sb("a0_lam_prod", [P, 2, DH0])
        lam_sum = m.sb("a0_lam_sum", [P, 2])
        lam_exp = m.sb("a0_lam_exp", [P, 2])
        lam_dif = m.sb("a0_lam_dif", [P, 1])
        sign = m.sb("a0_sign", [P, KV0, 2])
        ident_b = m.sb("a0_ident_b", [P, P], BF16)
        causal = m.sb("a0_causal", [P, 4, T], BF16)
        r_cos = m.sb("a0_r_cos", [P, 2, GT])
        r_sin = m.sb("a0_r_sin", [P, 2, GT])
        qT = m.sb("a0_qT", [P, G, NT, T])
        kT = m.sb("a0_kT", [P, GT])
        kz = m.sb("a0_kz", [P, G, R, T])
        vT = m.sb("a0_vT", [P, GT])
        v = m.sb("a0_v", [P, G, P])
        negmax = m.sb("a0_negmax", [P, 2, R])
        sums = m.sb("a0_sums", [P, 2, R])
        recip = m.sb("a0_recip", [P, 2, R])
        factor = m.sb("a0_factor", [P, 2, KV0, 2])
        probs = m.sb("a0_probs", [P, 3, KV0, 2, T])
        second = m.sb("a0_second", [P, 2, KV0, T])
        diff = m.sb("a0_diff", [P, 2, KV0, T])
        diffT = m.sb("a0_diffT", [P, 2, KV0, REP0, T])
        s_ps = [m.ps(f"a0_s_ps{i}", [P, 2 * BANK]) for i in range(2)]
        dT_ps = [m.ps(f"a0_dT_ps{i}", [P, BANK]) for i in range(2)]
        oT_ps = m.ps("a0_oT_ps", [P, BANK])
        proj_ps = [[s[:, 0:BANK], s[:, BANK:2 * BANK]] for s in s_ps]
        vT_ps, v_ps = dT_ps

        w_in = m.sem("a0_w_in")
        whi_done = m.sem("a0_whi_done")
        wlo_done = m.sem("a0_wlo_done")
        lam = m.sem("a0_lam")
        lam_exped = m.sem("a0_lam_exped")
        const = m.sem("a0_const")
        projected = m.sem("a0_projected")
        v_projected = m.sem("a0_v_projected")
        vT_done = m.sem("a0_vT_done")
        v_turned = m.sem("a0_v_turned")
        v_done = m.sem("a0_v_done")
        roped = m.sem("a0_roped")
        added = m.sem("a0_added")
        kz_done = m.sem("a0_kz_done")
        scored = m.sem("a0_scored")
        maxed = m.sem("a0_maxed")
        exped = m.sem("a0_exped")
        recip_done = m.sem("a0_recip_done")
        factor_done = m.sem("a0_factor_done")
        second_done = m.sem("a0_second_done")
        diff_done = m.sem("a0_diff_done")
        turned = m.sem("a0_turned")
        dT_done = m.sem("a0_dT_done")
        pv_done = m.sem("a0_pv_done")
        oT_done = m.sem("a0_oT_done")
        block = ctx.enter_context(nc.Block())

        @block.sync
        def _(sp):
            for dt in range(DT):
                sp.dma_start(w_raw[:, dt, :], inp["a0_w"][dt]).then_inc(w_in, 16)
            sp.dma_start(cos[:, :], inp["cos"]).then_inc(w_in, 16)
            sp.dma_start(sin[:, :], inp["sin"]).then_inc(w_in, 16)
            sp.dma_start(row_mask[:, :], inp["row_mask"]).then_inc(w_in, 16)
            sp.dma_start(lam_in[:, :, :].rearrange("p a d -> p (a d)"),
                         inp["lambdas"].partition_broadcast(P)).then_inc(w_in, 16)

        @block.gpsimd
        def _(pool):
            pool.sem_inc(added, 2)
            nc.gpsimd.memset(causal[:, :, :], 0.0).then_inc(const, 1)
            nc.gpsimd.memset(ident_b[:, :], 0.0).then_inc(const, 1)
            pool.wait_ge(const, 2)
            nc.gpsimd.affine_select(out=causal[:, :, :], in_=causal[:, :, :], compare_op=ALU.is_ge, fill=-1e38,
                                    base=0, pattern=[[0, 4], [-1, T]], channel_multiplier=1).then_inc(const, 1)
            nc.gpsimd.affine_select(out=ident_b[:, :], in_=ident_b[:, :], compare_op=ALU.not_equal, fill=1.0,
                                    base=0, pattern=[[-1, P]], channel_multiplier=1).then_inc(const, 1)
            with pool.Fori(0, NG) as g:
                for n in range(NT + 1):
                    pool.wait_ge(roped, g * (NT + 1) + (n + 1))
                    if n == 0:
                        nc.gpsimd.tensor_tensor(kT[:, :], r_cos[:, n % 2, :], r_sin[:, n % 2, :], ALU.add)\
                            .then_inc(added, 1)
                        pool.wait_ge(added, g * (NT + 1) + 3)
                        for b in range(G):
                            nc.gpsimd.tensor_tensor(kz[:, b, :, :],
                                                    kT[:, b * T:(b + 1) * T].unsqueeze(1).broadcast_to([P, R, T]),
                                                    row_mask[:, :].unsqueeze(2).broadcast_to([P, R, T]),
                                                    ALU.mult).then_inc(kz_done, 1)
                    else:
                        nc.gpsimd.tensor_tensor(qT[:, :, n - 1, :], r_cos[:, n % 2, :].rearrange("p (b t) -> p b t", b=G),
                                                r_sin[:, n % 2, :].rearrange("p (b t) -> p b t", b=G), ALU.add)\
                            .then_inc(added, 1)
                for u in range(U):
                    pool.wait_ge(factor_done, g * U + (u + 1))
                    nc.gpsimd.tensor_tensor(second[:, u % 2, :, :], probs[:, u % 3, :, 1, :],
                                            factor[:, u % 2, :, 1:2].broadcast_to([P, KV0, T]), ALU.mult)\
                        .then_inc(second_done, 1)

        @block.scalar
        def _(act):
            act.wait_ge(w_in, 16 * (DT + 4))
            for dt in range(DT):
                nc.scalar.activation(w_hi[:, dt, :], w_raw[:, dt, :], ACT.Copy).then_inc(whi_done, 1)
            act.wait_ge(lam, 2)
            nc.scalar.activation(lam_exp[:, :], lam_sum[:, :], ACT.Exp).then_inc(lam_exped, 1)
            act.sem_inc(dT_done, 2)
            act.sem_inc(oT_done, 1)
            with act.Fori(0, NG) as g:
                act.wait_ge(v_projected, g + 1)
                nc.scalar.activation(vT[:, :], vT_ps[:, :], ACT.Copy).then_inc(vT_done, 1)
                act.wait_ge(v_turned, g + 1)
                nc.scalar.activation(v[:, :, :].rearrange("p b c -> p (b c)"), v_ps[:, :], ACT.Copy).then_inc(v_done, 1)
                for step in range(-1, LAST):
                    u = step + 1
                    if u < U:
                        act.wait_ge(maxed, g * U + (u + 1))
                        for r in range(R):
                            nc.scalar.activation(probs[:, u % 3, r // 2, r % 2, :],
                                                 s_ps[u % 2][:, r * T:(r + 1) * T], ACT.Exp,
                                                 bias=negmax[:, u % 2, r:r + 1],
                                                 accum_out=sums[:, u % 2, r:r + 1]).then_inc(exped, 1)
                    u = step - 2
                    if 0 <= u < U:
                        act.wait_ge(turned, g * U + (u + 1))
                        nc.scalar.activation(diffT[:, u // REP0 % 2, :, u % REP0, :],
                                             dT_ps[u % 2][:, :].rearrange("p (k t) -> p k t", k=KV0), ACT.Copy)\
                            .then_inc(dT_done, 1)
                    b, at = divmod(step - 8, REP0)
                    if at == 0 and 0 <= b < G:
                        act.wait_ge(pv_done, g * G + (b + 1))
                        hold(act)
                        nc.scalar.activation(one(OT, g * G + b), oT_ps[:, :], ACT.Copy).then_inc(oT_done, 1)

        @block.vector
        def _(dve):
            dve.wait_ge(w_in, 16 * (DT + 4))
            nc.vector.tensor_tensor(lam_prod[:, :, :], lam_in[:, 0:4:2, :], lam_in[:, 1:4:2, :], ALU.mult).then_inc(lam, 1)
            dve.wait_ge(lam, 1)
            nc.vector.tensor_reduce(lam_sum[:, :], lam_prod[:, :, :], AX_X, ALU.add).then_inc(lam, 1)
            for dt in range(DT):
                dve.wait_ge(whi_done, dt + 1)
                nc.vector.tensor_tensor(w_lo[:, dt, :], w_raw[:, dt, :], w_hi[:, dt, :].bitcast(F32),
                                        ALU.subtract).then_inc(wlo_done, 1)
            dve.wait_ge(lam_exped, 1)
            nc.vector.memset(sign[:, :, 0:1], 1.0).then_inc(lam, 1)
            nc.vector.tensor_tensor(lam_dif[:, :], lam_exp[:, 1:2], lam_exp[:, 0:1], ALU.subtract).then_inc(lam, 1)
            dve.wait_ge(lam, 4)
            nc.vector.tensor_scalar(sign[:, :, 1], lam_dif[:, 0:1].broadcast_to([P, KV0]), 1.0, -LAMBDA_INIT,
                                    ALU.mult, ALU.add).then_inc(lam, 1)
            dve.wait_ge(lam, 5)
            with dve.Fori(0, NG) as g:
                for n in range(NT + 1):
                    dve.wait_ge(projected, g * (NT + 1) + (n + 1))
                    dve.wait_ge(added, g * (NT + 1) + (n + 1))
                    v3 = "p (b t) -> p b t"
                    nc.vector.tensor_tensor(r_cos[:, n % 2, :].rearrange(v3, b=G),
                                            proj_ps[n % 2][0].rearrange(v3, b=G),
                                            cos[:, :].unsqueeze(1).broadcast_to([P, G, T]), ALU.mult)
                    nc.vector.tensor_tensor(r_sin[:, n % 2, :].rearrange(v3, b=G),
                                            proj_ps[n % 2][1].rearrange(v3, b=G),
                                            sin[:, :].unsqueeze(1).broadcast_to([P, G, T]), ALU.mult)\
                        .then_inc(roped, 1)
                for step in range(-1, LAST):
                    u = step + 1
                    if u < U:
                        dve.wait_ge(scored, g * U + (u + 1))
                        nc.vector.tensor_reduce(negmax[:, u % 2, :], s_ps[u % 2][:, :].rearrange("p (r s) -> p r s", r=R),
                                                AX_X, ALU.max, negate=True).then_inc(maxed, 1)
                    u = step
                    if 0 <= u < U:
                        dve.wait_ge(exped, g * R * U + (R * u + R))
                        nc.vector.reciprocal(recip[:, u % 2, :], sums[:, u % 2, :]).then_inc(recip_done, 1)
                        dve.wait_ge(recip_done, g * U + (u + 1))
                        nc.vector.tensor_tensor(factor[:, u % 2, :, :].rearrange("p k h -> p (k h)"), recip[:, u % 2, :],
                                                sign[:, :, :].rearrange("p k h -> p (k h)"), ALU.mult)\
                            .then_inc(factor_done, 1)
                    u = step - 1
                    if 0 <= u < U:
                        dve.wait_ge(second_done, g * U + (u + 1))
                        if u + 2 >= U:
                            dve.wait_ge(turned, g * U + (u - 1))
                        for kv in range(KV0):
                            last = nc.vector.scalar_tensor_tensor(diff[:, u % 2, kv, :], probs[:, u % 3, kv, 0, :],
                                                                  factor[:, u % 2, kv, 0:1], second[:, u % 2, kv, :],
                                                                  ALU.mult, ALU.add)
                        last.then_inc(diff_done, 1)

        @block.tensor
        def _(pe):
            pe.wait_ge(wlo_done, DT)
            pe.wait_ge(const, 4)
            hold(pe)
            w_halves = [lambda c: lambda dt: w_hi[:, dt, c], lambda c: lambda dt: w_lo[:, dt, c]]
            with pe.Fori(0, NG) as g:
                toks = bass.ds(g * GT, GT)
                x_halves = [lambda dt: XTh[:, dt, toks], lambda dt: XTl[:, dt, toks]]
                for n in range(NT + 1):
                    if n >= 2:
                        pe.wait_ge(roped, g * (NT + 1) + (n - 1))
                    for pr in range(2):
                        c = slice((2 * n + pr) * P, (2 * n + pr + 1) * P)
                        last = halves(nc, proj_ps[n % 2][pr], [w(c) for w in w_halves], x_halves, DT)
                    last.then_inc(projected, 1)
                    if n == 0:
                        c = slice(NK * P, NK * P + P)
                        halves(nc, vT_ps[:, :], [w(c) for w in w_halves], x_halves, DT).then_inc(v_projected, 1)
                    if n == 1:
                        pe.wait_ge(vT_done, g + 1)
                        for b in range(G):
                            last = nc.tensor.transpose(v_ps[:, b * T:(b + 1) * T], vT[:, b * T:(b + 1) * T],
                                                       env["ident"][:, :])
                        last.then_inc(v_turned, 1)
                for step in range(-1, LAST):
                    u = step + 1
                    if u < U:
                        b, j = divmod(u, REP0)
                        if u == 0:
                            pe.wait_ge(added, g * (NT + 1) + (NT + 3))
                            pe.wait_ge(kz_done, g * G + G)
                            pe.wait_ge(v_done, g + 1)
                        if u >= 2:
                            pe.wait_ge(exped, g * R * U + (R * (u - 2) + R))
                        for k in range(2):
                            nc.tensor.matmul(s_ps[u % 2][:, k * BANK:(k + 1) * BANK], ident_b[:, :],
                                             causal[:, :, :].rearrange("p a s -> p (a s)"), start=True, stop=False)
                            last = nc.tensor.matmul(s_ps[u % 2][:, k * BANK:(k + 1) * BANK], qT[:, b, j, :],
                                                    kz[:, b, 4 * k:4 * k + 4, :].rearrange("p r s -> p (r s)"),
                                                    start=False, stop=True)
                        last.then_inc(scored, 1)
                    u = step - 2
                    if 0 <= u < U:
                        pe.wait_ge(dT_done, g * U + (u + 1))
                        pe.wait_ge(diff_done, g * U + (u + 1))
                        for kv in range(KV0):
                            last = nc.tensor.transpose(dT_ps[u % 2][:, kv * T:(kv + 1) * T], diff[:, u % 2, kv, :],
                                                       env["ident"][:, :])
                        last.then_inc(turned, 1)
                    b, at = divmod(step - 7, REP0)
                    if at == 0 and 0 <= b < G:
                        pe.wait_ge(dT_done, g * U + (REP0 * b + REP0 + 2))
                        pe.wait_ge(oT_done, g * G + (b + 1))
                        for kv in range(KV0):
                            last = nc.tensor.matmul(oT_ps[kv * V:(kv + 1) * V, :], v[:, b, kv * V:(kv + 1) * V],
                                                    diffT[:, b % 2, kv, :, :].rearrange("p j t -> p (j t)"),
                                                    start=True, stop=True)
                        last.then_inc(pv_done, 1)


def stage_attn0_out(nc, env, inp):
    X, OT = env["X"], env["OT"]
    NJ = REP0
    with ExitStack() as ctx:
        m = Mem(nc, ctx)
        wo_raw = m.sb("n0_wo_raw", [P, NJ, D])
        wo_b = m.sb("n0_wo_b", [P, NJ, D])
        wo = m.sb("n0_wo", [P, NJ, D])
        gn_w = m.sb("n0_gn_w", [P, NJ])
        gn_b = m.sb("n0_gn_b", [P, NJ])
        bias = m.sb("n0_bias", [P, G, D])
        share = m.sb("n0_share", [P, P])
        stats = m.sb("n0_stats", [P, 2, NJ, 6])
        moments = m.sb("n0_moments", [P, 2, NJ, 2])
        square = m.sb("n0_square", [P, 2, NJ])
        avg = m.sb("n0_avg", [P, 2, NJ, 2])
        avg2 = m.sb("n0_avg2", [P, 2, NJ])
        var = m.sb("n0_var", [P, 2, NJ])
        rstd = m.sb("n0_rstd", [P, 2, NJ])
        yT = m.sb("n0_yT", [P, 2, NJ, T])
        avg_ps = [m.ps(f"n0_avg_ps{i}", [P, BANK]) for i in range(2)]
        out_ps = [m.ps(f"n0_out_ps{i}", [P, BANK]) for i in range(2)]
        bias_ps = m.ps("n0_bias_ps", [P, BANK])
        w_in = m.sem("n0_w_in")
        wb_done = m.sem("n0_wb_done")
        wo_done = m.sem("n0_wo_done")
        bias_ready = m.sem("n0_bias_ready")
        bias_done = m.sem("n0_bias_done")
        stats_done = m.sem("n0_stats_done")
        moments_done = m.sem("n0_moments_done")
        squared = m.sem("n0_squared")
        power_done = m.sem("n0_power_done")
        averaged = m.sem("n0_averaged")
        avg_done = m.sem("n0_avg_done")
        avg2_done = m.sem("n0_avg2_done")
        var_done = m.sem("n0_var_done")
        rstd_done = m.sem("n0_rstd_done")
        y_done = m.sem("n0_y_done")
        multiplied = m.sem("n0_multiplied")
        block = ctx.enter_context(nc.Block())

        @block.sync
        def _(sp):
            sp.dma_start(wo_raw[:, :, :], inp["a0_wo"].rearrange("(k p) n -> p k n", p=P)).then_inc(w_in, 16)
            sp.dma_start(gn_w[:, :], inp["gn_w"]).then_inc(w_in, 16)
            sp.dma_start(gn_b[:, :], inp["gn_b"]).then_inc(w_in, 16)
            sp.dma_start(share[:, :], inp["share"]).then_inc(w_in, 16)

        @block.gpsimd
        def _(pool):
            pool.wait_ge(w_in, 64)
            for k in range(NJ):
                nc.gpsimd.tensor_scalar(wo_b[:, k, :], wo_raw[:, k, :], gn_b[:, k:k + 1], 1.0 - LAMBDA_INIT,
                                        ALU.mult, ALU.mult).then_inc(wb_done, 1)
                nc.gpsimd.tensor_scalar(wo[:, k, :], wo_raw[:, k, :], gn_w[:, k:k + 1], 1.0 - LAMBDA_INIT,
                                        ALU.mult, ALU.mult).then_inc(wo_done, 1)
            with pool.Fori(0, B // 2) as i:
                for r in range(2):
                    pool.wait_ge(var_done, i * 2 + (r + 1))
                    nc.gpsimd.tensor_tensor(rstd[:, r, :], var[:, r, :], env["minus_half"][:, 0:NJ], ALU.pow)\
                        .then_inc(rstd_done, 1)

        @block.vector
        def _(dve):
            dve.wait_ge(bias_ready, 1)
            nc.vector.tensor_copy(bias[:, 0, :], bias_ps[:, 0:D]).then_inc(bias_done, 1)
            dve.wait_ge(bias_done, 1)
            with dve.Fori(0, B // 2) as i:
                for r in range(2):
                    for j in range(NJ):
                        last = nc.vector.bn_stats(stats[:, r, j, :], one(OT, i * 2 + r)[:, j * T:(j + 1) * T])
                    last.then_inc(stats_done, 1)
                for r in range(2):
                    dve.wait_ge(stats_done, i * 2 + (r + 1))
                    hold(dve)
                    for j in range(NJ):
                        last = nc.vector.bn_aggr(moments[:, r, j, :], stats[:, r, j, :])
                    last.then_inc(moments_done, 1)
                for r in range(2):
                    dve.wait_ge(moments_done, i * 2 + (r + 1))
                    nc.vector.tensor_tensor(square[:, r, :], moments[:, r, :, 0], moments[:, r, :, 0], ALU.mult)\
                        .then_inc(squared, 1)
                for r in range(2):
                    dve.wait_ge(squared, i * 2 + (r + 1))
                    nc.vector.tensor_tensor(moments[:, r, :, 1], moments[:, r, :, 1], square[:, r, :], ALU.add)\
                        .then_inc(power_done, 1)
                for r in range(2):
                    dve.wait_ge(averaged, i * 2 + (r + 1))
                    nc.vector.tensor_copy(avg[:, r, :, :].rearrange("p j a -> p (j a)"), avg_ps[r][:, 0:2 * NJ])\
                        .then_inc(avg_done, 1)
                for r in range(2):
                    dve.wait_ge(avg_done, i * 2 + (r + 1))
                    nc.vector.tensor_tensor(avg2[:, r, :], avg[:, r, :, 0], avg[:, r, :, 0], ALU.mult).then_inc(avg2_done, 1)
                for r in range(2):
                    dve.wait_ge(avg2_done, i * 2 + (r + 1))
                    nc.vector.scalar_tensor_tensor(var[:, r, :], avg[:, r, :, 1], LN_EPS, avg2[:, r, :],
                                                   ALU.add, ALU.subtract).then_inc(var_done, 1)
                for r in range(2):
                    dve.wait_ge(rstd_done, i * 2 + (r + 1))
                    dve.wait_ge(multiplied, i * 2 + (r + 1))
                    hold(dve)
                    for j in range(NJ):
                        last = nc.vector.tensor_scalar(yT[:, r, j, :], one(OT, i * 2 + r)[:, j * T:(j + 1) * T],
                                                       avg[:, r, j, 0:1], rstd[:, r, j:j + 1], ALU.subtract, ALU.mult)
                    last.then_inc(y_done, 1)
                for r in range(2):
                    dve.wait_ge(multiplied, i * 2 + (r + 3))
                    hold(dve)
                    nc.vector.tensor_tensor(one(X, i * 2 + r), one(X, i * 2 + r), out_ps[r][:, 0:D], ALU.add)

        @block.tensor
        def _(pe):
            pe.sem_inc(multiplied, 2)
            pe.wait_ge(wb_done, NJ)
            for k in range(NJ):
                last = nc.tensor.matmul(bias_ps[:, 0:D], env["ones"][:, :], wo_b[:, k, :], start=(k == 0), stop=(k == NJ - 1))
            last.then_inc(bias_ready, 1)
            pe.wait_ge(wo_done, NJ)
            pe.wait_ge(bias_done, 1)
            hold(pe)
            with pe.Fori(0, B // 2) as i:
                for r in range(2):
                    pe.wait_ge(power_done, i * 2 + (r + 1))
                    nc.tensor.matmul(avg_ps[r][:, 0:2 * NJ], share[:, :],
                                     moments[:, r, :, :].rearrange("p j a -> p (j a)"), start=True, stop=True)\
                        .then_inc(averaged, 1)
                for r in range(2):
                    pe.wait_ge(y_done, i * 2 + (r + 1))
                    nc.tensor.matmul(out_ps[r][:, 0:D], env["ident"][:, :], bias[:, 0, :], start=True, stop=False)
                    for k in range(NJ):
                        last = nc.tensor.matmul(out_ps[r][:, 0:D], yT[:, r, k, :], wo[:, k, :], start=False,
                                                stop=(k == NJ - 1))
                    last.then_inc(multiplied, 1)


def stage_conv0(nc, env, inp):
    XTf, Z, C = env["XTf"], env["Z"], env["C"]
    HD = 8
    H = T // HD
    LB = D // P
    with ExitStack() as ctx:
        m = Mem(nc, ctx)
        toep = [m.sb(f"c0_toep{i}", [P, LB * P]) for i in range(2)]
        toep_d = [m.sb(f"c0_toep_d{i}", [P, P]) for i in range(2)]
        d_all = m.sb("c0_d_all", [P, H])
        anti = m.sb("c0_anti", [P, P])
        d_diag = m.sb("c0_d_diag", [P, H, P])
        pairs = m.sb("c0_pairs", [P, 2, LB, HD, HD, B])
        weighted = m.sb("c0_weighted", [P, 2, HD, HD, B])
        y_ps = [[m.ps(f"c0_y_ps{r}{lb}", [P, 2 * BANK]) for lb in range(LB)] for r in range(2)]
        d_in = m.sem("c0_d_in")
        toep_in = [m.sem(f"c0_toep_in{r}") for r in range(2)]
        diag_done = m.sem("c0_diag_done")
        toep_done = m.sem("c0_toep_done")
        paired = m.sem("c0_paired")
        convolved = m.sem("c0_convolved")
        weighted_done = m.sem("c0_weighted_done")
        summed = m.sem("c0_summed")
        block = ctx.enter_context(nc.Block())

        @block.sync
        def _(sp):
            sp.dma_start(d_all[:, :], inp["c0_D"].partition_broadcast(P)).then_inc(d_in, 16)
            sp.dma_start(anti[:, :], inp["anti"]).then_inc(d_in, 16)
            sp.sem_inc(convolved, 4)
            with sp.Fori(0, H // 2) as i:
                for r in range(2):
                    sp.wait_ge(convolved, i * 4 + (2 * r + 2))
                    hold(sp)
                    sp.dma_start(toep[r][:, :], inp["toeplitz"][bass.ds(i * 2 + r, 1), :, :]
                                 .rearrange("o p l -> p (o l)")).then_inc(toep_in[r], 16)

        @block.gpsimd
        def _(pool):
            pool.wait_ge(d_in, 32)
            nc.gpsimd.tensor_tensor(d_diag[:, :, :], anti[:, :].unsqueeze(1).broadcast_to([P, H, P]),
                                    d_all[:, :].unsqueeze(2).broadcast_to([P, H, P]), ALU.mult).then_inc(diag_done, 1)
            with pool.Fori(0, H // 2) as i:
                for r in range(2):
                    pool.wait_ge(convolved, i * 4 + (2 * r + 2))
                    for mb in range(LB):
                        hold(pool)
                        c = C[:, mb, bass.ds((i * 2 + r) * HD, HD), :]
                        nc.gpsimd.tensor_tensor(pairs[:, r, mb, :, :, :],
                                                c.unsqueeze(2).broadcast_to([P, HD, HD, B]),
                                                c.unsqueeze(1).broadcast_to([P, HD, HD, B]), ALU.mult).then_inc(paired, 1)

        @block.vector
        def _(dve):
            dve.sem_inc(weighted_done, 4)
            dve.wait_ge(diag_done, 1)
            hold(dve)

            def diagonal(i, r):
                dve.wait_ge(toep_in[r], i * 16 + 16)
                dve.wait_ge(convolved, i * 4 + (2 * r + 2))
                nc.vector.tensor_tensor(toep_d[r][:, :], toep[r][:, 0:P], one(d_diag, i * 2 + r), ALU.add)\
                    .then_inc(toep_done, 1)

            with dve.Fori(0, H // 2) as i:
                for r in range(2):
                    diagonal(i, r)
                for r in range(2):
                    for lb in range(LB):
                        n = 2 * r + lb
                        dve.wait_ge(convolved, i * 4 + (n + 5))
                        h = i * 2 + r
                        q = XTf[:, lb, :].rearrange("p (b t) -> p t b", b=B)[:, bass.ds(h * HD, HD), :]
                        nc.vector.tensor_tensor(weighted[:, lb, :, :, :],
                                                y_ps[r][lb][:, :].rearrange("p (i j b) -> p i j b", i=HD, j=HD),
                                                q.unsqueeze(2).broadcast_to([P, HD, HD, B]), ALU.mult)\
                            .then_inc(weighted_done, 1)
                        dve.wait_ge(weighted_done, i * 4 + (n + 5))
                        nc.vector.tensor_reduce(Z[:, lb, :, :].rearrange("p b t -> p t b")[:, bass.ds(h * HD, HD), :],
                                                weighted[:, lb, :, :, :].rearrange("p i j b -> p j b i"),
                                                AX_X, ALU.add).then_inc(summed, 1)

        @block.tensor
        def _(pe):
            with pe.Fori(0, H // 2) as i:
                for r in range(2):
                    halves2 = [slice(0, HD // 2), slice(HD // 2, HD)]

                    def product(lb, mb, weights, start, stop):
                        for k, half in enumerate(halves2):
                            last = nc.tensor.matmul(y_ps[r][lb][:, k * BANK:(k + 1) * BANK], weights,
                                                    pairs[:, r, mb, half, :, :].rearrange("p i j b -> p (i j b)"),
                                                    start=start, stop=stop)
                        return last

                    pe.wait_ge(weighted_done, i * 4 + (2 * r + 2))
                    pe.wait_ge(toep_done, i * 2 + (r + 1))
                    pe.wait_ge(paired, i * 4 + (2 * r + 1))
                    product(0, 0, toep_d[r][:, :], True, True).then_inc(convolved, 1)
                    product(1, 0, toep[r][:, P:2 * P], True, False)
                    pe.wait_ge(paired, i * 4 + (2 * r + 2))
                    product(1, 1, toep_d[r][:, :], False, True).then_inc(convolved, 1)


def stage_conv0_out(nc, env):
    X, Z = env["X"], env["Z"]
    with ExitStack() as ctx:
        m = Mem(nc, ctx)
        z = m.sb("z0_z", [P, 2, D // P, T])
        z_ps = [m.ps(f"z0_z_ps{i}", [P, BANK]) for i in range(2)]
        copied = m.sem("z0_copied")
        turned = m.sem("z0_turned")
        added = m.sem("z0_added")
        block = ctx.enter_context(nc.Block())

        @block.scalar
        def _(act):
            with act.Fori(0, B // 2) as i:
                for r in range(2):
                    act.wait_ge(turned, i * 2 + (r + 1))
                    hold(act)
                    nc.scalar.activation(z[:, r, :, :], Z[:, :, bass.ds(i * 2 + r, 1), :].rearrange("p l o t -> p l (o t)"),
                                         ACT.Copy).then_inc(copied, 1)

        @block.tensor
        def _(pe):
            pe.sem_inc(turned, 2)
            with pe.Fori(0, B // 2) as i:
                for r in range(2):
                    pe.wait_ge(copied, i * 2 + (r + 1))
                    pe.wait_ge(added, i * 2 + (r + 1))
                    for lb in range(D // P):
                        last = nc.tensor.transpose(z_ps[r][:, lb * P:(lb + 1) * P], z[:, r, lb, :], env["ident"][:, :])
                    last.then_inc(turned, 1)

        @block.vector
        def _(dve):
            dve.sem_inc(added, 2)
            with dve.Fori(0, B // 2) as i:
                for r in range(2):
                    dve.wait_ge(turned, i * 2 + (r + 3))
                    hold(dve)
                    nc.vector.tensor_tensor(one(X, i * 2 + r), one(X, i * 2 + r), z_ps[r][:, 0:D], ALU.add)\
                        .then_inc(added, 1)


def stage_moe0(nc, env, inp):
    X, XTh, XTl, ident = env["X"], env["XTh"], env["XTl"], env["ident"]
    E = 8
    HT = D // P
    WG = 2 * D
    WE = WG + D
    NU = E * HT
    with ExitStack() as ctx:
        m = Mem(nc, ctx)
        w_raw = m.sb("m0_w_raw", [P, 2, DT, WE])
        w_hi = m.sb("m0_w_hi", [P, E, DT, WE], F32R)
        w_lo = m.sb("m0_w_lo", [P, E, DT, WE], F32R)
        r_raw = m.sb("m0_r_raw", [P, DT, P])
        r_scale = m.sb("m0_r_scale", [P, DT])
        r_scaled = m.sb("m0_r_scaled", [P, DT, P])
        r_hi = m.sb("m0_r_hi", [P, DT, P], F32R)
        r_lo = m.sb("m0_r_lo", [P, DT, P], F32R)
        rank = m.sb("m0_rank", [P, E])
        per_expert = m.sb("m0_per_expert", [P, E])
        square = m.sb("m0_square", [P, D])
        power = m.sb("m0_power", [P, B])
        power_eps = m.sb("m0_power_eps", [P, B])
        x_rstd = m.sb("m0_x_rstd", [P, B])
        lgT = m.sb("m0_lgT", [P, GT])
        small = {n: m.sb(f"m0_{n}", [P, B, E]) for n in
                 ("logit", "tie", "order", "first", "rest", "tie2", "order2", "second", "chosen", "less", "exp",
                  "picked", "share", "weight")}
        top = {n: m.sb(f"m0_{n}", [P, B]) for n in ("max1", "rank1", "max2", "rank2", "total", "inverse")}
        w_grp = m.sb("m0_w_grp", [P, G, E])
        act_g = m.sb("m0_act_g", [P, 2, GT])
        hid = m.sb("m0_hid", [P, 2, GT])
        hid_hi = m.sb("m0_hid_hi", [P, 2, HT, GT], F32R)
        hid_lo = m.sb("m0_hid_lo", [P, 2, HT, GT], F32R)
        acc = m.sb("m0_acc", [P, G, D])
        gate_ps = [m.ps(f"m0_gate_ps{i}", [P, BANK]) for i in range(2)]
        up_ps = [m.ps(f"m0_up_ps{i}", [P, BANK]) for i in range(2)]
        out_ps = [[m.ps(f"m0_out_ps{i}{k}", [P, BANK]) for k in range(2)] for i in range(2)]
        w_in = [m.sem(f"m0_w_in{i}") for i in range(2)]
        r_in = m.sem("m0_r_in")
        whi_done = m.sem("m0_whi_done")
        wlo_done = m.sem("m0_wlo_done")
        power_done = m.sem("m0_power_done")
        eps_done = m.sem("m0_eps_done")
        x_rstd_done = m.sem("m0_x_rstd_done")
        r_scaled_done = m.sem("m0_r_scaled_done")
        rhi_done = m.sem("m0_rhi_done")
        rlo_done = m.sem("m0_rlo_done")
        lgT_ready = m.sem("m0_lgT_ready")
        lgT_done = m.sem("m0_lgT_done")
        lg_ready = m.sem("m0_lg_ready")
        logit_done = m.sem("m0_logit_done")
        routed = m.sem("m0_routed")
        exp_done = m.sem("m0_exp_done")
        grp_done = m.sem("m0_grp_done")
        gated = m.sem("m0_gated")
        gelu_done = m.sem("m0_gelu_done")
        hid_done = m.sem("m0_hid_done")
        hid_hi_done = m.sem("m0_hid_hi_done")
        hid_lo_done = m.sem("m0_hid_lo_done")
        down_done = m.sem("m0_down_done")
        acc_done = m.sem("m0_acc_done")
        block = ctx.enter_context(nc.Block())

        @block.sync
        def _(sp):
            sp.dma_start(r_raw[:, :, :], inp["m0_router"].rearrange("(k p) e -> p k e", p=P)).then_inc(r_in, 16)
            sp.dma_start(r_scale[:, :], inp["m0_router_scale"]).then_inc(r_in, 16)
            sp.dma_start(rank[:, :], inp["m0_rank"].partition_broadcast(P)).then_inc(r_in, 16)
            sp.dma_start(per_expert[:, :], inp["m0_per_expert"].partition_broadcast(P)).then_inc(r_in, 16)
            for e in range(E):
                if e >= 2:
                    sp.wait_ge(wlo_done, e - 1)
                sp.dma_start(w_raw[:, e % 2, :, :], inp["m0_w"][e].rearrange("(k p) n -> p k n", p=P))\
                    .then_inc(w_in[e % 2], 16)

        @block.gpsimd
        def _(pool):
            pool.wait_ge(power_done, B)
            nc.gpsimd.tensor_scalar(power_eps[:, :], power[:, :], 1.0 / D, 1e-6, ALU.mult, ALU.add).then_inc(eps_done, 1)
            pool.wait_ge(eps_done, 1)
            nc.gpsimd.tensor_tensor(x_rstd[:, :], power_eps[:, :], env["minus_half"][:, 0:B], ALU.pow)\
                .then_inc(x_rstd_done, 1)
            for e in range(E):
                pool.wait_ge(whi_done, e + 1)
                nc.gpsimd.tensor_tensor(w_lo[:, e, :, :], w_raw[:, e % 2, :, :], w_hi[:, e, :, :].bitcast(F32),
                                        ALU.subtract).then_inc(wlo_done, 1)
            with pool.Fori(0, NG) as g:
                for u in range(NU):
                    pool.wait_ge(hid_hi_done, g * NU + (u + 1))
                    nc.gpsimd.tensor_tensor(hid_lo[:, u // HT % 2, u % HT, :], hid[:, u % 2, :],
                                            hid_hi[:, u // HT % 2, u % HT, :].bitcast(F32), ALU.subtract)\
                        .then_inc(hid_lo_done, 1)

        def high(act, g, u):
            act.wait_ge(hid_done, g * NU + (u + 3))
            nc.scalar.activation(hid_hi[:, u // HT % 2, u % HT, :], hid[:, u % 2, :], ACT.Copy).then_inc(hid_hi_done, 1)

        @block.scalar
        def _(act):
            for b in range(B):
                if b:
                    act.wait_ge(power_done, b)
                nc.scalar.activation(square[:, :], X[:, b, :], ACT.Square, accum_out=power[:, b:b + 1])\
                    .then_inc(power_done, 1)
            act.wait_ge(r_scaled_done, DT)
            nc.scalar.activation(r_hi[:, :, :], r_scaled[:, :, :], ACT.Copy).then_inc(rhi_done, 1)
            for g in range(NG):
                act.wait_ge(lgT_ready, g + 1)
                nc.scalar.activation(lgT[:, :], gate_ps[g % 2][:, :], ACT.Copy).then_inc(lgT_done, 1)
            act.wait_ge(routed, 11)
            nc.scalar.activation(small["exp"][:, :, :], small["less"][:, :, :], ACT.Exp).then_inc(exp_done, 1)
            for e in range(E):
                act.wait_ge(w_in[e % 2], 16 * (e // 2 + 1))
                nc.scalar.activation(w_hi[:, e, :, :], w_raw[:, e % 2, :, :], ACT.Copy).then_inc(whi_done, 1)
            with act.Fori(0, NG) as g:
                for u in range(NU):
                    act.wait_ge(gated, g * NU + (u + 1))
                    nc.scalar.activation(act_g[:, u % 2, :], gate_ps[u % 2][:, :], ACT.Gelu_apprx_tanh)\
                        .then_inc(gelu_done, 1)
                    if u >= 1:
                        high(act, g, u - 1)
                high(act, g, NU - 1)

        @block.vector
        def _(dve):
            dve.wait_ge(r_in, 64)
            for dt in range(DT):
                nc.vector.tensor_scalar(r_scaled[:, dt, :], r_raw[:, dt, :], r_scale[:, dt:dt + 1], D ** -0.5,
                                        ALU.mult, ALU.mult).then_inc(r_scaled_done, 1)
            dve.wait_ge(rhi_done, 1)
            nc.vector.tensor_tensor(r_lo[:, :, :], r_scaled[:, :, :], r_hi[:, :, :].bitcast(F32), ALU.subtract)\
                .then_inc(rlo_done, 1)
            dve.wait_ge(x_rstd_done, 1)
            for g in range(NG):
                dve.wait_ge(lg_ready, g + 1)
                nc.vector.tensor_tensor(small["logit"][:, g * G:(g + 1) * G, :],
                                        up_ps[g % 2][:, :].rearrange("p (b t) -> p b t", b=G)[:, :, 0:E],
                                        x_rstd[:, g * G:(g + 1) * G].unsqueeze(2).broadcast_to([P, G, E]),
                                        ALU.mult).then_inc(logit_done, 1)

            def wide(name):
                return top[name][:, :].unsqueeze(2).broadcast_to([P, B, E])

            def expert_row(ap):
                return ap[:, :].unsqueeze(1).broadcast_to([P, B, E])

            s = {n: ap[:, :, :] for n, ap in small.items()}
            step = [0]

            def chained(ins):
                step[0] += 1
                ins.then_inc(routed, 1)
                dve.wait_ge(routed, step[0])

            tt = nc.vector.tensor_tensor
            dve.wait_ge(logit_done, NG)
            chained(nc.vector.tensor_reduce(top["max1"][:, :], s["logit"], AX_X, ALU.max))
            chained(tt(s["tie"], s["logit"], wide("max1"), ALU.is_equal))
            chained(tt(s["order"], s["tie"], expert_row(rank), ALU.mult))
            chained(nc.vector.tensor_reduce(top["rank1"][:, :], s["order"], AX_X, ALU.max))
            chained(tt(s["first"], s["order"], wide("rank1"), ALU.is_equal))
            chained(nc.vector.scalar_tensor_tensor(s["rest"].rearrange("p b e -> p (b e)"),
                                                   s["first"].rearrange("p b e -> p (b e)"), -1e38,
                                                   s["logit"].rearrange("p b e -> p (b e)"), ALU.mult, ALU.add))
            chained(nc.vector.tensor_reduce(top["max2"][:, :], s["rest"], AX_X, ALU.max))
            chained(tt(s["tie2"], s["rest"], wide("max2"), ALU.is_equal))
            chained(tt(s["order2"], s["tie2"], expert_row(rank), ALU.mult))
            chained(nc.vector.tensor_reduce(top["rank2"][:, :], s["order2"], AX_X, ALU.max))
            chained(tt(s["less"], s["logit"], wide("max1"), ALU.subtract))
            chained(tt(s["second"], s["order2"], wide("rank2"), ALU.is_equal))
            chained(tt(s["chosen"], s["first"], s["second"], ALU.add))
            dve.wait_ge(exp_done, 1)
            chained(tt(s["picked"], s["exp"], s["chosen"], ALU.mult))
            chained(nc.vector.tensor_reduce(top["total"][:, :], s["picked"], AX_X, ALU.add))
            chained(nc.vector.reciprocal(top["inverse"][:, :], top["total"][:, :]))
            chained(tt(s["share"], s["picked"], wide("inverse"), ALU.mult))
            chained(tt(s["weight"], s["share"], expert_row(per_expert), ALU.mult))

            def accumulate(g, e):
                for j in range(G):
                    dve.wait_ge(down_done, g * E * G + (e * G + j // 2 * 2 + 2))
                    if e:
                        dve.wait_ge(acc_done, g * E * G + ((e + 1) * G + j + 1))
                    hold(dve)
                    src = acc[:, j, :] if e else one(X, g * G + j)
                    dst = acc[:, j, :] if e < E - 1 else one(X, g * G + j)
                    nc.vector.scalar_tensor_tensor(dst, out_ps[e % 2][j // 2][:, (j % 2) * D:(j % 2 + 1) * D],
                                                   w_grp[:, j, e:e + 1], src, ALU.mult, ALU.add).then_inc(acc_done, 1)

            dve.sem_inc(hid_done, 2)
            dve.sem_inc(acc_done, 2 * G)
            with dve.Fori(0, NG) as g:
                dve.wait_ge(acc_done, g * E * G + 2 * G)
                hold(dve)
                nc.vector.tensor_copy(w_grp[:, :, :], small["weight"][:, bass.ds(g * G, G), :]).then_inc(grp_done, 1)
                dve.wait_ge(grp_done, g + 1)
                hold(dve)
                for u in range(NU):
                    dve.wait_ge(gelu_done, g * NU + (u + 1))
                    if u >= 2:
                        dve.wait_ge(hid_lo_done, g * NU + (u - 1))
                    nc.vector.tensor_tensor(hid[:, u % 2, :], act_g[:, u % 2, :], up_ps[u % 2][:, :], ALU.mult)\
                        .then_inc(hid_done, 1)
                    if u % HT == HT - 1 and u >= 2 * HT - 1:
                        accumulate(g, u // HT - 1)
                accumulate(g, E - 1)

        @block.tensor
        def _(pe):
            pe.wait_ge(rlo_done, 1)
            for g in range(NG):
                toks = slice(g * GT, (g + 1) * GT)
                if g >= 2:
                    pe.wait_ge(lgT_done, g - 1)
                halves(nc, gate_ps[g % 2][:, :], [lambda dt: r_hi[:, dt, :], lambda dt: r_lo[:, dt, :]],
                       [lambda dt: XTh[:, dt, toks], lambda dt: XTl[:, dt, toks]], DT).then_inc(lgT_ready, 1)
                pe.wait_ge(lgT_done, g + 1)
                if g >= 2:
                    pe.wait_ge(logit_done, g - 1)
                for b in range(G):
                    last = nc.tensor.transpose(up_ps[g % 2][:, b * P:(b + 1) * P], lgT[:, b * T:(b + 1) * T], ident[:, :])
                last.then_inc(lg_ready, 1)
            pe.wait_ge(logit_done, NG)

            def gates(g, e):
                toks = bass.ds(g * GT, GT)
                x_halves = [lambda dt: XTh[:, dt, toks], lambda dt: XTl[:, dt, toks]]
                pe.wait_ge(wlo_done, e + 1)
                for ht in range(HT):
                    u = e * HT + ht
                    pe.wait_ge(hid_done, g * NU + (u + 1))
                    for ps, c0 in ((gate_ps[u % 2], ht * P), (up_ps[u % 2], D + ht * P)):
                        c = slice(c0, c0 + P)
                        last = halves(nc, ps[:, :], [lambda dt: w_hi[:, e, dt, c], lambda dt: w_lo[:, e, dt, c]],
                                      x_halves, DT)
                    last.then_inc(gated, 1)

            def down(g, e):
                pe.wait_ge(hid_lo_done, g * NU + (e * HT + HT))
                pe.wait_ge(acc_done, g * E * G + (e * G + G))
                for j in range(G):
                    toks = slice(j * T, (j + 1) * T)
                    halves(nc, out_ps[e % 2][j // 2][:, (j % 2) * D:(j % 2 + 1) * D],
                           [lambda n: hid_hi[:, e % 2, n, toks], lambda n: hid_lo[:, e % 2, n, toks]],
                           [lambda n: w_hi[:, e, n, WG:WE], lambda n: w_lo[:, e, n, WG:WE]], HT).then_inc(down_done, 1)

            with pe.Fori(0, NG) as g:
                gates(g, 0)
                for e in range(E):
                    if e + 1 < E:
                        gates(g, e + 1)
                    down(g, e)


def stage_attn1(nc, env, inp):
    X, XTh, XTl, ident = env["X"], env["XTh"], env["XTl"], env["ident"]
    H, DH = 16, P
    SCALE = 1.0 / math.sqrt(DH)
    N = H * NG
    BODY = 2 * NG
    FIRST = 3
    TURNS = (N - FIRST - NG - 2) // BODY
    QKV = 3 * DH
    with ExitStack() as ctx:
        m = Mem(nc, ctx)
        w_raw = m.sb("a1_w_raw", [P, 2, DT, 2, QKV])
        w_bias = m.sb("a1_w_bias", [P, 2, 3])
        w_full = m.sb("a1_w_full", [P, DT, QKV])
        w_hi = m.sb("a1_w_hi", [P, 2, DT, QKV], F32R)
        w_lo = m.sb("a1_w_lo", [P, 2, DT, QKV], F32R)
        o_raw = m.sb("a1_o_raw", [P, 2, 2, D])
        o_full = m.sb("a1_o_full", [P, D])
        o_hi = m.sb("a1_o_hi", [P, 2, D], F32R)
        o_lo = m.sb("a1_o_lo", [P, 2, D], F32R)
        bo = m.sb("a1_bo", [P, D])
        qT = m.sb("a1_qT", [P, 4, GT])
        kT = m.sb("a1_kT", [P, 4, GT])
        vT = m.sb("a1_vT", [P, GT])
        v = m.sb("a1_v", [P, 4, GT])
        negmax = m.sb("a1_negmax", [P, 2, G])
        shift = m.sb("a1_shift", [P, 2, G])
        sums = m.sb("a1_sums", [P, 2, G])
        recip = m.sb("a1_recip", [P, 2, G])
        probs = m.sb("a1_probs", [P, 2, G, T])
        normed = m.sb("a1_normed", [P, 2, G, T])
        normedT = m.sb("a1_normedT", [P, 2, GT])
        head_hi = m.sb("a1_head_hi", [P, 2, GT], F32R)
        head_lo = m.sb("a1_head_lo", [P, 2, GT], F32R)
        proj_ps = [m.ps(f"a1_proj_ps{i}", [P, BANK]) for i in range(2)]
        s_ps = m.ps("a1_s_ps", [P, BANK])
        nT_ps = m.ps("a1_nT_ps", [P, BANK])
        v_ps = m.ps("a1_v_ps", [P, BANK])
        head_ps = m.ps("a1_head_ps", [P, BANK])
        out_ps = [m.ps(f"a1_out_ps{i}", [P, BANK]) for i in range(2)]
        w_in = [m.sem(f"a1_w_in{i}") for i in range(2)]
        o_in = [m.sem(f"a1_o_in{i}") for i in range(2)]
        b_in = [m.sem(f"a1_b_in{i}") for i in range(2)]
        bo_in = m.sem("a1_bo_in")
        bo_done = m.sem("a1_bo_done")
        wfull_done = m.sem("a1_wfull_done")
        whi_done = m.sem("a1_whi_done")
        wlo_done = m.sem("a1_wlo_done")
        ofull_done = m.sem("a1_ofull_done")
        ohi_done = m.sem("a1_ohi_done")
        olo_done = m.sem("a1_olo_done")
        projected = m.sem("a1_projected")
        proj_read = m.sem("a1_proj_read")
        v_turned = m.sem("a1_v_turned")
        v_done = m.sem("a1_v_done")
        scored = m.sem("a1_scored")
        maxed = m.sem("a1_maxed")
        shifted = m.sem("a1_shifted")
        exped = m.sem("a1_exped")
        recip_done = m.sem("a1_recip_done")
        normed_done = m.sem("a1_normed_done")
        turned = m.sem("a1_turned")
        nT_done = m.sem("a1_nT_done")
        valued = m.sem("a1_valued")
        hi_done = m.sem("a1_hi_done")
        lo_done = m.sem("a1_lo_done")
        multiplied = m.sem("a1_multiplied")
        added = m.sem("a1_added")
        block = ctx.enter_context(nc.Block())

        def run(eng, step):
            for k in range(FIRST):
                step(0, k)
            with eng.Fori(0, TURNS) as i:
                for k in range(FIRST, FIRST + BODY):
                    step(i, k)
            for k in range(FIRST, N + 3 - TURNS * BODY):
                step(TURNS, k)

        def inside(i, k):
            return not isinstance(i, int) or 0 <= i * BODY + k < N

        def w_low(pool, i, h):
            pool.wait_ge(whi_done, i * 2 + (h + 1))
            nc.gpsimd.tensor_tensor(w_lo[:, h % 2, :, :], w_full[:, :, :], w_hi[:, h % 2, :, :].bitcast(F32),
                                    ALU.subtract).then_inc(wlo_done, 1)

        def w_high(act, i, h):
            act.wait_ge(wfull_done, i * 2 + (h + 1))
            nc.scalar.activation(w_hi[:, h % 2, :, :], w_full[:, :, :], ACT.Copy).then_inc(whi_done, 1)

        def w_multiply(dve, i, h):
            dve.wait_ge(w_in[h % 2], i * 16 + (h // 2 + 1) * 16)
            if not (isinstance(i, int) and i * BODY + h == 0):
                dve.wait_ge(wlo_done, i * 2 + h)
            nc.vector.tensor_tensor(w_full[:, :, :], w_raw[:, h % 2, :, 0, :], w_raw[:, h % 2, :, 1, :], ALU.mult)\
                .then_inc(wfull_done, 1)

        def project_read(act, i, k):
            par = k // NG % 2
            if k % NG == 0:
                act.wait_ge(b_in[par], i * 16 + (k // BODY + 1) * 16)
            for a, dst in enumerate((qT[:, k % 4, :], kT[:, k % 4, :], vT[:, :])):
                act.wait_ge(projected, i * (3 * BODY) + (3 * k + a + 1))
                nc.scalar.activation(dst, proj_ps[(3 * k + a) % 2][:, :], ACT.Identity, bias=w_bias[:, par, a:a + 1])\
                    .then_inc(proj_read, 1)
            if isinstance(i, int) and i * BODY + k < 2:
                act.wait_ge(v_turned, k + 1)
                nc.scalar.activation(v[:, k % 4, :], v_ps[:, :], ACT.Copy).then_inc(v_done, 1)

        @block.sync
        def _(sp):
            sp.dma_start(bo[:, :], inp["a1_bo"].partition_broadcast(P)).then_inc(bo_in, 16)

            def load(h, par, guard):
                if guard is not None:
                    sp.wait_ge(wlo_done, guard)
                    sp.wait_ge(olo_done, guard)
                    hold(sp)
                pick = (lambda x: x[bass.ds(h, 1)].rearrange("o r c -> r (o c)")) if guard is not None else (lambda x: x[h])
                w_src = pick(inp["a1_w"])
                sp.dma_start(w_raw[:, par, :, :, :].rearrange("p k a n -> p k (a n)"),
                             w_src.rearrange("(k p) n -> p k n", p=P)).then_inc(w_in[par], 16)
                sp.dma_start(o_raw[:, par, :, :].rearrange("p a n -> p (a n)"), pick(inp["a1_wo"])).then_inc(o_in[par], 16)
                if guard is not None:
                    sp.wait_ge(proj_read, guard * (3 * NG))
                    hold(sp)
                sp.dma_start(w_bias[:, par, :], pick(inp["a1_bias"])).then_inc(b_in[par], 16)

            for h in range(2):
                load(h, h, None)
            with sp.Fori(1, H // 2) as i:
                for par in range(2):
                    load(i * 2 + par, par, i * 2 + (par - 1))

        @block.gpsimd
        def _(pool):
            w_low(pool, 0, 0)
            w_low(pool, 0, 1)
            pool.wait_ge(bo_in, 16)
            nc.gpsimd.tensor_tensor(X[:, :, :], X[:, :, :], bo[:, :].unsqueeze(1).broadcast_to([P, B, D]), ALU.add)\
                .then_inc(bo_done, 1)

            def step(i, k):
                if inside(i, k):
                    pool.wait_ge(recip_done, i * BODY + (k + 1))
                    nc.gpsimd.tensor_tensor(normed[:, k % 2, :, :], probs[:, k % 2, :, :],
                                            recip[:, k % 2, :].unsqueeze(2).broadcast_to([P, G, T]), ALU.mult)\
                        .then_inc(normed_done, 1)
                if k % NG == 2 and inside(i, k + 6):
                    w_low(pool, i, (k + 6) // NG)
                if k % NG == 0 and inside(i, k):
                    hq = k // NG
                    pool.wait_ge(ohi_done, i * 2 + (hq + 1))
                    nc.gpsimd.tensor_tensor(o_lo[:, hq % 2, :], o_full[:, :], o_hi[:, hq % 2, :].bitcast(F32),
                                            ALU.subtract).then_inc(olo_done, 1)

            run(pool, step)

        @block.scalar
        def _(act):
            w_high(act, 0, 0)
            project_read(act, 0, 0)
            w_high(act, 0, 1)
            project_read(act, 0, 1)

            def step(i, k):
                if inside(i, k):
                    act.wait_ge(shifted, i * BODY + (k + 1))
                    for j in range(G):
                        nc.scalar.activation(probs[:, k % 2, j, :], s_ps[:, j * T:(j + 1) * T], ACT.Exp, scale=SCALE,
                                             bias=shift[:, k % 2, j:j + 1], accum_out=sums[:, k % 2, j:j + 1])\
                            .then_inc(exped, 1)
                if inside(i, k - 1):
                    act.wait_ge(turned, i * BODY + k)
                    nc.scalar.activation(normedT[:, (k - 1) % 2, :], nT_ps[:, :], ACT.Copy).then_inc(nT_done, 1)
                if inside(i, k + 2):
                    project_read(act, i, k + 2)
                if inside(i, k - 1):
                    act.wait_ge(valued, i * BODY + k)
                    nc.scalar.activation(head_hi[:, (k - 1) % 2, :], head_ps[:, :], ACT.Copy).then_inc(hi_done, 1)
                if inside(i, k + 2):
                    act.wait_ge(v_turned, i * BODY + (k + 3))
                    nc.scalar.activation(v[:, (k + 2) % 4, :], v_ps[:, :], ACT.Copy).then_inc(v_done, 1)
                if k % NG == 2 and inside(i, k + 6):
                    w_high(act, i, (k + 6) // NG)
                if k % NG == 0 and inside(i, k):
                    hq = k // NG
                    act.wait_ge(ofull_done, i * 2 + (hq + 1))
                    nc.scalar.activation(o_hi[:, hq % 2, :], o_full[:, :], ACT.Copy).then_inc(ohi_done, 1)

            run(act, step)

        @block.vector
        def _(dve):
            w_multiply(dve, 0, 0)
            w_multiply(dve, 0, 1)

            def step(i, k):
                if inside(i, k):
                    dve.wait_ge(scored, i * BODY + (k + 1))
                    nc.vector.tensor_reduce(negmax[:, k % 2, :], s_ps[:, :].rearrange("p (b s) -> p b s", b=G),
                                            AX_X, ALU.max, negate=True).then_inc(maxed, 1)
                    dve.wait_ge(maxed, i * BODY + (k + 1))
                    nc.vector.tensor_scalar(shift[:, k % 2, :], negmax[:, k % 2, :], SCALE, None, ALU.mult)\
                        .then_inc(shifted, 1)
                if inside(i, k - 3):
                    g = (k - 3) % NG
                    if isinstance(i, int) and i * BODY + k == 3:
                        dve.wait_ge(bo_done, 1)
                    dve.wait_ge(multiplied, i * BODY + (k - 2))
                    for c in range(2):
                        xs = X[:, g * G + 2 * c:g * G + 2 * c + 2, :].rearrange("p b d -> p (b d)")
                        last = nc.vector.tensor_tensor(xs, xs, out_ps[c][:, :], ALU.add)
                    last.then_inc(added, 1)
                if k % NG == 2 and inside(i, k + 6):
                    w_multiply(dve, i, (k + 6) // NG)
                if k % NG == 0 and inside(i, k):
                    hq = k // NG
                    dve.wait_ge(o_in[hq % 2], i * 16 + (hq // 2 + 1) * 16)
                    if hq or not isinstance(i, int) or i:
                        dve.wait_ge(olo_done, i * 2 + hq)
                    nc.vector.tensor_tensor(o_full[:, :], o_raw[:, hq % 2, 0, :], o_raw[:, hq % 2, 1, :], ALU.mult)\
                        .then_inc(ofull_done, 1)
                if inside(i, k):
                    dve.wait_ge(exped, i * (G * BODY) + (G * k + G))
                    nc.vector.reciprocal(recip[:, k % 2, :], sums[:, k % 2, :]).then_inc(recip_done, 1)
                if inside(i, k - 1):
                    dve.wait_ge(hi_done, i * BODY + k)
                    nc.vector.tensor_tensor(head_lo[:, (k - 1) % 2, :], head_ps[:, :],
                                            head_hi[:, (k - 1) % 2, :].bitcast(F32), ALU.subtract).then_inc(lo_done, 1)

            run(dve, step)

        @block.tensor
        def _(pe):
            def project(i, k):
                g, par = k % NG, k // NG % 2
                toks = slice(g * GT, (g + 1) * GT)
                if g == 0:
                    pe.wait_ge(wlo_done, i * 2 + (k // NG + 1))
                for a in range(3):
                    p = 3 * k + a
                    if not (isinstance(i, int) and i * BODY * 3 + p < 2):
                        pe.wait_ge(proj_read, i * (3 * BODY) + (p - 1))
                    c = slice(a * DH, (a + 1) * DH)
                    halves(nc, proj_ps[p % 2][:, :],
                           [lambda dt: w_hi[:, par, dt, c], lambda dt: w_lo[:, par, dt, c]],
                           [lambda dt: XTh[:, dt, toks], lambda dt: XTl[:, dt, toks]], DT).then_inc(projected, 1)

            def turn_values(i, k):
                pe.wait_ge(proj_read, i * (3 * BODY) + (3 * k + 3))
                if not (isinstance(i, int) and i * BODY + k < 1):
                    pe.wait_ge(v_done, i * BODY + k)
                for j in range(G):
                    last = nc.tensor.transpose(v_ps[:, j * T:(j + 1) * T], vT[:, j * T:(j + 1) * T], ident[:, :])
                last.then_inc(v_turned, 1)

            for k in range(2):
                project(0, k)
                turn_values(0, k)

            def step(i, k):
                if inside(i, k):
                    if not (isinstance(i, int) and i * BODY + k < 1):
                        pe.wait_ge(exped, i * (G * BODY) + G * k)
                    pe.wait_ge(proj_read, i * (3 * BODY) + (3 * k + 2))
                    for j in range(G):
                        toks = slice(j * T, (j + 1) * T)
                        last = nc.tensor.matmul(s_ps[:, toks], qT[:, k % 4, toks], kT[:, k % 4, toks],
                                                start=True, stop=True)
                    last.then_inc(scored, 1)
                if inside(i, k - 1):
                    pe.wait_ge(normed_done, i * BODY + k)
                    for j in range(G):
                        last = nc.tensor.transpose(nT_ps[:, j * T:(j + 1) * T], normed[:, (k - 1) % 2, j, :], ident[:, :])
                    last.then_inc(turned, 1)
                if inside(i, k + 2):
                    project(i, k + 2)
                if inside(i, k - 1):
                    pe.wait_ge(nT_done, i * BODY + k)
                    if inside(i, k - 2):
                        pe.wait_ge(lo_done, i * BODY + (k - 1))
                    pe.wait_ge(v_done, i * BODY + k)
                    for j in range(G):
                        toks = slice(j * T, (j + 1) * T)
                        last = nc.tensor.matmul(head_ps[:, toks], v[:, (k - 1) % 4, toks], normedT[:, (k - 1) % 2, toks],
                                                start=True, stop=True)
                    last.then_inc(valued, 1)
                if inside(i, k + 2):
                    turn_values(i, k + 2)
                if inside(i, k - 2):
                    q, hq = (k - 2) % 2, (k - 2) // NG
                    pe.wait_ge(lo_done, i * BODY + (k - 1))
                    pe.wait_ge(olo_done, i * 2 + (hq + 1))
                    if inside(i, k - 3):
                        pe.wait_ge(added, i * BODY + (k - 2))
                    for j in range(G):
                        toks = slice(j * T, (j + 1) * T)
                        last = halves(nc, out_ps[j // 2][:, (j % 2) * D:(j % 2 + 1) * D],
                                      [lambda n: head_hi[:, q, toks], lambda n: head_lo[:, q, toks]],
                                      [lambda n: o_hi[:, hq % 2, :], lambda n: o_lo[:, hq % 2, :]], 1)
                    last.then_inc(multiplied, 1)

            run(pe, step)


def stage_wkv1(nc, env, inp):
    X, XTk, ident = env["X"], env["XTk"], env["ident"]
    N = NG * DT
    LOW = -1e38
    with ExitStack() as ctx:
        m = Mem(nc, ctx)
        values = m.sb("k1_values", [P, DT, B * T])
        decay = m.sb("k1_decay", [P, DT])
        first = m.sb("k1_first", [P, DT])
        exp_decay = m.sb("k1_exp_decay", [P, DT])
        w = m.sb("k1_w", [P, DT])
        w_row = m.sb("k1_w_row", [P, DT, G, T + 1])
        pp = m.sb("k1_pp", [P, 2, G, T + 1])
        aa = m.sb("k1_aa", [P, G, T + 1])
        bb = m.sb("k1_bb", [P, G, T + 1])
        q = m.sb("k1_q", [P, G, T])
        d_out = m.sb("k1_d_out", [P, 2, 2, G, T])
        d_next = m.sb("k1_d_next", [P, 2, 2, G, T])
        e_out = m.sb("k1_e_out", [P, 2, 2, G, T])
        e_next = m.sb("k1_e_next", [P, 2, 2, G, T + 1])
        ev_next = m.sb("k1_ev_next", [P, 2, G, T + 1])
        ev_out = m.sb("k1_ev_out", [P, 2, G, T])
        num = m.sb("k1_num", [P, G, T])
        den = m.sb("k1_den", [P, G, T])
        num_sum = m.sb("k1_num_sum", [P, G, T])
        den_sum = m.sb("k1_den_sum", [P, G, T])
        den_inv = m.sb("k1_den_inv", [P, G, T])
        y = m.sb("k1_y", [P, 2, G, T])
        y_ps = [m.ps(f"k1_y_ps{i}", [P, BANK]) for i in range(2)]
        v_in = m.sem("k1_v_in")
        p_in = m.sem("k1_p_in")
        exp_decay_done = m.sem("k1_exp_decay_done")
        w_done = m.sem("k1_w_done")
        row_done = m.sem("k1_row_done")
        starts = m.sem("k1_starts")
        pp_done = m.sem("k1_pp_done")
        q_done = m.sem("k1_q_done")
        dve_exponents = m.sem("k1_dve_exponents")
        pool_exponents = m.sem("k1_pool_exponents")
        next_done = m.sem("k1_next_done")
        out_done = m.sem("k1_out_done")
        ev_next_done = m.sem("k1_ev_next_done")
        ev_out_done = m.sem("k1_ev_out_done")
        scanned = m.sem("k1_scanned")
        weighted = m.sem("k1_weighted")
        summed = m.sem("k1_summed")
        inverted = m.sem("k1_inverted")
        y_done = m.sem("k1_y_done")
        turned = m.sem("k1_turned")
        added = m.sem("k1_added")
        block = ctx.enter_context(nc.Block())

        def group(g, n):
            return slice(g * n, (g + 1) * n) if isinstance(g, int) else bass.ds(g * n, n)

        def k_of(g, ct):
            return XTk[:, ct, group(g, G), 1:T + 1]

        def v_of(g, ct):
            return values[:, ct, group(g, GT)].rearrange("p (b t) -> p b t", b=G)

        def flat(ap):
            return ap.rearrange("p b t -> p (b t)")

        @block.sync
        def _(sp):
            sp.dma_start(decay[:, :], inp["k1_decay"]).then_inc(p_in, 16)
            sp.dma_start(first[:, :], inp["k1_first"]).then_inc(p_in, 16)
            sp.dma_start(values[:, :, :], inp["ctxT"].rearrange("k p n -> p k n")).then_inc(v_in, 16)

        @block.scalar
        def _(act):
            act.wait_ge(p_in, 32)
            nc.scalar.activation(exp_decay[:, :], decay[:, :], ACT.Exp).then_inc(exp_decay_done, 1)
            with act.Fori(0, NG) as g:
                for ct in range(DT):
                    act.wait_ge(dve_exponents, g * (2 * DT) + (2 * ct + 2))
                    act.wait_ge(pool_exponents, g * (2 * DT) + (2 * ct + 3))
                    act.wait_ge(y_done, g * DT + (ct + 1))
                    nc.scalar.activation(e_next[:, ct, :, :, 1:T + 1].rearrange("p k b t -> p (k b) t"),
                                         d_next[:, ct, :, :, :].rearrange("p k b t -> p (k b) t"), ACT.Exp)\
                        .then_inc(next_done, 1)
                    nc.scalar.activation(e_out[:, ct, :, :, :], d_out[:, ct, :, :, :], ACT.Exp).then_inc(out_done, 1)

        @block.gpsimd
        def _(pool):
            pool.wait_ge(exp_decay_done, 1)
            nc.gpsimd.tensor_scalar(w[:, :], exp_decay[:, :], -1.0, None, ALU.mult).then_inc(w_done, 1)
            pool.wait_ge(w_done, 1)
            for ct in range(DT):
                nc.gpsimd.tensor_copy(w_row[:, ct, :, 1:T + 1], w[:, ct:ct + 1].unsqueeze(2).broadcast_to([P, G, T]))\
                    .then_inc(row_done, 1)
                nc.gpsimd.memset(w_row[:, ct, :, 0:1], LOW).then_inc(row_done, 1)
                nc.gpsimd.memset(XTk[:, ct, :, 0:1], LOW).then_inc(starts, 1)
                nc.gpsimd.memset(ev_next[:, ct, :, 0:1], 0.0).then_inc(starts, 1)
                for k in range(2):
                    nc.gpsimd.memset(e_next[:, ct, k, :, 0:1], 0.0).then_inc(starts, 1)

            def exponents(g, ct):
                pool.wait_ge(q_done, g * DT + (ct + 1))
                pool.wait_ge(next_done, g * DT + (ct + 1))
                hold(pool)
                nc.gpsimd.tensor_tensor(d_next[:, ct, 1, :, :], k_of(g, ct), pp[:, ct, :, 1:T + 1], ALU.subtract)\
                    .then_inc(pool_exponents, 1)
                pool.wait_ge(out_done, g * DT + (ct + 1))
                nc.gpsimd.tensor_tensor(d_out[:, ct, 0, :, :], pp[:, ct, :, 0:T], q[:, :, :], ALU.subtract)\
                    .then_inc(pool_exponents, 1)

            def weigh(g, ct):
                pool.wait_ge(next_done, g * DT + (ct + 3))
                pool.wait_ge(y_done, g * DT + (ct + 1))
                hold(pool)
                nc.gpsimd.tensor_tensor(ev_next[:, ct, :, 1:T + 1], e_next[:, ct, 1, :, 1:T + 1], v_of(g, ct), ALU.mult)\
                    .then_inc(ev_next_done, 1)
                pool.wait_ge(out_done, g * DT + (ct + 3))
                hold(pool)
                nc.gpsimd.tensor_tensor(ev_out[:, ct, :, :], e_out[:, ct, 1, :, :], v_of(g, ct), ALU.mult)\
                    .then_inc(ev_out_done, 1)

            pool.sem_inc(next_done, 2)
            pool.sem_inc(out_done, 2)
            pool.wait_ge(v_in, 16)
            exponents(0, 0)
            with pool.Fori(0, NG - 1) as g:
                exponents(g, 1)
                weigh(g, 0)
                exponents(g + 1, 0)
                weigh(g, 1)
            exponents(NG - 1, 1)
            weigh(NG - 1, 0)
            weigh(NG - 1, 1)

        @block.vector
        def _(dve):
            def exponents(g, ct):
                dve.wait_ge(pool_exponents, g * (2 * DT) + (2 * ct + 1))
                hold(dve)
                nc.vector.tensor_tensor_scan(flat(pp[:, ct, :, :]), flat(w_row[:, ct, :, :]),
                                             flat(XTk[:, ct, group(g, G), :]), LOW,
                                             ALU.add, ALU.max).then_inc(pp_done, 1)
                dve.wait_ge(pp_done, g * DT + (ct + 1))
                hold(dve)
                nc.vector.scalar_tensor_tensor(q[:, :, :], k_of(g, ct), first[:, ct:ct + 1], pp[:, ct, :, 0:T],
                                               ALU.add, ALU.max).then_inc(q_done, 1)
                nc.vector.scalar_tensor_tensor(d_next[:, ct, 0, :, :], pp[:, ct, :, 0:T], w[:, ct:ct + 1],
                                               pp[:, ct, :, 1:T + 1], ALU.add, ALU.subtract).then_inc(dve_exponents, 1)
                dve.wait_ge(q_done, g * DT + (ct + 1))
                hold(dve)
                nc.vector.scalar_tensor_tensor(d_out[:, ct, 1, :, :], k_of(g, ct), first[:, ct:ct + 1], q[:, :, :],
                                               ALU.add, ALU.subtract).then_inc(dve_exponents, 1)

            def output(g, ct):
                n = g * DT + ct
                tt = nc.vector.tensor_tensor
                dve.wait_ge(next_done, n + 3)
                nc.vector.tensor_tensor_scan(flat(bb[:, :, :]), flat(e_next[:, ct, 0, :, :]), flat(e_next[:, ct, 1, :, :]), 0.0,
                                             ALU.mult, ALU.add).then_inc(scanned, 1)
                dve.wait_ge(ev_next_done, n + 1)
                nc.vector.tensor_tensor_scan(flat(aa[:, :, :]), flat(e_next[:, ct, 0, :, :]), flat(ev_next[:, ct, :, :]), 0.0,
                                             ALU.mult, ALU.add).then_inc(scanned, 1)
                dve.wait_ge(out_done, n + 3)
                dve.wait_ge(scanned, n * 2 + 1)
                tt(den[:, :, :], e_out[:, ct, 0, :, :], bb[:, :, 0:T], ALU.mult).then_inc(weighted, 1)
                dve.wait_ge(scanned, n * 2 + 2)
                tt(num[:, :, :], e_out[:, ct, 0, :, :], aa[:, :, 0:T], ALU.mult).then_inc(weighted, 1)
                dve.wait_ge(weighted, n * 2 + 1)
                tt(den_sum[:, :, :], den[:, :, :], e_out[:, ct, 1, :, :], ALU.add).then_inc(summed, 1)
                dve.wait_ge(weighted, n * 2 + 2)
                dve.wait_ge(ev_out_done, n + 1)
                tt(num_sum[:, :, :], num[:, :, :], ev_out[:, ct, :, :], ALU.add).then_inc(summed, 1)
                dve.wait_ge(summed, n * 2 + 1)
                nc.vector.reciprocal(den_inv[:, :, :], den_sum[:, :, :]).then_inc(inverted, 1)
                dve.wait_ge(summed, n * 2 + 2)
                dve.wait_ge(inverted, n + 1)
                dve.wait_ge(turned, n + 1)
                tt(y[:, ct, :, :], num_sum[:, :, :], den_inv[:, :, :], ALU.mult).then_inc(y_done, 1)

            def add(g, ct):
                n = g * DT + ct
                dve.wait_ge(turned, n + 3)
                hold(dve)
                xs = X[:, group(g, G), ct * P:(ct + 1) * P]
                nc.vector.tensor_tensor(xs, xs, y_ps[ct][:, :].rearrange("p (b c) -> p b c", b=G), ALU.add)\
                    .then_inc(added, 1)

            dve.sem_inc(pool_exponents, 1)
            dve.sem_inc(y_done, 2)
            dve.wait_ge(row_done, 2 * DT)
            dve.wait_ge(starts, 4 * DT)
            hold(dve)
            exponents(0, 0)
            with dve.Fori(0, NG - 1) as g:
                exponents(g, 1)
                output(g, 0)
                exponents(g + 1, 0)
                add(g, 0)
                output(g, 1)
                add(g, 1)
            exponents(NG - 1, 1)
            for ct in range(DT):
                output(NG - 1, ct)
                add(NG - 1, ct)

        @block.tensor
        def _(pe):
            pe.sem_inc(turned, 2)
            pe.sem_inc(added, 2)
            with pe.Fori(0, NG) as g:
                for ct in range(DT):
                    pe.wait_ge(y_done, g * DT + (ct + 3))
                    pe.wait_ge(added, g * DT + (ct + 1))
                    for j in range(G):
                        last = nc.tensor.transpose(y_ps[ct][:, j * P:(j + 1) * P], y[:, ct, j, :], ident[:, :])
                    last.then_inc(turned, 1)


def stage_ffn1(nc, env, inp):
    X, XTh, XTl, ident = env["X"], env["XTh"], env["XTl"], env["ident"]
    E, R = 8, 16
    SCALING = 32.0 / R
    LG = slice(D, D + E)
    LR = slice(D + E, D + E + E * R)
    W = D + E + E * R
    with ExitStack() as ctx:
        m = Mem(nc, ctx)
        w_raw = m.sb("f1_w_raw", [P, DT, W])
        w_hi = m.sb("f1_w_hi", [P, DT, W], F32R)
        w_lo = m.sb("f1_w_lo", [P, DT, W], F32R)
        b_raw = m.sb("f1_b_raw", [P, D])
        b_hi = m.sb("f1_b_hi", [P, D], F32R)
        b_lo = m.sb("f1_b_lo", [P, D], F32R)
        bias = m.sb("f1_bias", [P, D])
        rank = m.sb("f1_rank", [P, E])
        x_hi = m.sb("f1_x_hi", [P, DT, GT], F32R)
        x_lo = m.sb("f1_x_lo", [P, DT, GT], F32R)
        best = m.sb("f1_best", [P, G])
        tie = m.sb("f1_tie", [P, G, E])
        order = m.sb("f1_order", [P, G, E])
        best_rank = m.sb("f1_best_rank", [P, G])
        chosen = m.sb("f1_chosen", [P, G, E])
        low = m.sb("f1_low", [P, G, E * R])
        low_hi = m.sb("f1_low_hi", [P, GT], F32R)
        low_lo = m.sb("f1_low_lo", [P, GT], F32R)
        in_ps = m.ps("f1_in_ps", [P, G, BANK])
        lowT_ps = m.ps("f1_lowT_ps", [P, BANK])
        delta_ps = m.ps("f1_delta_ps", [P, G, D])
        w_in = m.sem("f1_w_in")
        b_in = m.sem("f1_b_in")
        whi_done = m.sem("f1_whi_done")
        wlo_done = m.sem("f1_wlo_done")
        bhi_done = m.sem("f1_bhi_done")
        blo_done = m.sem("f1_blo_done")
        bias_done = m.sem("f1_bias_done")
        xhi_done = m.sem("f1_xhi_done")
        xlo_done = m.sem("f1_xlo_done")
        multiplied = m.sem("f1_multiplied")
        routed = m.sem("f1_routed")
        low_done = m.sem("f1_low_done")
        turned = m.sem("f1_turned")
        low_hi_done = m.sem("f1_low_hi_done")
        low_lo_done = m.sem("f1_low_lo_done")
        base_added = m.sem("f1_base_added")
        delta_done = m.sem("f1_delta_done")
        delta_added = m.sem("f1_delta_added")
        block = ctx.enter_context(nc.Block())

        @block.sync
        def _(sp):
            sp.dma_start(w_raw[:, :, :], inp["f1_w"].rearrange("(k p) n -> p k n", p=P)).then_inc(w_in, 16)
            sp.dma_start(b_raw[:, :], inp["f1_b"]).then_inc(b_in, 16)
            sp.dma_start(bias[:, :], inp["f1_bias"].partition_broadcast(P)).then_inc(b_in, 16)
            sp.dma_start(rank[:, :], inp["m0_rank"].partition_broadcast(P)).then_inc(b_in, 16)

        @block.gpsimd
        def _(pool):
            pool.wait_ge(b_in, 48)
            nc.gpsimd.tensor_tensor(X[:, :, :], X[:, :, :], bias[:, :].unsqueeze(1).broadcast_to([P, B, D]), ALU.add)\
                .then_inc(bias_done, 1)
            with pool.Fori(0, NG) as g:
                pool.wait_ge(multiplied, g + 1)
                hold(pool)
                nc.gpsimd.tensor_copy(x_lo[:, :, :], XTl[:, :, bass.ds(g * GT, GT)]).then_inc(xlo_done, 1)

        @block.scalar
        def _(act):
            act.wait_ge(w_in, 16)
            nc.scalar.activation(w_hi[:, :, :], w_raw[:, :, :], ACT.Copy).then_inc(whi_done, 1)
            act.wait_ge(b_in, 48)
            nc.scalar.activation(b_hi[:, :], b_raw[:, :], ACT.Copy, scale=SCALING).then_inc(bhi_done, 1)
            with act.Fori(0, NG) as g:
                act.wait_ge(multiplied, g + 1)
                hold(act)
                nc.scalar.activation(x_hi[:, :, :], XTh[:, :, bass.ds(g * GT, GT)].bitcast(F32), ACT.Copy)\
                    .then_inc(xhi_done, 1)
                act.wait_ge(turned, g + 1)
                nc.scalar.activation(low_hi[:, :], lowT_ps[:, :], ACT.Copy).then_inc(low_hi_done, 1)

        @block.vector
        def _(dve):
            dve.wait_ge(whi_done, 1)
            nc.vector.tensor_tensor(w_lo[:, :, :], w_raw[:, :, :], w_hi[:, :, :].bitcast(F32), ALU.subtract)\
                .then_inc(wlo_done, 1)
            dve.wait_ge(bhi_done, 1)
            nc.vector.scalar_tensor_tensor(b_lo[:, :], b_raw[:, :], SCALING, b_hi[:, :].bitcast(F32), ALU.mult, ALU.subtract)\
                .then_inc(blo_done, 1)
            dve.wait_ge(bias_done, 1)
            hold(dve)
            tt = nc.vector.tensor_tensor
            with dve.Fori(0, NG) as g:
                dve.wait_ge(multiplied, g + 2)
                hold(dve)
                nc.vector.tensor_reduce(best[:, :], in_ps[:, :, LG], AX_X, ALU.max).then_inc(routed, 1)
                dve.wait_ge(routed, g * 5 + 1)
                tt(tie[:, :, :], in_ps[:, :, LG], best[:, :].unsqueeze(2).broadcast_to([P, G, E]), ALU.is_equal)\
                    .then_inc(routed, 1)
                dve.wait_ge(routed, g * 5 + 2)
                tt(order[:, :, :], tie[:, :, :], rank[:, :].unsqueeze(1).broadcast_to([P, G, E]), ALU.mult)\
                    .then_inc(routed, 1)
                dve.wait_ge(routed, g * 5 + 3)
                hold(dve)
                nc.vector.tensor_reduce(best_rank[:, :], order[:, :, :], AX_X, ALU.max).then_inc(routed, 1)
                dve.wait_ge(routed, g * 5 + 4)
                tt(chosen[:, :, :], order[:, :, :], best_rank[:, :].unsqueeze(2).broadcast_to([P, G, E]), ALU.is_equal)\
                    .then_inc(routed, 1)
                dve.wait_ge(routed, g * 5 + 5)
                tt(low[:, :, :].rearrange("p b (e r) -> p b e r", e=E),
                   in_ps[:, :, LR].rearrange("p b (e r) -> p b e r", e=E),
                   chosen[:, :, :].unsqueeze(3).broadcast_to([P, G, E, R]), ALU.mult).then_inc(low_done, 1)
                xs = X[:, bass.ds(g * G, G), :]
                hold(dve)
                tt(xs, xs, in_ps[:, :, 0:D], ALU.add).then_inc(base_added, 1)
                dve.wait_ge(low_hi_done, g + 1)
                tt(low_lo[:, :], lowT_ps[:, :], low_hi[:, :].bitcast(F32), ALU.subtract).then_inc(low_lo_done, 1)
                dve.wait_ge(delta_done, g + 1)
                dve.wait_ge(base_added, g + 1)
                hold(dve)
                tt(xs, xs, delta_ps[:, :, :], ALU.add).then_inc(delta_added, 1)

        @block.tensor
        def _(pe):
            pe.sem_inc(multiplied, 1)
            pe.wait_ge(wlo_done, 1)
            pe.wait_ge(blo_done, 1)
            hold(pe)
            with pe.Fori(0, NG) as g:
                pe.wait_ge(xhi_done, g + 1)
                pe.wait_ge(xlo_done, g + 1)
                hold(pe)
                for j in range(G):
                    toks = slice(j * T, (j + 1) * T)
                    last = halves(nc, in_ps[:, j, 0:W], [lambda dt: x_hi[:, dt, toks], lambda dt: x_lo[:, dt, toks]],
                                  [lambda dt: w_hi[:, dt, :], lambda dt: w_lo[:, dt, :]], DT)
                last.then_inc(multiplied, 1)
                pe.wait_ge(low_done, g + 1)
                for j in range(G):
                    last = nc.tensor.transpose(lowT_ps[:, j * T:(j + 1) * T], low[:, j, :], ident[:, :])
                last.then_inc(turned, 1)
                pe.wait_ge(low_lo_done, g + 1)
                for j in range(G):
                    toks = slice(j * T, (j + 1) * T)
                    last = halves(nc, delta_ps[:, j, :], [lambda n: low_hi[:, toks], lambda n: low_lo[:, toks]],
                                  [lambda n: b_hi[:, :], lambda n: b_lo[:, :]], 1)
                last.then_inc(delta_done, 1)
                pe.wait_ge(delta_added, g + 1)
                hold(pe)


def stage_context(nc, env, inp):
    with ExitStack() as ctx:
        ctx_in = Mem(nc, ctx).sem("ctx_in")
        block = ctx.enter_context(nc.Block())

        @block.sync
        def _(sp):
            sp.dma_start(env["C"][:, :, :, :].rearrange("p m t b -> p (m t b)"), inp["c0_ctx"]).then_inc(ctx_in, 16)
            sp.wait_ge(ctx_in, 16)
            hold(sp)


def program(nc, inp, out):
    with ExitStack() as ctx:
        m = Mem(nc, ctx)
        env = {
            "X": m.sb("X", [P, B, D]),
            "XTh": m.sb("XTh", [P, DT, B * T], F32R),
            "XTl": m.sb("XTl", [P, DT, B * T], F32R),
            "ident": m.sb("ident", [P, P]),
            "ones": m.sb("ones", [P, P]),
            "minus_half": m.sb("minus_half", [P, 16]),
        }
        stage_load(nc, env, inp)
        with ExitStack() as c0:
            env["OT"] = Mem(nc, c0).sb("OT", [P, B, REP0 * T])
            stage_attn0_heads(nc, env, inp)
            stage_attn0_out(nc, env, inp)
        with ExitStack() as c0:
            env["XTf"] = Mem(nc, c0).sb("XTf", [P, DT, B * T])
            stage_norm(nc, env, "ln0", "whole")
            env["C"] = Mem(nc, c0).sb("C", [P, DT, T, B])
            env["Z"] = Mem(nc, c0).sb("Z", [P, DT, B, T])
            stage_context(nc, env, inp)
            stage_conv0(nc, env, inp)
            stage_conv0_out(nc, env)
        stage_norm(nc, env, "ln1", "halves")
        stage_moe0(nc, env, inp)
        stage_norm(nc, env, "ln2", "halves")
        stage_attn1(nc, env, inp)
        with ExitStack() as c1:
            env["XTk"] = Mem(nc, c1).sb("XTk", [P, DT, B, T + 1])
            stage_norm(nc, env, "ln3", "spaced")
            stage_wkv1(nc, env, inp)
        stage_norm(nc, env, "ln4", "halves")
        stage_ffn1(nc, env, inp)
        stage_norm(nc, env, "ln5", None, out=out)


def rope_rows(w, kv, rep):
    import numpy as np
    c = w.reshape(D, kv, rep, 2, DH0)
    partner = c[..., np.arange(DH0) ^ 1]
    tiles = []
    for j in range(rep):
        tiles += [c[:, :, j].reshape(D, P), partner[:, :, j].reshape(D, P)]
    return tiles


def head_rows(w):
    return w.reshape(KV0, REP0, 2 * DH0, -1).swapaxes(0, 1).reshape(w.shape)


def per_head(w):
    return w.reshape(2, D, -1, P).transpose(2, 1, 0, 3)


def kernel(**inputs):
    import numpy as np
    import concourse.bacc as bacc
    from concourse.bass_utils import run_bass_kernel_spmd
    a = {k: np.asarray(v) for k, v in inputs.items()}
    wq = rope_rows(a["L0_attn_Wq"], KV0, REP0)
    wk = rope_rows(a["L0_attn_Wk"], KV0, 1)
    inv = (1.0 / np.float32(10000.0) ** (np.arange(0, DH0, 2, dtype=np.float32) / np.float32(DH0))).astype(np.float32)
    freqs = (np.arange(T, dtype=np.float32)[:, None] * inv[None, :]).astype(np.float32)
    d = np.arange(P) % DH0
    sign = np.where(d % 2 == 0, -1.0, 1.0).astype(np.float32)
    rows = np.arange(P) // (2 * DH0)
    arrays = {
        "x": a["x"],
        "xT": a["x"].reshape(B * T, DT, P).transpose(1, 2, 0),
        "a0_w": np.concatenate(wk + wq + [a["L0_attn_Wv"]], axis=1).reshape(DT, P, -1),
        "a0_wo": head_rows(a["L0_attn_Wo"]),
        "cos": np.cos(freqs).T[d // 2],
        "sin": np.sin(freqs).T[d // 2] * sign[:, None],
        "row_mask": (np.arange(P)[:, None] // DH0 == np.arange(2 * KV0)).astype(np.float32) * np.float32(DH0 ** -0.5),
        "share": (rows[:, None] == rows[None, :]).astype(np.float32) / np.float32(2 * DH0),
        "lambdas": np.concatenate([a[f"L0_attn_lambda_{n}"] for n in ("q1", "k1", "q2", "k2")]),
        "gn_w": head_rows(a["L0_attn_gn_w"]).reshape(-1, P).T,
        "gn_b": head_rows(a["L0_attn_gn_b"]).reshape(-1, P).T,
        "ident": np.eye(P, dtype=np.float32),
        "anti": np.eye(P, dtype=np.float32)[::-1],
        "c0_ctx": a["ctx_2048"].reshape(B, T, DT, P)[..., ::-1].transpose(3, 2, 1, 0).reshape(P, -1),
        "c0_D": a["L0_xattn_D"],
        "m0_router": np.pad(a["L0_ffn_router_logits"], ((0, 0), (0, P - 8))),
        "m0_router_scale": a["L0_ffn_router_scale"].reshape(DT, P).T,
        "m0_rank": np.arange(8, 0, -1).astype(np.float32),
        "m0_per_expert": a["L0_ffn_per_expert_scale"],
        "a1_w": np.stack([per_head(np.stack([a[f"L1_attn_w{n}_codes"], a[f"L1_attn_w{n}_scales"].repeat(32, axis=0)]))
                          for n in "qkv"], axis=3).reshape(16, D, 2 * 3 * P),
        "a1_bias": np.stack([a[f"L1_attn_b{n}"].reshape(16, P) for n in "qkv"], axis=2),
        "a1_wo": np.stack([a["L1_attn_wo_codes"], a["L1_attn_wo_scales"].repeat(32, axis=0)], axis=1).reshape(16, P, 2 * D),
        "a1_bo": a["L1_attn_bo"],
        "m0_w": np.concatenate([a["L0_ffn_gating_einsum"].transpose(0, 3, 1, 2).reshape(8, D, 2 * D),
                                a["L0_ffn_linear"]], axis=2),
        "ctxT": a["ctx_2048"].reshape(B * T, DT, P).transpose(1, 2, 0),
        "k1_decay": a["L1_xattn_time_decay"].reshape(DT, P).T,
        "k1_first": a["L1_xattn_time_first"].reshape(DT, P).T,
        "f1_w": np.concatenate([a["L1_ffn_W_base"].T, a["L1_ffn_router_W"].T,
                                a["L1_ffn_A"].reshape(8 * 16, D).T], axis=1),
        "f1_b": a["L1_ffn_Bw"].transpose(0, 2, 1).reshape(8 * 16, D),
        "f1_bias": a["L1_ffn_b_base"],
        "toeplitz": np.pad(a["L0_xattn_ssm_kernel"], ((0, 0), (P - 1, 0)))[:, np.arange(P)[:, None] + np.arange(D)],
    }
    arrays = {k: np.ascontiguousarray(v) for k, v in arrays.items()}
    nc = bacc.Bacc("TRN2", target_bir_lowering=False, num_devices=1)
    inp = {k: nc.dram_tensor(f"in_{k}", v.shape, mybir.dt.from_np(v.dtype), kind="ExternalInput").ap() for k, v in arrays.items()}
    out = nc.dram_tensor("out", (B, T, D), F32, kind="ExternalOutput").ap()
    program(nc, inp, out)
    r = run_bass_kernel_spmd(nc, [{f"in_{k}": v for k, v in arrays.items()}], core_ids=[0])
    return r.results[0]["out"]
```

```python
import math
from contextlib import ExitStack

import concourse.bass as bass
from concourse import mybir
from concourse.alu_op_type import AluOpType as ALU

F32 = mybir.dt.float32
F32R = mybir.dt.float32r
BF16 = mybir.dt.bfloat16
ACT = mybir.ActivationFunctionType
AX_X = mybir.AxisListType.X

P = 128
B = 16
T = 128
D = 256
DT = D // P
G = 4
NG = B // G
GT = G * T
BANK = 512
LN_EPS = 1e-5

H0, KV0, DH0 = 16, 4, 16
REP0 = H0 // KV0
LAMBDA_INIT = 0.8 - 0.6 * math.exp(-0.3 * 0)


def one(ap_3d, i):
    return ap_3d[:, bass.ds(i, 1), :].rearrange("p o n -> p (o n)")


def batch(ap_4d, i, b):
    if isinstance(i, int):
        return ap_4d[:, 2 * i + b, :, :]
    return ap_4d[:, bass.ds(i * 2 + b, 1), :, :].rearrange("p o j t -> p (o j) t")


def flat_batch(ap_3d, i, b):
    return ap_3d[:, 2 * i + b, :] if isinstance(i, int) else one(ap_3d, i * 2 + b)


def hold(eng):
    eng.nop(nofuse=True)


class Mem:

    def __init__(self, nc, ctx):
        self.nc, self.ctx, self.sems = nc, ctx, []

    def recycle(self):
        self.nc.clear_and_free_semaphores(self.sems)
        self.nc.all_engine_barrier()

    def sb(self, name, shape, dt=F32):
        return self.ctx.enter_context(self.nc.sbuf_tensor(name, shape, dt))

    def ps(self, name, shape, dt=F32):
        return self.ctx.enter_context(self.nc.psum_tensor(name, shape, dt))

    def sem(self, name):
        if not self.sems:
            self.ctx.callback(self.recycle)
        self.sems.append(self.nc.alloc_semaphore(name=name))
        return self.sems[-1]


def stage_norm(nc, env, tag, turn=None, out=None):
    X, XTh, XTl, ident = env["X"], env["XTh"], env["XTl"], env["ident"]
    split = turn == "halves"
    with ExitStack() as ctx:
        m = Mem(nc, ctx)
        stats = m.sb(f"{tag}_stats", [P, B, 6])
        moments = m.sb(f"{tag}_moments", [P, B, 2])
        var_eps = m.sb(f"{tag}_var_eps", [P, B])
        rstd = m.sb(f"{tag}_rstd", [P, B])
        scaled = m.sb(f"{tag}_scaled", [P, B])
        shift = m.sb(f"{tag}_shift", [P, B])
        xT_ps = [m.ps(f"{tag}_xT_ps{i}", [P, DT, GT]) for i in range(2)]
        stats_done = m.sem(f"{tag}_stats_done")
        moments_done = m.sem(f"{tag}_moments_done")
        eps_done = m.sem(f"{tag}_eps_done")
        rstd_done = m.sem(f"{tag}_rstd_done")
        shift_done = m.sem(f"{tag}_shift_done")
        normed_dve = m.sem(f"{tag}_normed_dve")
        normed_act = m.sem(f"{tag}_normed_act")
        turned = m.sem(f"{tag}_turned")
        hi_done = m.sem(f"{tag}_hi_done")
        lo_done = m.sem(f"{tag}_lo_done")
        out_done = m.sem(f"{tag}_out_done")
        block = ctx.enter_context(nc.Block())
        half = G // 2

        @block.vector
        def _(dve):
            def normalise(g):
                dve.wait_ge(rstd_done, g + 1)
                for b in range(g * G, g * G + half):
                    last = nc.vector.tensor_scalar(X[:, b, :], X[:, b, :], moments[:, b, 0:1], rstd[:, b:b + 1],
                                                   ALU.subtract, ALU.mult)
                last.then_inc(normed_dve, 1)

            def low(g):
                for dt in range(DT):
                    cols = slice(g * GT, (g + 1) * GT)
                    dve.wait_ge(hi_done, g * DT + (dt + 1))
                    nc.vector.tensor_tensor(XTl[:, dt, cols], xT_ps[g % 2][:, dt, :],
                                            XTh[:, dt, cols].bitcast(F32), ALU.subtract).then_inc(lo_done, 1)

            for g in range(NG):
                for b in range(g * G, (g + 1) * G):
                    nc.vector.bn_stats(stats[:, b, :], X[:, b, :]).then_inc(stats_done, 1)
                for b in range(g * G, (g + 1) * G):
                    dve.wait_ge(stats_done, b + 1)
                    nc.vector.bn_aggr(moments[:, b, :], stats[:, b, :]).then_inc(moments_done, 1)
                if g >= 1:
                    normalise(g - 1)
                if g >= 2 and split:
                    low(g - 2)
            if split:
                low(NG - 2)
            normalise(NG - 1)
            if split:
                low(NG - 1)

        @block.gpsimd
        def _(pool):
            for g in range(NG):
                bs = slice(g * G, (g + 1) * G)
                pool.wait_ge(moments_done, g * G + G)
                nc.gpsimd.tensor_scalar(var_eps[:, bs], moments[:, bs, 1], 1.0, LN_EPS, ALU.mult, ALU.add).then_inc(eps_done, 1)
                pool.wait_ge(eps_done, 2 * g + 1)
                nc.gpsimd.tensor_tensor(rstd[:, bs], var_eps[:, bs], env["minus_half"][:, 0:G], ALU.pow).then_inc(rstd_done, 1)
                pool.wait_ge(rstd_done, g + 1)
                nc.gpsimd.tensor_tensor(scaled[:, bs], moments[:, bs, 0], rstd[:, bs], ALU.mult).then_inc(eps_done, 1)
                pool.wait_ge(eps_done, 2 * g + 2)
                nc.gpsimd.tensor_scalar(shift[:, bs], scaled[:, bs], -1.0, None, ALU.mult).then_inc(shift_done, 1)

        @block.scalar
        def _(act):
            for g in range(NG + 1):
                if g < NG:
                    act.wait_ge(shift_done, g + 1)
                    for b in range(g * G + half, (g + 1) * G):
                        last = nc.scalar.activation(X[:, b, :], X[:, b, :], ACT.Identity, scale=rstd[:, b:b + 1],
                                                    bias=shift[:, b:b + 1])
                    last.then_inc(normed_act, 1)
                if g >= 1 and turn is not None:
                    act.wait_ge(turned, g)
                    for dt in range(DT):
                        src = xT_ps[(g - 1) % 2][:, dt, :]
                        if turn == "spaced":
                            src = src.rearrange("p (b t) -> p b t", b=G)
                            dst = env["XTk"][:, dt, (g - 1) * G:g * G, 1:T + 1]
                        else:
                            dst = (XTh if split else env["XTf"])[:, dt, (g - 1) * GT:g * GT]
                        nc.scalar.activation(dst, src, ACT.Copy).then_inc(hi_done, 1)

        if turn is not None:
            @block.tensor
            def _(pe):
                for g in range(NG):
                    pe.wait_ge(normed_dve, g + 1)
                    pe.wait_ge(normed_act, g + 1)
                    if g >= 2:
                        pe.wait_ge(lo_done if split else hi_done, (g - 1) * DT)
                    for dt in range(DT):
                        for j in range(G):
                            last = nc.tensor.transpose(xT_ps[g % 2][:, dt, j * T:(j + 1) * T],
                                                       X[:, g * G + j, dt * P:(dt + 1) * P], ident[:, :])
                    last.then_inc(turned, 1)

        if out is not None:
            @block.sync
            def _(sp):
                for g in range(NG):
                    sp.wait_ge(normed_dve, g + 1)
                    sp.wait_ge(normed_act, g + 1)
                    sp.dma_start(out[g * G:(g + 1) * G, :, :].rearrange("b t d -> t b d"), X[:, g * G:(g + 1) * G, :])\
                        .then_inc(out_done, 16)
                sp.wait_ge(out_done, 16 * NG)


def halves(nc, out, lhs, rhs, tiles):
    terms = [(lhs[i], rhs[k], n) for n in range(tiles) for i, k in ((0, 0), (0, 1), (1, 0))]
    for at, (lh, rh, n) in enumerate(terms):
        last = nc.tensor.matmul(out, lh(n), rh(n), start=(at == 0), stop=(at == len(terms) - 1))
    return last


def stage_attn0_project(nc, env, inp):
    X, XTh, XTl, Q, K, V = (env[n] for n in ("X", "XTh", "XTl", "Q", "K", "V"))
    NT = REP0
    NPAIR = NT + 1
    first, rest = slice(0, GT), slice(GT, B * T)
    with ExitStack() as ctx:
        m = Mem(nc, ctx)
        x_raw = m.sb("p0_x_raw", [P, DT, B * T])
        w_raw = m.sb("p0_w_raw", [P, DT, NPAIR * 2 * P + P])
        w_hi = m.sb("p0_w_hi", [P, DT, NPAIR * 2 * P + P], F32R)
        w_lo = m.sb("p0_w_lo", [P, DT, NPAIR * 2 * P + P], F32R)
        cos = m.sb("p0_cos", [P, T])
        sin = m.sb("p0_sin", [P, T])
        lam_in = m.sb("p0_lam_in", [P, 4, DH0])
        lam_prod = m.sb("p0_lam_prod", [P, 2, DH0])
        lam_sum = m.sb("p0_lam_sum", [P, 2])
        lam_exp = m.sb("p0_lam_exp", [P, 2])
        lam_dif = m.sb("p0_lam_dif", [P, 1])
        r_cos = m.sb("p0_r_cos", [P, 3, GT])
        r_sin = m.sb("p0_r_sin", [P, 3, GT])
        vT = m.sb("p0_vT", [P, GT])
        proj_ps = [[m.ps(f"p0_proj_ps{i}{k}", [P, BANK]) for k in range(2)] for i in range(3)]
        vT_ps = m.ps("p0_vT_ps", [P, BANK])
        v_ps = m.ps("p0_v_ps", [P, BANK])
        w_in = [m.sem(f"p0_w_in{i}") for i in range(NPAIR)]
        x_in = [m.sem(f"p0_x_in{i}") for i in range(2)]
        const_in = m.sem("p0_const_in")
        X_in = m.sem("p0_X_in")
        ident_in = m.sem("p0_ident_in")
        whi_done = m.sem("p0_whi_done")
        wlo_done = m.sem("p0_wlo_done")
        xhi_done = m.sem("p0_xhi_done")
        xlo_done = m.sem("p0_xlo_done")
        lam = m.sem("p0_lam")
        lam_exped = m.sem("p0_lam_exped")
        const = m.sem("p0_const")
        projected = m.sem("p0_projected")
        v_projected = m.sem("p0_v_projected")
        vT_done = m.sem("p0_vT_done")
        v_turned = m.sem("p0_v_turned")
        v_done = m.sem("p0_v_done")
        roped = m.sem("p0_roped")
        added = m.sem("p0_added")
        block = ctx.enter_context(nc.Block())

        def columns(n):
            return slice(0, 3 * P) if n == 0 else slice((2 * n + 1) * P, (2 * n + 3) * P)

        @block.sync
        def _(sp):
            x_src = inp["xT"].rearrange("k p n -> p k n")
            w_src = inp["a0_w"].rearrange("k p n -> p k n")
            sp.dma_start(w_raw[:, :, columns(0)], w_src[:, :, columns(0)]).then_inc(w_in[0], 16)
            sp.dma_start(x_raw[:, :, first], x_src[:, :, first]).then_inc(x_in[0], 16)
            sp.dma_start(w_raw[:, :, columns(1)], w_src[:, :, columns(1)]).then_inc(w_in[1], 16)
            sp.dma_start(cos[:, :], inp["cos"]).then_inc(const_in, 16)
            sp.dma_start(sin[:, :], inp["sin"]).then_inc(const_in, 16)
            sp.dma_start(lam_in[:, :, :].rearrange("p a d -> p (a d)"),
                         inp["lambdas"].partition_broadcast(P)).then_inc(const_in, 16)
            sp.dma_start(env["ident"][:, :], inp["ident"]).then_inc(ident_in, 16)
            for n in range(2, NPAIR):
                sp.dma_start(w_raw[:, :, columns(n)], w_src[:, :, columns(n)]).then_inc(w_in[n], 16)
            sp.dma_start(x_raw[:, :, rest], x_src[:, :, rest]).then_inc(x_in[1], 16)
            sp.dma_start(env["row_mask"][:, :], inp["row_mask"]).then_inc(X_in, 16)
            sp.dma_start(X[:, :, :], inp["x"].rearrange("b t d -> t b d")).then_inc(X_in, 16)
            sp.wait_ge(X_in, 32)

        @block.gpsimd
        def _(pool):
            causal, ident_b = env["causal"], env["ident_b"]
            nc.gpsimd.memset(env["minus_half"][:, :], -0.5).then_inc(const, 1)
            nc.gpsimd.memset(env["ones"][:, :], 1.0).then_inc(const, 1)
            nc.gpsimd.memset(causal[:, :, :], 0.0).then_inc(const, 1)
            nc.gpsimd.memset(ident_b[:, :], 0.0).then_inc(const, 1)
            pool.wait_ge(const, 4)
            nc.gpsimd.affine_select(out=causal[:, :, :], in_=causal[:, :, :], compare_op=ALU.is_ge, fill=-1e38,
                                    base=0, pattern=[[0, 4], [-1, T]], channel_multiplier=1).then_inc(const, 1)
            nc.gpsimd.affine_select(out=ident_b[:, :], in_=ident_b[:, :], compare_op=ALU.not_equal, fill=1.0,
                                    base=0, pattern=[[-1, P]], channel_multiplier=1).then_inc(const, 1)
            pool.sem_inc(added, 2)
            with pool.Fori(0, NG) as g:
                for n in range(NPAIR):
                    pool.wait_ge(roped, g * NPAIR + (n + 1))
                    hold(pool)
                    if n == 0:
                        nc.gpsimd.tensor_tensor(K[:, bass.ds(g * GT, GT)], r_cos[:, n % 3, :], r_sin[:, n % 3, :], ALU.add)\
                            .then_inc(added, 1)
                    else:
                        nc.gpsimd.tensor_tensor(Q[:, bass.ds(g * G, G), n - 1, :],
                                                r_cos[:, n % 3, :].rearrange("p (b t) -> p b t", b=G),
                                                r_sin[:, n % 3, :].rearrange("p (b t) -> p b t", b=G), ALU.add)\
                            .then_inc(added, 1)

        @block.scalar
        def _(act):
            def w_high(n):
                act.wait_ge(w_in[n], 16)
                nc.scalar.activation(w_hi[:, :, columns(n)], w_raw[:, :, columns(n)], ACT.Copy).then_inc(whi_done, 1)

            def x_high(n, toks):
                act.wait_ge(x_in[n], 16)
                nc.scalar.activation(XTh[:, :, toks], x_raw[:, :, toks], ACT.Copy).then_inc(xhi_done, 1)

            w_high(0)
            x_high(0, first)
            for n in range(1, NPAIR):
                w_high(n)
            x_high(1, rest)
            with act.Fori(0, NG) as g:
                act.wait_ge(v_projected, g + 1)
                nc.scalar.activation(vT[:, :], vT_ps[:, :], ACT.Copy).then_inc(vT_done, 1)
                act.wait_ge(v_turned, g + 1)
                hold(act)
                nc.scalar.activation(V[:, bass.ds(g * G, G), :], v_ps[:, :].rearrange("p (b c) -> p b c", b=G), ACT.Copy)\
                    .then_inc(v_done, 1)
            act.wait_ge(lam, 2)
            nc.scalar.activation(lam_exp[:, :], lam_sum[:, :], ACT.Exp).then_inc(lam_exped, 1)

        @block.vector
        def _(dve):
            def w_low(n):
                dve.wait_ge(whi_done, n + 1)
                nc.vector.tensor_tensor(w_lo[:, :, columns(n)], w_raw[:, :, columns(n)],
                                        w_hi[:, :, columns(n)].bitcast(F32), ALU.subtract).then_inc(wlo_done, 1)

            def x_low(n, toks):
                dve.wait_ge(xhi_done, n + 1)
                nc.vector.tensor_tensor(XTl[:, :, toks], x_raw[:, :, toks], XTh[:, :, toks].bitcast(F32),
                                        ALU.subtract).then_inc(xlo_done, 1)

            def rotate(g, n):
                dve.wait_ge(projected, g * NPAIR + (n + 1))
                dve.wait_ge(added, g * NPAIR + (n + 1))
                v3 = "p (b t) -> p b t"
                for dst, src, table in ((r_cos, proj_ps[n % 3][0], cos), (r_sin, proj_ps[n % 3][1], sin)):
                    last = nc.vector.tensor_tensor(dst[:, n % 3, :].rearrange(v3, b=G), src[:, :].rearrange(v3, b=G),
                                                   table[:, :].unsqueeze(1).broadcast_to([P, G, T]), ALU.mult)
                last.then_inc(roped, 1)

            w_low(0)
            x_low(0, first)
            dve.wait_ge(const_in, 48)
            for n in range(NPAIR):
                if n + 1 < NPAIR:
                    w_low(n + 1)
                rotate(0, n)
            x_low(1, rest)
            sign = env["sign"]
            nc.vector.tensor_tensor(lam_prod[:, :, :], lam_in[:, 0:4:2, :], lam_in[:, 1:4:2, :], ALU.mult).then_inc(lam, 1)
            dve.wait_ge(lam, 1)
            nc.vector.tensor_reduce(lam_sum[:, :], lam_prod[:, :, :], AX_X, ALU.add).then_inc(lam, 1)
            with dve.Fori(1, NG) as g:
                for n in range(NPAIR):
                    rotate(g, n)
            dve.wait_ge(lam_exped, 1)
            nc.vector.memset(sign[:, :, 0:1], 1.0).then_inc(lam, 1)
            nc.vector.tensor_tensor(lam_dif[:, :], lam_exp[:, 1:2], lam_exp[:, 0:1], ALU.subtract).then_inc(lam, 1)
            dve.wait_ge(lam, 4)
            nc.vector.tensor_scalar(sign[:, :, 1], lam_dif[:, 0:1].broadcast_to([P, KV0]), 1.0, -LAMBDA_INIT,
                                    ALU.mult, ALU.add).then_inc(lam, 1)

        @block.tensor
        def _(pe):
            w_halves = [lambda c: lambda dt: w_hi[:, dt, c], lambda c: lambda dt: w_lo[:, dt, c]]

            def project(g):
                toks = first if isinstance(g, int) else bass.ds(g * GT, GT)
                x_halves = [lambda dt: XTh[:, dt, toks], lambda dt: XTl[:, dt, toks]]
                for n in range(NPAIR):
                    if isinstance(g, int):
                        pe.wait_ge(wlo_done, n + 1)
                    if n >= 2 or not isinstance(g, int):
                        pe.wait_ge(roped, g * NPAIR + (n - 1))
                    at = 0 if n == 0 else 2 * n + 1
                    for pr in range(2):
                        c = slice((at + pr) * P, (at + pr + 1) * P)
                        last = halves(nc, proj_ps[n % 3][pr][:, :], [w(c) for w in w_halves], x_halves, DT)
                    last.then_inc(projected, 1)
                    if n == 0:
                        c = slice(2 * P, 3 * P)
                        halves(nc, vT_ps[:, :], [w(c) for w in w_halves], x_halves, DT).then_inc(v_projected, 1)
                    if n == 1:
                        pe.wait_ge(vT_done, g + 1)
                        if isinstance(g, int):
                            pe.wait_ge(ident_in, 16)
                        else:
                            pe.wait_ge(v_done, g)
                        for b in range(G):
                            last = nc.tensor.transpose(v_ps[:, b * T:(b + 1) * T], vT[:, b * T:(b + 1) * T],
                                                       env["ident"][:, :])
                        last.then_inc(v_turned, 1)

            pe.wait_ge(xlo_done, 1)
            project(0)
            pe.wait_ge(xlo_done, 2)
            hold(pe)
            with pe.Fori(1, NG) as g:
                project(g)


def stage_attn0_heads(nc, env, inp):
    Q, K, V, OT, ident = env["Q"], env["K"], env["V"], env["OT"], env["ident"]
    causal, ident_b, sign, row_mask = env["causal"], env["ident_b"], env["sign"], env["row_mask"]
    N = B * REP0
    BODY = 2 * REP0
    FIRST = BODY + 2
    TURNS = (N - FIRST) // BODY
    R = 2 * KV0
    VW = 2 * DH0
    with ExitStack() as ctx:
        m = Mem(nc, ctx)
        q_hi = m.sb("a0_q_hi", [P, 2, REP0, T], F32R)
        q_lo = m.sb("a0_q_lo", [P, 2, REP0, T], F32R)
        k_hi = m.sb("a0_k_hi", [P, 2, T], F32R)
        k_lo = m.sb("a0_k_lo", [P, 2, T], F32R)
        kz_hi = m.sb("a0_kz_hi", [P, 2, R, T], F32R)
        kz_lo = m.sb("a0_kz_lo", [P, 2, R, T], F32R)
        v = m.sb("a0_v", [P, 2, P])
        negmax = m.sb("a0_negmax", [P, 2, R])
        sums = m.sb("a0_sums", [P, 2, R])
        recip = m.sb("a0_recip", [P, 2, R])
        factor = m.sb("a0_factor", [P, 2, KV0, 2])
        probs = m.sb("a0_probs", [P, 4, KV0, 2, T])
        second = m.sb("a0_second", [P, 2, KV0, T])
        diff = m.sb("a0_diff", [P, 2, KV0, T])
        diffT = m.sb("a0_diffT", [P, 2, KV0, REP0, T])
        s_ps = [m.ps(f"a0_s_ps{i}", [P, 2 * BANK]) for i in range(2)]
        dT_ps = [m.ps(f"a0_dT_ps{i}", [P, BANK]) for i in range(2)]
        oT_ps = m.ps("a0_oT_ps", [P, BANK])
        khi_done = m.sem("a0_khi_done")
        klo_done = m.sem("a0_klo_done")
        qhi_done = m.sem("a0_qhi_done")
        qlo_done = m.sem("a0_qlo_done")
        kz_done = m.sem("a0_kz_done")
        v_done = m.sem("a0_v_done")
        scored = m.sem("a0_scored")
        maxed = m.sem("a0_maxed")
        exped = m.sem("a0_exped")
        recip_done = m.sem("a0_recip_done")
        factor_done = m.sem("a0_factor_done")
        second_done = m.sem("a0_second_done")
        diff_done = m.sem("a0_diff_done")
        turned = m.sem("a0_turned")
        dT_done = m.sem("a0_dT_done")
        pv_done = m.sem("a0_pv_done")
        oT_done = m.sem("a0_oT_done")
        block = ctx.enter_context(nc.Block())

        def run(eng, step):
            for k in range(FIRST):
                step(0, k)
            with eng.Fori(0, TURNS) as i:
                for k in range(FIRST, FIRST + BODY):
                    step(i, k)
            for k in range(FIRST, N + 6 - TURNS * BODY):
                step(TURNS, k)

        def inside(i, k):
            return not isinstance(i, int) or 0 <= i * BODY + k < N

        def early(i, k, n):
            return isinstance(i, int) and i * BODY + k < n

        @block.gpsimd
        def _(pool):
            def mask_keys(i, k, half):
                src, dst, ready = ((k_hi, kz_hi, khi_done), (k_lo, kz_lo, klo_done))[half]
                p = (k // REP0 + 1) % 2
                pool.wait_ge(ready, i * 2 + (k // REP0 + 2))
                if not early(i, k, REP0):
                    pool.wait_ge(scored, i * BODY + k // REP0 * REP0)
                nc.gpsimd.tensor_tensor(dst[:, p, :, :], src[:, p, :].bitcast(F32).unsqueeze(1).broadcast_to([P, R, T]),
                                        row_mask[:, :].unsqueeze(2).broadcast_to([P, R, T]), ALU.mult).then_inc(kz_done, 1)

            def step(i, k):
                if inside(i, k - 1):
                    pool.wait_ge(factor_done, i * BODY + k)
                    nc.gpsimd.tensor_tensor(second[:, (k - 1) % 2, :, :], probs[:, (k - 1) % 4, :, 1, :],
                                            factor[:, (k - 1) % 2, :, 1:2].broadcast_to([P, KV0, T]), ALU.mult)\
                        .then_inc(second_done, 1)
                if k % REP0 < 2 and inside(i, k // REP0 * REP0 + REP0):
                    mask_keys(i, k, k % REP0)

            mask_keys(0, -REP0, 0)
            mask_keys(0, -REP0, 1)
            run(pool, step)

        @block.scalar
        def _(act):
            def high_halves(i, k):
                b, p = k // REP0 + 1, (k // REP0 + 1) % 2
                if not early(i, k, REP0):
                    act.wait_ge(scored, i * BODY + k)
                hold(act)
                toks = bass.ds(i * (2 * T) + b * T, T) if not isinstance(i, int) else slice((2 * i + b) * T, (2 * i + b + 1) * T)
                nc.scalar.activation(k_hi[:, p, :], K[:, toks], ACT.Copy).then_inc(khi_done, 1)
                nc.scalar.activation(q_hi[:, p, :, :], batch(Q, i, b), ACT.Copy).then_inc(qhi_done, 1)

            def step(i, k):
                if k % REP0 == 0 and inside(i, k + REP0):
                    high_halves(i, k)
                if inside(i, k):
                    act.wait_ge(maxed, i * BODY + (k + 1))
                    for r in range(R):
                        nc.scalar.activation(probs[:, k % 4, r // 2, r % 2, :], s_ps[k % 2][:, r * T:(r + 1) * T],
                                             ACT.Exp, bias=negmax[:, k % 2, r:r + 1],
                                             accum_out=sums[:, k % 2, r:r + 1]).then_inc(exped, 1)
                if inside(i, k - 3):
                    u = k - 3
                    act.wait_ge(turned, i * BODY + (u + 1))
                    nc.scalar.activation(diffT[:, u // REP0 % 2, :, u % REP0, :],
                                         dT_ps[u % 2][:, :].rearrange("p (k t) -> p k t", k=KV0), ACT.Copy)\
                        .then_inc(dT_done, 1)
                if k % REP0 == 0 and inside(i, k - REP0):
                    b = k // REP0 - 1
                    if not early(i, k, 3 * REP0):
                        act.wait_ge(pv_done, i * 2 + (b - 1))
                        hold(act)
                    nc.scalar.activation(v[:, b % 2, :], flat_batch(V, i, b), ACT.Copy).then_inc(v_done, 1)
                if k % REP0 == 1 and inside(i, k - 9):
                    b = (k - 9) // REP0
                    act.wait_ge(pv_done, i * 2 + (b + 1))
                    hold(act)
                    nc.scalar.activation(flat_batch(OT, i, b), oT_ps[:, :], ACT.Copy).then_inc(oT_done, 1)

            high_halves(0, -REP0)
            run(act, step)

        @block.vector
        def _(dve):
            def low_halves(i, k):
                b, p = k // REP0 + 1, (k // REP0 + 1) % 2
                toks = bass.ds(i * (2 * T) + b * T, T) if not isinstance(i, int) else slice((2 * i + b) * T, (2 * i + b + 1) * T)
                dve.wait_ge(khi_done, i * 2 + (b + 1))
                hold(dve)
                nc.vector.tensor_tensor(k_lo[:, p, :], K[:, toks], k_hi[:, p, :].bitcast(F32), ALU.subtract)\
                    .then_inc(klo_done, 1)
                dve.wait_ge(qhi_done, i * 2 + (b + 1))
                hold(dve)
                nc.vector.tensor_tensor(q_lo[:, p, :, :], batch(Q, i, b), q_hi[:, p, :, :].bitcast(F32), ALU.subtract)\
                    .then_inc(qlo_done, 1)

            def step(i, k):
                if inside(i, k):
                    dve.wait_ge(scored, i * BODY + (k + 1))
                    nc.vector.tensor_reduce(negmax[:, k % 2, :], s_ps[k % 2][:, :].rearrange("p (r s) -> p r s", r=R),
                                            AX_X, ALU.max, negate=True).then_inc(maxed, 1)
                if k % REP0 == 0 and inside(i, k + REP0):
                    low_halves(i, k)
                if inside(i, k - 1):
                    p = (k - 1) % 2
                    dve.wait_ge(exped, i * (R * BODY) + R * k)
                    nc.vector.reciprocal(recip[:, p, :], sums[:, p, :]).then_inc(recip_done, 1)
                    dve.wait_ge(recip_done, i * BODY + k)
                    nc.vector.tensor_tensor(factor[:, p, :, :].rearrange("p k h -> p (k h)"), recip[:, p, :],
                                            sign[:, :, :].rearrange("p k h -> p (k h)"), ALU.mult).then_inc(factor_done, 1)
                if inside(i, k - 2):
                    u = k - 2
                    dve.wait_ge(second_done, i * BODY + (u + 1))
                    if not early(i, u, 2):
                        dve.wait_ge(turned, i * BODY + (u - 1))
                    for kv in range(KV0):
                        last = nc.vector.scalar_tensor_tensor(diff[:, u % 2, kv, :], probs[:, u % 4, kv, 0, :],
                                                              factor[:, u % 2, kv, 0:1], second[:, u % 2, kv, :],
                                                              ALU.mult, ALU.add)
                    last.then_inc(diff_done, 1)

            low_halves(0, -REP0)
            run(dve, step)

        @block.tensor
        def _(pe):
            def step(i, k):
                if inside(i, k):
                    p, j = k // REP0 % 2, k % REP0
                    if j == 0:
                        pe.wait_ge(kz_done, i * 4 + (2 * (k // REP0) + 2))
                        pe.wait_ge(qlo_done, i * 2 + (k // REP0 + 1))
                    if not early(i, k, 2):
                        pe.wait_ge(exped, i * (R * BODY) + R * (k - 1))
                    for h in range(2):
                        bank = s_ps[k % 2][:, h * BANK:(h + 1) * BANK]
                        nc.tensor.matmul(bank, ident_b[:, :], causal[:, :, :].rearrange("p a s -> p (a s)"),
                                         start=True, stop=False)
                        for q, kz in ((q_hi, kz_hi), (q_hi, kz_lo), (q_lo, kz_hi)):
                            last = nc.tensor.matmul(bank, q[:, p, j, :],
                                                    kz[:, p, 4 * h:4 * h + 4, :].rearrange("p r s -> p (r s)"),
                                                    start=False, stop=q is q_lo)
                    last.then_inc(scored, 1)
                if inside(i, k - 3):
                    u = k - 3
                    if not early(i, u, 2):
                        pe.wait_ge(dT_done, i * BODY + (u - 1))
                    pe.wait_ge(diff_done, i * BODY + (u + 1))
                    for kv in range(KV0):
                        last = nc.tensor.transpose(dT_ps[u % 2][:, kv * T:(kv + 1) * T], diff[:, u % 2, kv, :], ident[:, :])
                    last.then_inc(turned, 1)
                if k % REP0 == 0 and inside(i, k - 2 * REP0):
                    b = k // REP0 - 2
                    pe.wait_ge(dT_done, i * BODY + (REP0 * b + REP0))
                    pe.wait_ge(v_done, i * 2 + (b + 1))
                    if not early(i, b * REP0, REP0):
                        pe.wait_ge(oT_done, i * 2 + b)
                    for kv in range(KV0):
                        last = nc.tensor.matmul(oT_ps[kv * VW:(kv + 1) * VW, :], v[:, b % 2, kv * VW:(kv + 1) * VW],
                                                diffT[:, b % 2, kv, :, :].rearrange("p j t -> p (j t)"),
                                                start=True, stop=True)
                    last.then_inc(pv_done, 1)

            run(pe, step)


def stage_attn0_out(nc, env, inp):
    X, OT = env["X"], env["OT"]
    NJ = REP0
    N = B // 2
    BODY, FIRST = 2, 2
    TURNS = (N - FIRST - 1) // BODY
    with ExitStack() as ctx:
        m = Mem(nc, ctx)
        wo_raw = m.sb("n0_wo_raw", [P, NJ, D])
        wo_b = m.sb("n0_wo_b", [P, NJ, D])
        wo = m.sb("n0_wo", [P, NJ, D])
        gn_w = m.sb("n0_gn_w", [P, NJ])
        gn_b = m.sb("n0_gn_b", [P, NJ])
        bias = m.sb("n0_bias", [P, D])
        share = m.sb("n0_share", [P, P])
        stats = m.sb("n0_stats", [P, 2, 2, NJ, 6])
        moments = m.sb("n0_moments", [P, 2, 2, NJ, 2])
        square = m.sb("n0_square", [P, 2, 2, NJ])
        avg = m.sb("n0_avg", [P, 2, 2, NJ, 2])
        avg2 = m.sb("n0_avg2", [P, 2, 2, NJ])
        var = m.sb("n0_var", [P, 2, 2, NJ])
        rstd = m.sb("n0_rstd", [P, 2, 2, NJ])
        yT = m.sb("n0_yT", [P, 2, 2, NJ, T])
        avg_ps = [m.ps(f"n0_avg_ps{i}", [P, BANK]) for i in range(2)]
        out_ps = [m.ps(f"n0_out_ps{i}", [P, BANK]) for i in range(2)]
        bias_ps = m.ps("n0_bias_ps", [P, BANK])
        w_in = m.sem("n0_w_in")
        wb_done = m.sem("n0_wb_done")
        wo_done = m.sem("n0_wo_done")
        bias_ready = m.sem("n0_bias_ready")
        bias_done = m.sem("n0_bias_done")
        bias_added = m.sem("n0_bias_added")
        stats_done = m.sem("n0_stats_done")
        moments_done = m.sem("n0_moments_done")
        squared = m.sem("n0_squared")
        power_done = m.sem("n0_power_done")
        averaged = m.sem("n0_averaged")
        avg_done = m.sem("n0_avg_done")
        avg2_done = m.sem("n0_avg2_done")
        var_done = m.sem("n0_var_done")
        rstd_done = m.sem("n0_rstd_done")
        y_done = m.sem("n0_y_done")
        multiplied = m.sem("n0_multiplied")
        added = m.sem("n0_added")
        block = ctx.enter_context(nc.Block())

        def run(eng, step):
            for k in range(FIRST):
                step(0, k)
            with eng.Fori(0, TURNS) as i:
                for k in range(FIRST, FIRST + BODY):
                    step(i, k)
            for k in range(FIRST, N + 1 - TURNS * BODY):
                step(TURNS, k)

        def inside(i, k):
            return not isinstance(i, int) or 0 <= i * BODY + k < N

        def tokens(ap_3d, i, b):
            return ap_3d[:, 2 * BODY * i + b, :] if isinstance(i, int) else one(ap_3d, i * (2 * BODY) + b)

        def early(i, k):
            return isinstance(i, int) and i * BODY + k < 2

        @block.sync
        def _(sp):
            sp.dma_start(wo_raw[:, :, :], inp["a0_wo"].rearrange("(k p) n -> p k n", p=P)).then_inc(w_in, 16)
            sp.dma_start(gn_w[:, :], inp["gn_w"]).then_inc(w_in, 16)
            sp.dma_start(gn_b[:, :], inp["gn_b"]).then_inc(w_in, 16)
            sp.dma_start(share[:, :], inp["share"]).then_inc(w_in, 16)

        @block.gpsimd
        def _(pool):
            pool.wait_ge(w_in, 64)
            for k in range(NJ):
                nc.gpsimd.tensor_scalar(wo_b[:, k, :], wo_raw[:, k, :], gn_b[:, k:k + 1], 1.0 - LAMBDA_INIT,
                                        ALU.mult, ALU.mult).then_inc(wb_done, 1)
                nc.gpsimd.tensor_scalar(wo[:, k, :], wo_raw[:, k, :], gn_w[:, k:k + 1], 1.0 - LAMBDA_INIT,
                                        ALU.mult, ALU.mult).then_inc(wo_done, 1)
            pool.wait_ge(bias_done, 1)
            nc.gpsimd.tensor_tensor(X[:, :, :], X[:, :, :], bias[:, :].unsqueeze(1).broadcast_to([P, B, D]), ALU.add)\
                .then_inc(bias_added, 1)

            def step(i, k):
                if inside(i, k):
                    pool.wait_ge(var_done, i * BODY + (k + 1))
                    nc.gpsimd.tensor_tensor(rstd[:, k % 2, :, :], var[:, k % 2, :, :],
                                            env["minus_half"][:, 0:2 * NJ].rearrange("p (b j) -> p b j", b=2), ALU.pow)\
                        .then_inc(rstd_done, 1)

            run(pool, step)

        @block.vector
        def _(dve):
            def statistics(i, k):
                p = k % 2
                if not isinstance(i, int):
                    hold(dve)
                for r in range(2):
                    for j in range(NJ):
                        last = nc.vector.bn_stats(stats[:, p, r, j, :], tokens(OT, i, 2 * k + r)[:, j * T:(j + 1) * T])
                last.then_inc(stats_done, 1)
                dve.wait_ge(stats_done, i * BODY + (k + 1))
                hold(dve)
                for r in range(2):
                    for j in range(NJ):
                        last = nc.vector.bn_aggr(moments[:, p, r, j, :], stats[:, p, r, j, :])
                last.then_inc(moments_done, 1)
                mean, power = moments[:, p, :, :, 0], moments[:, p, :, :, 1]
                dve.wait_ge(moments_done, i * BODY + (k + 1))
                nc.vector.tensor_tensor(square[:, p, :, :], mean, mean, ALU.mult).then_inc(squared, 1)
                dve.wait_ge(squared, i * BODY + (k + 1))
                nc.vector.tensor_tensor(power, power, square[:, p, :, :], ALU.add).then_inc(power_done, 1)

            def step(i, k):
                p = k % 2
                if inside(i, k):
                    dve.wait_ge(averaged, i * BODY + (k + 1))
                    if not early(i, k):
                        dve.wait_ge(y_done, i * BODY + (k - 1))
                    nc.vector.tensor_copy(avg[:, p, :, :, :].rearrange("p b j a -> p (b j a)"), avg_ps[p][:, 0:4 * NJ])\
                        .then_inc(avg_done, 1)
                    dve.wait_ge(avg_done, i * BODY + (k + 1))
                    nc.vector.tensor_tensor(avg2[:, p, :, :], avg[:, p, :, :, 0], avg[:, p, :, :, 0], ALU.mult)\
                        .then_inc(avg2_done, 1)
                    dve.wait_ge(avg2_done, i * BODY + (k + 1))
                    nc.vector.scalar_tensor_tensor(var[:, p, :, :], avg[:, p, :, :, 1], LN_EPS, avg2[:, p, :, :],
                                                   ALU.add, ALU.subtract).then_inc(var_done, 1)
                if inside(i, k + 1):
                    statistics(i, k + 1)
                if inside(i, k):
                    dve.wait_ge(rstd_done, i * BODY + (k + 1))
                    if not early(i, k):
                        dve.wait_ge(multiplied, i * BODY + (k - 1))
                    hold(dve)
                    for r in range(2):
                        for j in range(NJ):
                            last = nc.vector.tensor_scalar(yT[:, p, r, j, :], tokens(OT, i, 2 * k + r)[:, j * T:(j + 1) * T],
                                                           avg[:, p, r, j, 0:1], rstd[:, p, r, j:j + 1],
                                                           ALU.subtract, ALU.mult)
                    last.then_inc(y_done, 1)
                if inside(i, k - 1):
                    dve.wait_ge(multiplied, i * BODY + k)
                    hold(dve)
                    bs = slice(2 * (i * BODY + k - 1), 2 * (i * BODY + k)) if isinstance(i, int) else \
                        bass.ds(i * (2 * BODY) + (2 * k - 2), 2)
                    nc.vector.tensor_tensor(X[:, bs, :], X[:, bs, :],
                                            out_ps[(k - 1) % 2][:, :].rearrange("p (b d) -> p b d", b=2), ALU.add)\
                        .then_inc(added, 1)

            dve.wait_ge(bias_ready, 1)
            nc.vector.tensor_copy(bias[:, :], bias_ps[:, 0:D]).then_inc(bias_done, 1)
            statistics(0, 0)
            dve.wait_ge(bias_added, 1)
            run(dve, step)

        @block.tensor
        def _(pe):
            pe.wait_ge(wb_done, NJ)
            for k in range(NJ):
                last = nc.tensor.matmul(bias_ps[:, 0:D], env["ones"][:, :], wo_b[:, k, :], start=(k == 0), stop=(k == NJ - 1))
            last.then_inc(bias_ready, 1)
            pe.wait_ge(wo_done, NJ)

            def average(i, k):
                pe.wait_ge(power_done, i * BODY + (k + 1))
                nc.tensor.matmul(avg_ps[k % 2][:, 0:4 * NJ], share[:, :],
                                 moments[:, k % 2, :, :, :].rearrange("p b j a -> p (b j a)"), start=True, stop=True)\
                    .then_inc(averaged, 1)

            def step(i, k):
                if inside(i, k + 1):
                    average(i, k + 1)
                if inside(i, k):
                    pe.wait_ge(y_done, i * BODY + (k + 1))
                    if not early(i, k):
                        pe.wait_ge(added, i * BODY + (k - 1))
                    for r in range(2):
                        for j in range(NJ):
                            last = nc.tensor.matmul(out_ps[k % 2][:, r * D:(r + 1) * D], yT[:, k % 2, r, j, :], wo[:, j, :],
                                                    start=(j == 0), stop=(j == NJ - 1))
                    last.then_inc(multiplied, 1)

            average(0, 0)
            run(pe, step)


def stage_conv0(nc, env, inp):
    XTf, Z, C = env["XTf"], env["Z"], env["C"]
    HD = 8
    H = T // HD
    LB = D // P
    with ExitStack() as ctx:
        m = Mem(nc, ctx)
        toep = [m.sb(f"c0_toep{i}", [P, LB * P]) for i in range(2)]
        toep_d = [m.sb(f"c0_toep_d{i}", [P, P]) for i in range(2)]
        d_all = m.sb("c0_d_all", [P, H])
        anti = m.sb("c0_anti", [P, P])
        d_diag = m.sb("c0_d_diag", [P, H, P])
        pairs = m.sb("c0_pairs", [P, 2, LB, HD, HD, B])
        weighted = m.sb("c0_weighted", [P, 2, HD, HD, B])
        y_ps = [[m.ps(f"c0_y_ps{r}{lb}", [P, 2 * BANK]) for lb in range(LB)] for r in range(2)]
        d_in = m.sem("c0_d_in")
        toep_in = [m.sem(f"c0_toep_in{r}") for r in range(2)]
        diag_done = m.sem("c0_diag_done")
        toep_done = m.sem("c0_toep_done")
        paired = m.sem("c0_paired")
        convolved = m.sem("c0_convolved")
        weighted_done = m.sem("c0_weighted_done")
        summed = m.sem("c0_summed")
        block = ctx.enter_context(nc.Block())

        @block.sync
        def _(sp):
            sp.dma_start(d_all[:, :], inp["c0_D"].partition_broadcast(P)).then_inc(d_in, 16)
            sp.dma_start(anti[:, :], inp["anti"]).then_inc(d_in, 16)
            sp.sem_inc(convolved, 4)
            with sp.Fori(0, H // 2) as i:
                for r in range(2):
                    sp.wait_ge(convolved, i * 4 + (2 * r + 2))
                    hold(sp)
                    sp.dma_start(toep[r][:, :], inp["toeplitz"][bass.ds(i * 2 + r, 1), :, :]
                                 .rearrange("o p l -> p (o l)")).then_inc(toep_in[r], 16)

        @block.gpsimd
        def _(pool):
            pool.wait_ge(d_in, 32)
            nc.gpsimd.tensor_tensor(d_diag[:, :, :], anti[:, :].unsqueeze(1).broadcast_to([P, H, P]),
                                    d_all[:, :].unsqueeze(2).broadcast_to([P, H, P]), ALU.mult).then_inc(diag_done, 1)
            with pool.Fori(0, H // 2) as i:
                for r in range(2):
                    pool.wait_ge(convolved, i * 4 + (2 * r + 2))
                    for mb in range(LB):
                        hold(pool)
                        c = C[:, mb, bass.ds((i * 2 + r) * HD, HD), :]
                        nc.gpsimd.tensor_tensor(pairs[:, r, mb, :, :, :],
                                                c.unsqueeze(2).broadcast_to([P, HD, HD, B]),
                                                c.unsqueeze(1).broadcast_to([P, HD, HD, B]), ALU.mult).then_inc(paired, 1)

        @block.vector
        def _(dve):
            dve.sem_inc(weighted_done, 4)
            dve.wait_ge(diag_done, 1)
            hold(dve)

            def diagonal(i, r):
                dve.wait_ge(toep_in[r], i * 16 + 16)
                dve.wait_ge(convolved, i * 4 + (2 * r + 2))
                nc.vector.tensor_tensor(toep_d[r][:, :], toep[r][:, 0:P], one(d_diag, i * 2 + r), ALU.add)\
                    .then_inc(toep_done, 1)

            with dve.Fori(0, H // 2) as i:
                for r in range(2):
                    diagonal(i, r)
                for r in range(2):
                    for lb in range(LB):
                        n = 2 * r + lb
                        dve.wait_ge(convolved, i * 4 + (n + 5))
                        h = i * 2 + r
                        q = XTf[:, lb, :].rearrange("p (b t) -> p t b", b=B)[:, bass.ds(h * HD, HD), :]
                        nc.vector.tensor_tensor(weighted[:, lb, :, :, :],
                                                y_ps[r][lb][:, :].rearrange("p (i j b) -> p i j b", i=HD, j=HD),
                                                q.unsqueeze(2).broadcast_to([P, HD, HD, B]), ALU.mult)\
                            .then_inc(weighted_done, 1)
                        dve.wait_ge(weighted_done, i * 4 + (n + 5))
                        nc.vector.tensor_reduce(Z[:, lb, :, :].rearrange("p b t -> p t b")[:, bass.ds(h * HD, HD), :],
                                                weighted[:, lb, :, :, :].rearrange("p i j b -> p j b i"),
                                                AX_X, ALU.add).then_inc(summed, 1)

        @block.tensor
        def _(pe):
            with pe.Fori(0, H // 2) as i:
                for r in range(2):
                    halves2 = [slice(0, HD // 2), slice(HD // 2, HD)]

                    def product(lb, mb, weights, start, stop):
                        for k, half in enumerate(halves2):
                            last = nc.tensor.matmul(y_ps[r][lb][:, k * BANK:(k + 1) * BANK], weights,
                                                    pairs[:, r, mb, half, :, :].rearrange("p i j b -> p (i j b)"),
                                                    start=start, stop=stop)
                        return last

                    pe.wait_ge(weighted_done, i * 4 + (2 * r + 2))
                    pe.wait_ge(toep_done, i * 2 + (r + 1))
                    pe.wait_ge(paired, i * 4 + (2 * r + 1))
                    product(0, 0, toep_d[r][:, :], True, True).then_inc(convolved, 1)
                    product(1, 0, toep[r][:, P:2 * P], True, False)
                    pe.wait_ge(paired, i * 4 + (2 * r + 2))
                    product(1, 1, toep_d[r][:, :], False, True).then_inc(convolved, 1)


def stage_conv0_out(nc, env):
    X, Z = env["X"], env["Z"]
    with ExitStack() as ctx:
        m = Mem(nc, ctx)
        z = m.sb("z0_z", [P, 2, D // P, T])
        z_ps = [m.ps(f"z0_z_ps{i}", [P, BANK]) for i in range(2)]
        copied = m.sem("z0_copied")
        turned = m.sem("z0_turned")
        added = m.sem("z0_added")
        block = ctx.enter_context(nc.Block())

        @block.scalar
        def _(act):
            with act.Fori(0, B // 2) as i:
                for r in range(2):
                    act.wait_ge(turned, i * 2 + (r + 1))
                    hold(act)
                    nc.scalar.activation(z[:, r, :, :], Z[:, :, bass.ds(i * 2 + r, 1), :].rearrange("p l o t -> p l (o t)"),
                                         ACT.Copy).then_inc(copied, 1)

        @block.tensor
        def _(pe):
            pe.sem_inc(turned, 2)
            with pe.Fori(0, B // 2) as i:
                for r in range(2):
                    pe.wait_ge(copied, i * 2 + (r + 1))
                    pe.wait_ge(added, i * 2 + (r + 1))
                    for lb in range(D // P):
                        last = nc.tensor.transpose(z_ps[r][:, lb * P:(lb + 1) * P], z[:, r, lb, :], env["ident"][:, :])
                    last.then_inc(turned, 1)

        @block.vector
        def _(dve):
            dve.sem_inc(added, 2)
            with dve.Fori(0, B // 2) as i:
                for r in range(2):
                    dve.wait_ge(turned, i * 2 + (r + 3))
                    hold(dve)
                    nc.vector.tensor_tensor(one(X, i * 2 + r), one(X, i * 2 + r), z_ps[r][:, 0:D], ALU.add)\
                        .then_inc(added, 1)


def stage_moe0(nc, env, inp):
    X, XTh, XTl, ident = env["X"], env["XTh"], env["XTl"], env["ident"]
    E = 8
    HT = D // P
    WG = 2 * D
    WE = WG + D
    NU = E * HT
    with ExitStack() as ctx:
        m = Mem(nc, ctx)
        w_raw = m.sb("m0_w_raw", [P, 2, DT, WE])
        w_hi = m.sb("m0_w_hi", [P, E, DT, WE], F32R)
        w_lo = m.sb("m0_w_lo", [P, E, DT, WE], F32R)
        r_raw = m.sb("m0_r_raw", [P, DT, P])
        r_scale = m.sb("m0_r_scale", [P, DT])
        r_scaled = m.sb("m0_r_scaled", [P, DT, P])
        r_hi = m.sb("m0_r_hi", [P, DT, P], F32R)
        r_lo = m.sb("m0_r_lo", [P, DT, P], F32R)
        rank = m.sb("m0_rank", [P, E])
        per_expert = m.sb("m0_per_expert", [P, E])
        square = m.sb("m0_square", [P, D])
        power = m.sb("m0_power", [P, B])
        power_eps = m.sb("m0_power_eps", [P, B])
        x_rstd = m.sb("m0_x_rstd", [P, B])
        lgT = m.sb("m0_lgT", [P, GT])
        small = {n: m.sb(f"m0_{n}", [P, B, E]) for n in
                 ("logit", "tie", "order", "first", "rest", "tie2", "order2", "second", "chosen", "less", "exp",
                  "picked", "share", "weight")}
        top = {n: m.sb(f"m0_{n}", [P, B]) for n in ("max1", "rank1", "max2", "rank2", "total", "inverse")}
        w_grp = m.sb("m0_w_grp", [P, G, E])
        act_g = m.sb("m0_act_g", [P, 2, GT])
        hid = m.sb("m0_hid", [P, 2, GT])
        hid_hi = m.sb("m0_hid_hi", [P, 2, HT, GT], F32R)
        hid_lo = m.sb("m0_hid_lo", [P, 2, HT, GT], F32R)
        acc = m.sb("m0_acc", [P, G, D])
        gate_ps = [m.ps(f"m0_gate_ps{i}", [P, BANK]) for i in range(2)]
        up_ps = [m.ps(f"m0_up_ps{i}", [P, BANK]) for i in range(2)]
        out_ps = [[m.ps(f"m0_out_ps{i}{k}", [P, BANK]) for k in range(2)] for i in range(2)]
        w_in = [m.sem(f"m0_w_in{i}") for i in range(2)]
        r_in = m.sem("m0_r_in")
        whi_done = m.sem("m0_whi_done")
        wlo_done = m.sem("m0_wlo_done")
        power_done = m.sem("m0_power_done")
        eps_done = m.sem("m0_eps_done")
        x_rstd_done = m.sem("m0_x_rstd_done")
        r_scaled_done = m.sem("m0_r_scaled_done")
        rhi_done = m.sem("m0_rhi_done")
        rlo_done = m.sem("m0_rlo_done")
        lgT_ready = m.sem("m0_lgT_ready")
        lgT_done = m.sem("m0_lgT_done")
        lg_ready = m.sem("m0_lg_ready")
        logit_done = m.sem("m0_logit_done")
        routed = m.sem("m0_routed")
        exp_done = m.sem("m0_exp_done")
        grp_done = m.sem("m0_grp_done")
        gated = m.sem("m0_gated")
        gelu_done = m.sem("m0_gelu_done")
        hid_done = m.sem("m0_hid_done")
        hid_hi_done = m.sem("m0_hid_hi_done")
        hid_lo_done = m.sem("m0_hid_lo_done")
        down_done = m.sem("m0_down_done")
        acc_done = m.sem("m0_acc_done")
        block = ctx.enter_context(nc.Block())

        @block.sync
        def _(sp):
            sp.dma_start(r_raw[:, :, :], inp["m0_router"].rearrange("(k p) e -> p k e", p=P)).then_inc(r_in, 16)
            sp.dma_start(r_scale[:, :], inp["m0_router_scale"]).then_inc(r_in, 16)
            sp.dma_start(rank[:, :], inp["m0_rank"].partition_broadcast(P)).then_inc(r_in, 16)
            sp.dma_start(per_expert[:, :], inp["m0_per_expert"].partition_broadcast(P)).then_inc(r_in, 16)
            for e in range(E):
                if e >= 2:
                    sp.wait_ge(wlo_done, e - 1)
                sp.dma_start(w_raw[:, e % 2, :, :], inp["m0_w"][e].rearrange("(k p) n -> p k n", p=P))\
                    .then_inc(w_in[e % 2], 16)

        @block.gpsimd
        def _(pool):
            pool.wait_ge(power_done, B)
            nc.gpsimd.tensor_scalar(power_eps[:, :], power[:, :], 1.0 / D, 1e-6, ALU.mult, ALU.add).then_inc(eps_done, 1)
            pool.wait_ge(eps_done, 1)
            nc.gpsimd.tensor_tensor(x_rstd[:, :], power_eps[:, :], env["minus_half"][:, 0:B], ALU.pow)\
                .then_inc(x_rstd_done, 1)
            for e in range(E):
                pool.wait_ge(whi_done, e + 1)
                nc.gpsimd.tensor_tensor(w_lo[:, e, :, :], w_raw[:, e % 2, :, :], w_hi[:, e, :, :].bitcast(F32),
                                        ALU.subtract).then_inc(wlo_done, 1)
            with pool.Fori(0, NG) as g:
                for u in range(NU):
                    pool.wait_ge(hid_hi_done, g * NU + (u + 1))
                    nc.gpsimd.tensor_tensor(hid_lo[:, u // HT % 2, u % HT, :], hid[:, u % 2, :],
                                            hid_hi[:, u // HT % 2, u % HT, :].bitcast(F32), ALU.subtract)\
                        .then_inc(hid_lo_done, 1)

        def high(act, g, u):
            act.wait_ge(hid_done, g * NU + (u + 3))
            nc.scalar.activation(hid_hi[:, u // HT % 2, u % HT, :], hid[:, u % 2, :], ACT.Copy).then_inc(hid_hi_done, 1)

        @block.scalar
        def _(act):
            for b in range(B):
                if b:
                    act.wait_ge(power_done, b)
                nc.scalar.activation(square[:, :], X[:, b, :], ACT.Square, accum_out=power[:, b:b + 1])\
                    .then_inc(power_done, 1)
            act.wait_ge(r_scaled_done, DT)
            nc.scalar.activation(r_hi[:, :, :], r_scaled[:, :, :], ACT.Copy).then_inc(rhi_done, 1)
            for g in range(NG):
                act.wait_ge(lgT_ready, g + 1)
                nc.scalar.activation(lgT[:, :], gate_ps[g % 2][:, :], ACT.Copy).then_inc(lgT_done, 1)
            act.wait_ge(routed, 11)
            nc.scalar.activation(small["exp"][:, :, :], small["less"][:, :, :], ACT.Exp).then_inc(exp_done, 1)
            for e in range(E):
                act.wait_ge(w_in[e % 2], 16 * (e // 2 + 1))
                nc.scalar.activation(w_hi[:, e, :, :], w_raw[:, e % 2, :, :], ACT.Copy).then_inc(whi_done, 1)
            with act.Fori(0, NG) as g:
                for u in range(NU):
                    act.wait_ge(gated, g * NU + (u + 1))
                    nc.scalar.activation(act_g[:, u % 2, :], gate_ps[u % 2][:, :], ACT.Gelu_apprx_tanh)\
                        .then_inc(gelu_done, 1)
                    if u >= 1:
                        high(act, g, u - 1)
                high(act, g, NU - 1)

        @block.vector
        def _(dve):
            dve.wait_ge(r_in, 64)
            for dt in range(DT):
                nc.vector.tensor_scalar(r_scaled[:, dt, :], r_raw[:, dt, :], r_scale[:, dt:dt + 1], D ** -0.5,
                                        ALU.mult, ALU.mult).then_inc(r_scaled_done, 1)
            dve.wait_ge(rhi_done, 1)
            nc.vector.tensor_tensor(r_lo[:, :, :], r_scaled[:, :, :], r_hi[:, :, :].bitcast(F32), ALU.subtract)\
                .then_inc(rlo_done, 1)
            dve.wait_ge(x_rstd_done, 1)
            for g in range(NG):
                dve.wait_ge(lg_ready, g + 1)
                nc.vector.tensor_tensor(small["logit"][:, g * G:(g + 1) * G, :],
                                        up_ps[g % 2][:, :].rearrange("p (b t) -> p b t", b=G)[:, :, 0:E],
                                        x_rstd[:, g * G:(g + 1) * G].unsqueeze(2).broadcast_to([P, G, E]),
                                        ALU.mult).then_inc(logit_done, 1)

            def wide(name):
                return top[name][:, :].unsqueeze(2).broadcast_to([P, B, E])

            def expert_row(ap):
                return ap[:, :].unsqueeze(1).broadcast_to([P, B, E])

            s = {n: ap[:, :, :] for n, ap in small.items()}
            step = [0]

            def chained(ins):
                step[0] += 1
                ins.then_inc(routed, 1)
                dve.wait_ge(routed, step[0])

            tt = nc.vector.tensor_tensor
            dve.wait_ge(logit_done, NG)
            chained(nc.vector.tensor_reduce(top["max1"][:, :], s["logit"], AX_X, ALU.max))
            chained(tt(s["tie"], s["logit"], wide("max1"), ALU.is_equal))
            chained(tt(s["order"], s["tie"], expert_row(rank), ALU.mult))
            chained(nc.vector.tensor_reduce(top["rank1"][:, :], s["order"], AX_X, ALU.max))
            chained(tt(s["first"], s["order"], wide("rank1"), ALU.is_equal))
            chained(nc.vector.scalar_tensor_tensor(s["rest"].rearrange("p b e -> p (b e)"),
                                                   s["first"].rearrange("p b e -> p (b e)"), -1e38,
                                                   s["logit"].rearrange("p b e -> p (b e)"), ALU.mult, ALU.add))
            chained(nc.vector.tensor_reduce(top["max2"][:, :], s["rest"], AX_X, ALU.max))
            chained(tt(s["tie2"], s["rest"], wide("max2"), ALU.is_equal))
            chained(tt(s["order2"], s["tie2"], expert_row(rank), ALU.mult))
            chained(nc.vector.tensor_reduce(top["rank2"][:, :], s["order2"], AX_X, ALU.max))
            chained(tt(s["less"], s["logit"], wide("max1"), ALU.subtract))
            chained(tt(s["second"], s["order2"], wide("rank2"), ALU.is_equal))
            chained(tt(s["chosen"], s["first"], s["second"], ALU.add))
            dve.wait_ge(exp_done, 1)
            chained(tt(s["picked"], s["exp"], s["chosen"], ALU.mult))
            chained(nc.vector.tensor_reduce(top["total"][:, :], s["picked"], AX_X, ALU.add))
            chained(nc.vector.reciprocal(top["inverse"][:, :], top["total"][:, :]))
            chained(tt(s["share"], s["picked"], wide("inverse"), ALU.mult))
            chained(tt(s["weight"], s["share"], expert_row(per_expert), ALU.mult))

            def accumulate(g, e):
                for j in range(G):
                    dve.wait_ge(down_done, g * E * G + (e * G + j // 2 * 2 + 2))
                    if e:
                        dve.wait_ge(acc_done, g * E * G + ((e + 1) * G + j + 1))
                    hold(dve)
                    src = acc[:, j, :] if e else one(X, g * G + j)
                    dst = acc[:, j, :] if e < E - 1 else one(X, g * G + j)
                    nc.vector.scalar_tensor_tensor(dst, out_ps[e % 2][j // 2][:, (j % 2) * D:(j % 2 + 1) * D],
                                                   w_grp[:, j, e:e + 1], src, ALU.mult, ALU.add).then_inc(acc_done, 1)

            dve.sem_inc(hid_done, 2)
            dve.sem_inc(acc_done, 2 * G)
            with dve.Fori(0, NG) as g:
                dve.wait_ge(acc_done, g * E * G + 2 * G)
                hold(dve)
                nc.vector.tensor_copy(w_grp[:, :, :], small["weight"][:, bass.ds(g * G, G), :]).then_inc(grp_done, 1)
                dve.wait_ge(grp_done, g + 1)
                hold(dve)
                for u in range(NU):
                    dve.wait_ge(gelu_done, g * NU + (u + 1))
                    if u >= 2:
                        dve.wait_ge(hid_lo_done, g * NU + (u - 1))
                    nc.vector.tensor_tensor(hid[:, u % 2, :], act_g[:, u % 2, :], up_ps[u % 2][:, :], ALU.mult)\
                        .then_inc(hid_done, 1)
                    if u % HT == HT - 1 and u >= 2 * HT - 1:
                        accumulate(g, u // HT - 1)
                accumulate(g, E - 1)

        @block.tensor
        def _(pe):
            pe.wait_ge(rlo_done, 1)
            for g in range(NG):
                toks = slice(g * GT, (g + 1) * GT)
                if g >= 2:
                    pe.wait_ge(lgT_done, g - 1)
                halves(nc, gate_ps[g % 2][:, :], [lambda dt: r_hi[:, dt, :], lambda dt: r_lo[:, dt, :]],
                       [lambda dt: XTh[:, dt, toks], lambda dt: XTl[:, dt, toks]], DT).then_inc(lgT_ready, 1)
                pe.wait_ge(lgT_done, g + 1)
                if g >= 2:
                    pe.wait_ge(logit_done, g - 1)
                for b in range(G):
                    last = nc.tensor.transpose(up_ps[g % 2][:, b * P:(b + 1) * P], lgT[:, b * T:(b + 1) * T], ident[:, :])
                last.then_inc(lg_ready, 1)
            pe.wait_ge(logit_done, NG)

            def gates(g, e):
                toks = bass.ds(g * GT, GT)
                x_halves = [lambda dt: XTh[:, dt, toks], lambda dt: XTl[:, dt, toks]]
                pe.wait_ge(wlo_done, e + 1)
                for ht in range(HT):
                    u = e * HT + ht
                    pe.wait_ge(hid_done, g * NU + (u + 1))
                    for ps, c0 in ((gate_ps[u % 2], ht * P), (up_ps[u % 2], D + ht * P)):
                        c = slice(c0, c0 + P)
                        last = halves(nc, ps[:, :], [lambda dt: w_hi[:, e, dt, c], lambda dt: w_lo[:, e, dt, c]],
                                      x_halves, DT)
                    last.then_inc(gated, 1)

            def down(g, e):
                pe.wait_ge(hid_lo_done, g * NU + (e * HT + HT))
                pe.wait_ge(acc_done, g * E * G + (e * G + G))
                for j in range(G):
                    toks = slice(j * T, (j + 1) * T)
                    halves(nc, out_ps[e % 2][j // 2][:, (j % 2) * D:(j % 2 + 1) * D],
                           [lambda n: hid_hi[:, e % 2, n, toks], lambda n: hid_lo[:, e % 2, n, toks]],
                           [lambda n: w_hi[:, e, n, WG:WE], lambda n: w_lo[:, e, n, WG:WE]], HT).then_inc(down_done, 1)

            with pe.Fori(0, NG) as g:
                gates(g, 0)
                for e in range(E):
                    if e + 1 < E:
                        gates(g, e + 1)
                    down(g, e)


def stage_attn1(nc, env, inp):
    X, XTh, XTl, ident = env["X"], env["XTh"], env["XTl"], env["ident"]
    H, DH = 16, P
    SCALE = 1.0 / math.sqrt(DH)
    N = H * NG
    BODY = 2 * NG
    FIRST = 3
    TURNS = (N - FIRST - NG - 2) // BODY
    QK = 2 * DH
    V2 = 2 * DH
    with ExitStack() as ctx:
        m = Mem(nc, ctx)
        w_raw = m.sb("a1_w_raw", [P, 2, DT, 2, QK])
        w_bias = m.sb("a1_w_bias", [P, 2, 3])
        w_full = m.sb("a1_w_full", [P, DT, QK])
        wv_raw = m.sb("a1_wv_raw", [P, DT, 2, V2])
        wv_full = m.sb("a1_wv_full", [P, DT, V2])
        wv_hi = m.sb("a1_wv_hi", [P, DT, V2], F32R)
        wv_lo = m.sb("a1_wv_lo", [P, DT, V2], F32R)
        w_hi = m.sb("a1_w_hi", [P, 2, DT, QK], F32R)
        w_lo = m.sb("a1_w_lo", [P, 2, DT, QK], F32R)
        o_raw = m.sb("a1_o_raw", [P, 2, 2, D])
        o_full = m.sb("a1_o_full", [P, D])
        o_hi = m.sb("a1_o_hi", [P, 2, D], F32R)
        o_lo = m.sb("a1_o_lo", [P, 2, D], F32R)
        bo = m.sb("a1_bo", [P, D])
        qT = m.sb("a1_qT", [P, 4, GT])
        kT = m.sb("a1_kT", [P, 4, GT])
        v = m.sb("a1_v", [P, NG, G, V2])
        negmax = m.sb("a1_negmax", [P, 2, G])
        shift = m.sb("a1_shift", [P, 2, G])
        sums = m.sb("a1_sums", [P, 2, G])
        recip = m.sb("a1_recip", [P, 2, G])
        probs = m.sb("a1_probs", [P, 2, G, T])
        normed = m.sb("a1_normed", [P, 2, G, T])
        normedT = m.sb("a1_normedT", [P, 2, GT])
        head_hi = m.sb("a1_head_hi", [P, 2, GT], F32R)
        head_lo = m.sb("a1_head_lo", [P, 2, GT], F32R)
        proj_ps = [m.ps(f"a1_proj_ps{i}", [P, BANK]) for i in range(2)]
        s_ps = m.ps("a1_s_ps", [P, BANK])
        nT_ps = m.ps("a1_nT_ps", [P, BANK])
        v_ps = m.ps("a1_v_ps", [P, BANK])
        head_ps = m.ps("a1_head_ps", [P, BANK])
        out_ps = [m.ps(f"a1_out_ps{i}", [P, BANK]) for i in range(2)]
        w_in = [m.sem(f"a1_w_in{i}") for i in range(2)]
        o_in = [m.sem(f"a1_o_in{i}") for i in range(2)]
        b_in = [m.sem(f"a1_b_in{i}") for i in range(2)]
        bo_in = m.sem("a1_bo_in")
        wv_in = m.sem("a1_wv_in")
        wvfull_done = m.sem("a1_wvfull_done")
        wvhi_done = m.sem("a1_wvhi_done")
        wvlo_done = m.sem("a1_wvlo_done")
        bo_done = m.sem("a1_bo_done")
        wfull_done = m.sem("a1_wfull_done")
        whi_done = m.sem("a1_whi_done")
        wlo_done = m.sem("a1_wlo_done")
        ofull_done = m.sem("a1_ofull_done")
        ohi_done = m.sem("a1_ohi_done")
        olo_done = m.sem("a1_olo_done")
        projected = m.sem("a1_projected")
        proj_read = m.sem("a1_proj_read")
        v_projected = m.sem("a1_v_projected")
        v_done = m.sem("a1_v_done")
        scored = m.sem("a1_scored")
        maxed = m.sem("a1_maxed")
        shifted = m.sem("a1_shifted")
        exped = m.sem("a1_exped")
        recip_done = m.sem("a1_recip_done")
        normed_done = m.sem("a1_normed_done")
        turned = m.sem("a1_turned")
        nT_done = m.sem("a1_nT_done")
        valued = m.sem("a1_valued")
        hi_done = m.sem("a1_hi_done")
        lo_done = m.sem("a1_lo_done")
        multiplied = m.sem("a1_multiplied")
        added = m.sem("a1_added")
        block = ctx.enter_context(nc.Block())

        def run(eng, step):
            for k in range(FIRST):
                step(0, k)
            with eng.Fori(0, TURNS) as i:
                for k in range(FIRST, FIRST + BODY):
                    step(i, k)
            for k in range(FIRST, N + 3 - TURNS * BODY):
                step(TURNS, k)

        def inside(i, k):
            return not isinstance(i, int) or 0 <= i * BODY + k < N

        def has_values(k):
            return k // NG % 2 == 0

        def rounds(i, k):
            return i * (2 * NG) + 2 * (k // BODY * NG + k % NG)

        def w_low(pool, i, h):
            pool.wait_ge(whi_done, i * 2 + (h + 1))
            nc.gpsimd.tensor_tensor(w_lo[:, h % 2, :, :], w_full[:, :, :], w_hi[:, h % 2, :, :].bitcast(F32),
                                    ALU.subtract).then_inc(wlo_done, 1)
            if h % 2 == 0:
                pool.wait_ge(wvhi_done, i + (h // 2 + 1))
                nc.gpsimd.tensor_tensor(wv_lo[:, :, :], wv_full[:, :, :], wv_hi[:, :, :].bitcast(F32),
                                        ALU.subtract).then_inc(wvlo_done, 1)

        def w_high(act, i, h):
            act.wait_ge(wfull_done, i * 2 + (h + 1))
            nc.scalar.activation(w_hi[:, h % 2, :, :], w_full[:, :, :], ACT.Copy).then_inc(whi_done, 1)
            if h % 2 == 0:
                act.wait_ge(wvfull_done, i + (h // 2 + 1))
                nc.scalar.activation(wv_hi[:, :, :], wv_full[:, :, :], ACT.Copy).then_inc(wvhi_done, 1)

        def w_multiply(dve, i, h):
            dve.wait_ge(w_in[h % 2], i * 16 + (h // 2 + 1) * 16)
            if not (isinstance(i, int) and i * BODY + h == 0):
                dve.wait_ge(wlo_done, i * 2 + h)
            nc.vector.tensor_tensor(w_full[:, :, :], w_raw[:, h % 2, :, 0, :], w_raw[:, h % 2, :, 1, :], ALU.mult)\
                .then_inc(wfull_done, 1)
            if h % 2 == 0:
                dve.wait_ge(wv_in, i * 16 + (h // 2 + 1) * 16)
                if not (isinstance(i, int) and i * BODY + h == 0):
                    dve.wait_ge(wvlo_done, i + h // 2)
                nc.vector.tensor_tensor(wv_full[:, :, :], wv_raw[:, :, 0, :], wv_raw[:, :, 1, :], ALU.mult)\
                    .then_inc(wvfull_done, 1)

        def project_read(act, i, k):
            par = k // NG % 2
            if k % NG == 0:
                act.wait_ge(b_in[par], i * 16 + (k // BODY + 1) * 16)
            for a, dst in enumerate((qT, kT)):
                act.wait_ge(projected, i * (2 * BODY) + (2 * k + a + 1))
                nc.scalar.activation(dst[:, k % 4, :], proj_ps[a][:, :], ACT.Identity, bias=w_bias[:, par, a:a + 1])\
                    .then_inc(proj_read, 1)

        def values_read(act, i, k, half):
            act.wait_ge(v_projected, rounds(i, k) + (half + 1))
            nc.scalar.activation(v[:, k % NG, 2 * half:2 * half + 2, :], v_ps[:, :].rearrange("p (b n) -> p b n", b=2),
                                 ACT.Copy).then_inc(v_done, 1)

        @block.sync
        def _(sp):
            sp.dma_start(bo[:, :], inp["a1_bo"].partition_broadcast(P)).then_inc(bo_in, 16)

            def load(h, par, guard, pair):
                if guard is not None:
                    if par == 0:
                        sp.wait_ge(wvlo_done, pair)
                    sp.wait_ge(wlo_done, guard)
                    sp.wait_ge(olo_done, guard)
                    hold(sp)
                pick = (lambda x: x[bass.ds(h, 1)].rearrange("o r c -> r (o c)")) if guard is not None else (lambda x: x[h])
                if par == 0:
                    wv_src = inp["a1_wv"][bass.ds(pair, 1)].rearrange("o r c -> r (o c)") if guard is not None \
                        else inp["a1_wv"][pair]
                w_src = pick(inp["a1_w"])
                sp.dma_start(w_raw[:, par, :, :, :].rearrange("p k a n -> p k (a n)"),
                             w_src.rearrange("(k p) n -> p k n", p=P)).then_inc(w_in[par], 16)
                if par == 0:
                    sp.dma_start(wv_raw[:, :, :, :].rearrange("p k a n -> p k (a n)"),
                                 wv_src.rearrange("(k p) n -> p k n", p=P)).then_inc(wv_in, 16)
                sp.dma_start(o_raw[:, par, :, :].rearrange("p a n -> p (a n)"), pick(inp["a1_wo"])).then_inc(o_in[par], 16)
                if guard is not None:
                    sp.wait_ge(lo_done, guard * NG)
                    hold(sp)
                sp.dma_start(w_bias[:, par, :], pick(inp["a1_bias"])).then_inc(b_in[par], 16)

            for h in range(2):
                load(h, h, None, 0)
            with sp.Fori(1, H // 2) as i:
                for par in range(2):
                    load(i * 2 + par, par, i * 2 + (par - 1), i)

        @block.gpsimd
        def _(pool):
            w_low(pool, 0, 0)
            w_low(pool, 0, 1)
            pool.wait_ge(bo_in, 16)
            nc.gpsimd.tensor_tensor(X[:, :, :], X[:, :, :], bo[:, :].unsqueeze(1).broadcast_to([P, B, D]), ALU.add)\
                .then_inc(bo_done, 1)

            def step(i, k):
                if inside(i, k):
                    pool.wait_ge(recip_done, i * BODY + (k + 1))
                    nc.gpsimd.tensor_tensor(normed[:, k % 2, :, :], probs[:, k % 2, :, :],
                                            recip[:, k % 2, :].unsqueeze(2).broadcast_to([P, G, T]), ALU.mult)\
                        .then_inc(normed_done, 1)
                if k % NG == 2 and inside(i, k + 6):
                    w_low(pool, i, (k + 6) // NG)
                if k % NG == 0 and inside(i, k):
                    hq = k // NG
                    pool.wait_ge(ohi_done, i * 2 + (hq + 1))
                    nc.gpsimd.tensor_tensor(o_lo[:, hq % 2, :], o_full[:, :], o_hi[:, hq % 2, :].bitcast(F32),
                                            ALU.subtract).then_inc(olo_done, 1)

            run(pool, step)

        @block.scalar
        def _(act):
            w_high(act, 0, 0)
            w_high(act, 0, 1)
            for k in range(2):
                project_read(act, 0, k)
                for half in range(2):
                    values_read(act, 0, k, half)

            def step(i, k):
                if inside(i, k):
                    act.wait_ge(shifted, i * BODY + (k + 1))
                    for j in range(G):
                        nc.scalar.activation(probs[:, k % 2, j, :], s_ps[:, j * T:(j + 1) * T], ACT.Exp, scale=SCALE,
                                             bias=shift[:, k % 2, j:j + 1], accum_out=sums[:, k % 2, j:j + 1])\
                            .then_inc(exped, 1)
                if inside(i, k - 1):
                    act.wait_ge(turned, i * BODY + k)
                    nc.scalar.activation(normedT[:, (k - 1) % 2, :], nT_ps[:, :], ACT.Copy).then_inc(nT_done, 1)
                if inside(i, k + 2):
                    project_read(act, i, k + 2)
                    if has_values(k + 2):
                        values_read(act, i, k + 2, 0)
                if inside(i, k - 1):
                    act.wait_ge(valued, i * BODY + k)
                    nc.scalar.activation(head_hi[:, (k - 1) % 2, :], head_ps[:, :], ACT.Identity,
                                         bias=w_bias[:, (k - 1) // NG % 2, 2:3]).then_inc(hi_done, 1)
                if inside(i, k + 2) and has_values(k + 2):
                    values_read(act, i, k + 2, 1)
                if k % NG == 2 and inside(i, k + 6):
                    w_high(act, i, (k + 6) // NG)
                if k % NG == 0 and inside(i, k):
                    hq = k // NG
                    act.wait_ge(ofull_done, i * 2 + (hq + 1))
                    nc.scalar.activation(o_hi[:, hq % 2, :], o_full[:, :], ACT.Copy).then_inc(ohi_done, 1)

            run(act, step)

        @block.vector
        def _(dve):
            w_multiply(dve, 0, 0)
            w_multiply(dve, 0, 1)

            def step(i, k):
                if inside(i, k):
                    dve.wait_ge(scored, i * BODY + (k + 1))
                    nc.vector.tensor_reduce(negmax[:, k % 2, :], s_ps[:, :].rearrange("p (b s) -> p b s", b=G),
                                            AX_X, ALU.max, negate=True).then_inc(maxed, 1)
                    dve.wait_ge(maxed, i * BODY + (k + 1))
                    nc.vector.tensor_scalar(shift[:, k % 2, :], negmax[:, k % 2, :], SCALE, None, ALU.mult)\
                        .then_inc(shifted, 1)
                if inside(i, k - 3):
                    g = (k - 3) % NG
                    if isinstance(i, int) and i * BODY + k == 3:
                        dve.wait_ge(bo_done, 1)
                    dve.wait_ge(multiplied, i * BODY + (k - 2))
                    for c in range(2):
                        xs = X[:, g * G + 2 * c:g * G + 2 * c + 2, :].rearrange("p b d -> p (b d)")
                        last = nc.vector.tensor_tensor(xs, xs, out_ps[c][:, :], ALU.add)
                    last.then_inc(added, 1)
                if k % NG == 2 and inside(i, k + 6):
                    w_multiply(dve, i, (k + 6) // NG)
                if k % NG == 0 and inside(i, k):
                    hq = k // NG
                    dve.wait_ge(o_in[hq % 2], i * 16 + (hq // 2 + 1) * 16)
                    if hq or not isinstance(i, int) or i:
                        dve.wait_ge(olo_done, i * 2 + hq)
                    nc.vector.tensor_tensor(o_full[:, :], o_raw[:, hq % 2, 0, :], o_raw[:, hq % 2, 1, :], ALU.mult)\
                        .then_inc(ofull_done, 1)
                if inside(i, k):
                    dve.wait_ge(exped, i * (G * BODY) + (G * k + G))
                    nc.vector.reciprocal(recip[:, k % 2, :], sums[:, k % 2, :]).then_inc(recip_done, 1)
                if inside(i, k - 1):
                    dve.wait_ge(hi_done, i * BODY + k)
                    nc.vector.scalar_tensor_tensor(head_lo[:, (k - 1) % 2, :], head_ps[:, :],
                                                   w_bias[:, (k - 1) // NG % 2, 2:3],
                                                   head_hi[:, (k - 1) % 2, :].bitcast(F32),
                                                   ALU.add, ALU.subtract).then_inc(lo_done, 1)

            run(dve, step)

        @block.tensor
        def _(pe):
            def project(i, k):
                g, par = k % NG, k // NG % 2
                toks = slice(g * GT, (g + 1) * GT)
                if g == 0:
                    pe.wait_ge(wlo_done, i * 2 + (k // NG + 1))
                for a in range(2):
                    if not (isinstance(i, int) and i * BODY + k < 1):
                        pe.wait_ge(proj_read, i * (2 * BODY) + (2 * k + a - 1))
                    c = slice(a * DH, (a + 1) * DH)
                    halves(nc, proj_ps[a][:, :],
                           [lambda dt: w_hi[:, par, dt, c], lambda dt: w_lo[:, par, dt, c]],
                           [lambda dt: XTh[:, dt, toks], lambda dt: XTl[:, dt, toks]], DT).then_inc(projected, 1)

            def project_values(i, k, half):
                if k % BODY == 0 and half == 0:
                    pe.wait_ge(wvlo_done, i + (k // BODY + 1))
                if not (isinstance(i, int) and i * BODY + k + half < 1):
                    pe.wait_ge(v_done, rounds(i, k) + half)
                for j in range(2):
                    at = (k % NG * G + 2 * half + j) * T
                    toks = slice(at, at + T)
                    last = halves(nc, v_ps[:, j * V2:(j + 1) * V2],
                                  [lambda dt: XTh[:, dt, toks], lambda dt: XTl[:, dt, toks]],
                                  [lambda dt: wv_hi[:, dt, :], lambda dt: wv_lo[:, dt, :]], DT)
                last.then_inc(v_projected, 1)

            for k in range(2):
                project(0, k)
                for half in range(2):
                    project_values(0, k, half)

            def step(i, k):
                if inside(i, k):
                    if not (isinstance(i, int) and i * BODY + k < 1):
                        pe.wait_ge(exped, i * (G * BODY) + G * k)
                    pe.wait_ge(proj_read, i * (2 * BODY) + (2 * k + 2))
                    for j in range(G):
                        toks = slice(j * T, (j + 1) * T)
                        last = nc.tensor.matmul(s_ps[:, toks], qT[:, k % 4, toks], kT[:, k % 4, toks],
                                                start=True, stop=True)
                    last.then_inc(scored, 1)
                if inside(i, k - 1):
                    pe.wait_ge(normed_done, i * BODY + k)
                    for j in range(G):
                        last = nc.tensor.transpose(nT_ps[:, j * T:(j + 1) * T], normed[:, (k - 1) % 2, j, :], ident[:, :])
                    last.then_inc(turned, 1)
                if inside(i, k + 2):
                    project(i, k + 2)
                    if has_values(k + 2):
                        project_values(i, k + 2, 0)
                if inside(i, k - 1):
                    pe.wait_ge(nT_done, i * BODY + k)
                    if inside(i, k - 2):
                        pe.wait_ge(lo_done, i * BODY + (k - 1))
                    pe.wait_ge(v_done, rounds(i, k - 1) + 2)
                    pair = slice((k - 1) // NG % 2 * DH, ((k - 1) // NG % 2 + 1) * DH)
                    for j in range(G):
                        toks = slice(j * T, (j + 1) * T)
                        last = nc.tensor.matmul(head_ps[:, toks], v[:, (k - 1) % NG, j, pair], normedT[:, (k - 1) % 2, toks],
                                                start=True, stop=True)
                    last.then_inc(valued, 1)
                if inside(i, k + 2) and has_values(k + 2):
                    project_values(i, k + 2, 1)
                if inside(i, k - 2):
                    q, hq = (k - 2) % 2, (k - 2) // NG
                    pe.wait_ge(lo_done, i * BODY + (k - 1))
                    pe.wait_ge(olo_done, i * 2 + (hq + 1))
                    if inside(i, k - 3):
                        pe.wait_ge(added, i * BODY + (k - 2))
                    for j in range(G):
                        toks = slice(j * T, (j + 1) * T)
                        last = halves(nc, out_ps[j // 2][:, (j % 2) * D:(j % 2 + 1) * D],
                                      [lambda n: head_hi[:, q, toks], lambda n: head_lo[:, q, toks]],
                                      [lambda n: o_hi[:, hq % 2, :], lambda n: o_lo[:, hq % 2, :]], 1)
                    last.then_inc(multiplied, 1)

            run(pe, step)


def stage_wkv1(nc, env, inp):
    X, XTk, ident = env["X"], env["XTk"], env["ident"]
    N = NG * DT
    LOW = -1e38
    with ExitStack() as ctx:
        m = Mem(nc, ctx)
        values = m.sb("k1_values", [P, DT, B * T])
        decay = m.sb("k1_decay", [P, DT])
        first = m.sb("k1_first", [P, DT])
        exp_decay = m.sb("k1_exp_decay", [P, DT])
        w = m.sb("k1_w", [P, DT])
        w_row = m.sb("k1_w_row", [P, DT, G, T + 1])
        pp = m.sb("k1_pp", [P, 2, G, T + 1])
        aa = m.sb("k1_aa", [P, G, T + 1])
        bb = m.sb("k1_bb", [P, G, T + 1])
        q = m.sb("k1_q", [P, G, T])
        d_out = m.sb("k1_d_out", [P, 2, 2, G, T])
        d_next = m.sb("k1_d_next", [P, 2, 2, G, T])
        e_out = m.sb("k1_e_out", [P, 2, 2, G, T])
        e_next = m.sb("k1_e_next", [P, 2, 2, G, T + 1])
        ev_next = m.sb("k1_ev_next", [P, 2, G, T + 1])
        ev_out = m.sb("k1_ev_out", [P, 2, G, T])
        num = m.sb("k1_num", [P, G, T])
        den = m.sb("k1_den", [P, G, T])
        num_sum = m.sb("k1_num_sum", [P, G, T])
        den_sum = m.sb("k1_den_sum", [P, G, T])
        den_inv = m.sb("k1_den_inv", [P, G, T])
        y = m.sb("k1_y", [P, 2, G, T])
        y_ps = [m.ps(f"k1_y_ps{i}", [P, BANK]) for i in range(2)]
        v_in = m.sem("k1_v_in")
        p_in = m.sem("k1_p_in")
        exp_decay_done = m.sem("k1_exp_decay_done")
        w_done = m.sem("k1_w_done")
        row_done = m.sem("k1_row_done")
        starts = m.sem("k1_starts")
        pp_done = m.sem("k1_pp_done")
        q_done = m.sem("k1_q_done")
        dve_exponents = m.sem("k1_dve_exponents")
        pool_exponents = m.sem("k1_pool_exponents")
        next_done = m.sem("k1_next_done")
        out_done = m.sem("k1_out_done")
        ev_next_done = m.sem("k1_ev_next_done")
        ev_out_done = m.sem("k1_ev_out_done")
        scanned = m.sem("k1_scanned")
        weighted = m.sem("k1_weighted")
        summed = m.sem("k1_summed")
        inverted = m.sem("k1_inverted")
        y_done = m.sem("k1_y_done")
        turned = m.sem("k1_turned")
        added = m.sem("k1_added")
        block = ctx.enter_context(nc.Block())

        def group(g, n):
            return slice(g * n, (g + 1) * n) if isinstance(g, int) else bass.ds(g * n, n)

        def k_of(g, ct):
            return XTk[:, ct, group(g, G), 1:T + 1]

        def v_of(g, ct):
            return values[:, ct, group(g, GT)].rearrange("p (b t) -> p b t", b=G)

        def flat(ap):
            return ap.rearrange("p b t -> p (b t)")

        @block.sync
        def _(sp):
            sp.dma_start(decay[:, :], inp["k1_decay"]).then_inc(p_in, 16)
            sp.dma_start(first[:, :], inp["k1_first"]).then_inc(p_in, 16)
            sp.dma_start(values[:, :, :], inp["ctxT"].rearrange("k p n -> p k n")).then_inc(v_in, 16)

        @block.scalar
        def _(act):
            act.wait_ge(p_in, 32)
            nc.scalar.activation(exp_decay[:, :], decay[:, :], ACT.Exp).then_inc(exp_decay_done, 1)
            with act.Fori(0, NG) as g:
                for ct in range(DT):
                    act.wait_ge(dve_exponents, g * (2 * DT) + (2 * ct + 2))
                    act.wait_ge(pool_exponents, g * (2 * DT) + (2 * ct + 3))
                    act.wait_ge(y_done, g * DT + (ct + 1))
                    nc.scalar.activation(e_next[:, ct, :, :, 1:T + 1].rearrange("p k b t -> p (k b) t"),
                                         d_next[:, ct, :, :, :].rearrange("p k b t -> p (k b) t"), ACT.Exp)\
                        .then_inc(next_done, 1)
                    nc.scalar.activation(e_out[:, ct, :, :, :], d_out[:, ct, :, :, :], ACT.Exp).then_inc(out_done, 1)

        @block.gpsimd
        def _(pool):
            pool.wait_ge(exp_decay_done, 1)
            nc.gpsimd.tensor_scalar(w[:, :], exp_decay[:, :], -1.0, None, ALU.mult).then_inc(w_done, 1)
            pool.wait_ge(w_done, 1)
            for ct in range(DT):
                nc.gpsimd.tensor_copy(w_row[:, ct, :, 1:T + 1], w[:, ct:ct + 1].unsqueeze(2).broadcast_to([P, G, T]))\
                    .then_inc(row_done, 1)
                nc.gpsimd.memset(w_row[:, ct, :, 0:1], LOW).then_inc(row_done, 1)
                nc.gpsimd.memset(XTk[:, ct, :, 0:1], LOW).then_inc(starts, 1)
                nc.gpsimd.memset(ev_next[:, ct, :, 0:1], 0.0).then_inc(starts, 1)
                for k in range(2):
                    nc.gpsimd.memset(e_next[:, ct, k, :, 0:1], 0.0).then_inc(starts, 1)

            def exponents(g, ct):
                pool.wait_ge(q_done, g * DT + (ct + 1))
                pool.wait_ge(next_done, g * DT + (ct + 1))
                hold(pool)
                nc.gpsimd.tensor_tensor(d_next[:, ct, 1, :, :], k_of(g, ct), pp[:, ct, :, 1:T + 1], ALU.subtract)\
                    .then_inc(pool_exponents, 1)
                pool.wait_ge(out_done, g * DT + (ct + 1))
                nc.gpsimd.tensor_tensor(d_out[:, ct, 0, :, :], pp[:, ct, :, 0:T], q[:, :, :], ALU.subtract)\
                    .then_inc(pool_exponents, 1)

            def weigh(g, ct):
                pool.wait_ge(next_done, g * DT + (ct + 3))
                pool.wait_ge(y_done, g * DT + (ct + 1))
                hold(pool)
                nc.gpsimd.tensor_tensor(ev_next[:, ct, :, 1:T + 1], e_next[:, ct, 1, :, 1:T + 1], v_of(g, ct), ALU.mult)\
                    .then_inc(ev_next_done, 1)
                pool.wait_ge(out_done, g * DT + (ct + 3))
                hold(pool)
                nc.gpsimd.tensor_tensor(ev_out[:, ct, :, :], e_out[:, ct, 1, :, :], v_of(g, ct), ALU.mult)\
                    .then_inc(ev_out_done, 1)

            pool.sem_inc(next_done, 2)
            pool.sem_inc(out_done, 2)
            pool.wait_ge(v_in, 16)
            exponents(0, 0)
            with pool.Fori(0, NG - 1) as g:
                exponents(g, 1)
                weigh(g, 0)
                exponents(g + 1, 0)
                weigh(g, 1)
            exponents(NG - 1, 1)
            weigh(NG - 1, 0)
            weigh(NG - 1, 1)

        @block.vector
        def _(dve):
            def exponents(g, ct):
                dve.wait_ge(pool_exponents, g * (2 * DT) + (2 * ct + 1))
                hold(dve)
                nc.vector.tensor_tensor_scan(flat(pp[:, ct, :, :]), flat(w_row[:, ct, :, :]),
                                             flat(XTk[:, ct, group(g, G), :]), LOW,
                                             ALU.add, ALU.max).then_inc(pp_done, 1)
                dve.wait_ge(pp_done, g * DT + (ct + 1))
                hold(dve)
                nc.vector.scalar_tensor_tensor(q[:, :, :], k_of(g, ct), first[:, ct:ct + 1], pp[:, ct, :, 0:T],
                                               ALU.add, ALU.max).then_inc(q_done, 1)
                nc.vector.scalar_tensor_tensor(d_next[:, ct, 0, :, :], pp[:, ct, :, 0:T], w[:, ct:ct + 1],
                                               pp[:, ct, :, 1:T + 1], ALU.add, ALU.subtract).then_inc(dve_exponents, 1)
                dve.wait_ge(q_done, g * DT + (ct + 1))
                hold(dve)
                nc.vector.scalar_tensor_tensor(d_out[:, ct, 1, :, :], k_of(g, ct), first[:, ct:ct + 1], q[:, :, :],
                                               ALU.add, ALU.subtract).then_inc(dve_exponents, 1)

            def output(g, ct):
                n = g * DT + ct
                tt = nc.vector.tensor_tensor
                dve.wait_ge(next_done, n + 3)
                nc.vector.tensor_tensor_scan(flat(bb[:, :, :]), flat(e_next[:, ct, 0, :, :]), flat(e_next[:, ct, 1, :, :]), 0.0,
                                             ALU.mult, ALU.add).then_inc(scanned, 1)
                dve.wait_ge(ev_next_done, n + 1)
                nc.vector.tensor_tensor_scan(flat(aa[:, :, :]), flat(e_next[:, ct, 0, :, :]), flat(ev_next[:, ct, :, :]), 0.0,
                                             ALU.mult, ALU.add).then_inc(scanned, 1)
                dve.wait_ge(out_done, n + 3)
                dve.wait_ge(scanned, n * 2 + 1)
                tt(den[:, :, :], e_out[:, ct, 0, :, :], bb[:, :, 0:T], ALU.mult).then_inc(weighted, 1)
                dve.wait_ge(scanned, n * 2 + 2)
                tt(num[:, :, :], e_out[:, ct, 0, :, :], aa[:, :, 0:T], ALU.mult).then_inc(weighted, 1)
                dve.wait_ge(weighted, n * 2 + 1)
                tt(den_sum[:, :, :], den[:, :, :], e_out[:, ct, 1, :, :], ALU.add).then_inc(summed, 1)
                dve.wait_ge(weighted, n * 2 + 2)
                dve.wait_ge(ev_out_done, n + 1)
                tt(num_sum[:, :, :], num[:, :, :], ev_out[:, ct, :, :], ALU.add).then_inc(summed, 1)
                dve.wait_ge(summed, n * 2 + 1)
                nc.vector.reciprocal(den_inv[:, :, :], den_sum[:, :, :]).then_inc(inverted, 1)
                dve.wait_ge(summed, n * 2 + 2)
                dve.wait_ge(inverted, n + 1)
                dve.wait_ge(turned, n + 1)
                tt(y[:, ct, :, :], num_sum[:, :, :], den_inv[:, :, :], ALU.mult).then_inc(y_done, 1)

            def add(g, ct):
                n = g * DT + ct
                dve.wait_ge(turned, n + 3)
                hold(dve)
                xs = X[:, group(g, G), ct * P:(ct + 1) * P]
                nc.vector.tensor_tensor(xs, xs, y_ps[ct][:, :].rearrange("p (b c) -> p b c", b=G), ALU.add)\
                    .then_inc(added, 1)

            dve.sem_inc(pool_exponents, 1)
            dve.sem_inc(y_done, 2)
            dve.wait_ge(row_done, 2 * DT)
            dve.wait_ge(starts, 4 * DT)
            hold(dve)
            exponents(0, 0)
            with dve.Fori(0, NG - 1) as g:
                exponents(g, 1)
                output(g, 0)
                exponents(g + 1, 0)
                add(g, 0)
                output(g, 1)
                add(g, 1)
            exponents(NG - 1, 1)
            for ct in range(DT):
                output(NG - 1, ct)
                add(NG - 1, ct)

        @block.tensor
        def _(pe):
            pe.sem_inc(turned, 2)
            pe.sem_inc(added, 2)
            with pe.Fori(0, NG) as g:
                for ct in range(DT):
                    pe.wait_ge(y_done, g * DT + (ct + 3))
                    pe.wait_ge(added, g * DT + (ct + 1))
                    for j in range(G):
                        last = nc.tensor.transpose(y_ps[ct][:, j * P:(j + 1) * P], y[:, ct, j, :], ident[:, :])
                    last.then_inc(turned, 1)


def stage_ffn1(nc, env, inp):
    X, XTh, XTl, ident = env["X"], env["XTh"], env["XTl"], env["ident"]
    E, R = 8, 16
    SCALING = 32.0 / R
    LG = slice(D, D + E)
    LR = slice(D + E, D + E + E * R)
    W = D + E + E * R
    with ExitStack() as ctx:
        m = Mem(nc, ctx)
        w_raw = m.sb("f1_w_raw", [P, DT, W])
        w_hi = m.sb("f1_w_hi", [P, DT, W], F32R)
        w_lo = m.sb("f1_w_lo", [P, DT, W], F32R)
        b_raw = m.sb("f1_b_raw", [P, D])
        b_hi = m.sb("f1_b_hi", [P, D], F32R)
        b_lo = m.sb("f1_b_lo", [P, D], F32R)
        bias = m.sb("f1_bias", [P, D])
        rank = m.sb("f1_rank", [P, E])
        x_hi = m.sb("f1_x_hi", [P, DT, GT], F32R)
        x_lo = m.sb("f1_x_lo", [P, DT, GT], F32R)
        best = m.sb("f1_best", [P, G])
        tie = m.sb("f1_tie", [P, G, E])
        order = m.sb("f1_order", [P, G, E])
        best_rank = m.sb("f1_best_rank", [P, G])
        chosen = m.sb("f1_chosen", [P, G, E])
        low = m.sb("f1_low", [P, G, E * R])
        low_hi = m.sb("f1_low_hi", [P, GT], F32R)
        low_lo = m.sb("f1_low_lo", [P, GT], F32R)
        in_ps = m.ps("f1_in_ps", [P, G, BANK])
        lowT_ps = m.ps("f1_lowT_ps", [P, BANK])
        delta_ps = m.ps("f1_delta_ps", [P, G, D])
        w_in = m.sem("f1_w_in")
        b_in = m.sem("f1_b_in")
        whi_done = m.sem("f1_whi_done")
        wlo_done = m.sem("f1_wlo_done")
        bhi_done = m.sem("f1_bhi_done")
        blo_done = m.sem("f1_blo_done")
        bias_done = m.sem("f1_bias_done")
        xhi_done = m.sem("f1_xhi_done")
        xlo_done = m.sem("f1_xlo_done")
        multiplied = m.sem("f1_multiplied")
        routed = m.sem("f1_routed")
        low_done = m.sem("f1_low_done")
        turned = m.sem("f1_turned")
        low_hi_done = m.sem("f1_low_hi_done")
        low_lo_done = m.sem("f1_low_lo_done")
        base_added = m.sem("f1_base_added")
        delta_done = m.sem("f1_delta_done")
        delta_added = m.sem("f1_delta_added")
        block = ctx.enter_context(nc.Block())

        @block.sync
        def _(sp):
            sp.dma_start(w_raw[:, :, :], inp["f1_w"].rearrange("(k p) n -> p k n", p=P)).then_inc(w_in, 16)
            sp.dma_start(b_raw[:, :], inp["f1_b"]).then_inc(b_in, 16)
            sp.dma_start(bias[:, :], inp["f1_bias"].partition_broadcast(P)).then_inc(b_in, 16)
            sp.dma_start(rank[:, :], inp["m0_rank"].partition_broadcast(P)).then_inc(b_in, 16)

        @block.gpsimd
        def _(pool):
            pool.wait_ge(b_in, 48)
            nc.gpsimd.tensor_tensor(X[:, :, :], X[:, :, :], bias[:, :].unsqueeze(1).broadcast_to([P, B, D]), ALU.add)\
                .then_inc(bias_done, 1)
            with pool.Fori(0, NG) as g:
                pool.wait_ge(multiplied, g + 1)
                hold(pool)
                nc.gpsimd.tensor_copy(x_lo[:, :, :], XTl[:, :, bass.ds(g * GT, GT)]).then_inc(xlo_done, 1)

        @block.scalar
        def _(act):
            act.wait_ge(w_in, 16)
            nc.scalar.activation(w_hi[:, :, :], w_raw[:, :, :], ACT.Copy).then_inc(whi_done, 1)
            act.wait_ge(b_in, 48)
            nc.scalar.activation(b_hi[:, :], b_raw[:, :], ACT.Copy, scale=SCALING).then_inc(bhi_done, 1)
            with act.Fori(0, NG) as g:
                act.wait_ge(multiplied, g + 1)
                hold(act)
                nc.scalar.activation(x_hi[:, :, :], XTh[:, :, bass.ds(g * GT, GT)].bitcast(F32), ACT.Copy)\
                    .then_inc(xhi_done, 1)
                act.wait_ge(turned, g + 1)
                nc.scalar.activation(low_hi[:, :], lowT_ps[:, :], ACT.Copy).then_inc(low_hi_done, 1)

        @block.vector
        def _(dve):
            dve.wait_ge(whi_done, 1)
            nc.vector.tensor_tensor(w_lo[:, :, :], w_raw[:, :, :], w_hi[:, :, :].bitcast(F32), ALU.subtract)\
                .then_inc(wlo_done, 1)
            dve.wait_ge(bhi_done, 1)
            nc.vector.scalar_tensor_tensor(b_lo[:, :], b_raw[:, :], SCALING, b_hi[:, :].bitcast(F32), ALU.mult, ALU.subtract)\
                .then_inc(blo_done, 1)
            dve.wait_ge(bias_done, 1)
            hold(dve)
            tt = nc.vector.tensor_tensor
            with dve.Fori(0, NG) as g:
                dve.wait_ge(multiplied, g + 2)
                hold(dve)
                nc.vector.tensor_reduce(best[:, :], in_ps[:, :, LG], AX_X, ALU.max).then_inc(routed, 1)
                dve.wait_ge(routed, g * 5 + 1)
                tt(tie[:, :, :], in_ps[:, :, LG], best[:, :].unsqueeze(2).broadcast_to([P, G, E]), ALU.is_equal)\
                    .then_inc(routed, 1)
                dve.wait_ge(routed, g * 5 + 2)
                tt(order[:, :, :], tie[:, :, :], rank[:, :].unsqueeze(1).broadcast_to([P, G, E]), ALU.mult)\
                    .then_inc(routed, 1)
                dve.wait_ge(routed, g * 5 + 3)
                hold(dve)
                nc.vector.tensor_reduce(best_rank[:, :], order[:, :, :], AX_X, ALU.max).then_inc(routed, 1)
                dve.wait_ge(routed, g * 5 + 4)
                tt(chosen[:, :, :], order[:, :, :], best_rank[:, :].unsqueeze(2).broadcast_to([P, G, E]), ALU.is_equal)\
                    .then_inc(routed, 1)
                dve.wait_ge(routed, g * 5 + 5)
                tt(low[:, :, :].rearrange("p b (e r) -> p b e r", e=E),
                   in_ps[:, :, LR].rearrange("p b (e r) -> p b e r", e=E),
                   chosen[:, :, :].unsqueeze(3).broadcast_to([P, G, E, R]), ALU.mult).then_inc(low_done, 1)
                xs = X[:, bass.ds(g * G, G), :]
                hold(dve)
                tt(xs, xs, in_ps[:, :, 0:D], ALU.add).then_inc(base_added, 1)
                dve.wait_ge(low_hi_done, g + 1)
                tt(low_lo[:, :], lowT_ps[:, :], low_hi[:, :].bitcast(F32), ALU.subtract).then_inc(low_lo_done, 1)
                dve.wait_ge(delta_done, g + 1)
                dve.wait_ge(base_added, g + 1)
                hold(dve)
                tt(xs, xs, delta_ps[:, :, :], ALU.add).then_inc(delta_added, 1)

        @block.tensor
        def _(pe):
            pe.sem_inc(multiplied, 1)
            pe.wait_ge(wlo_done, 1)
            pe.wait_ge(blo_done, 1)
            hold(pe)
            with pe.Fori(0, NG) as g:
                pe.wait_ge(xhi_done, g + 1)
                pe.wait_ge(xlo_done, g + 1)
                hold(pe)
                for j in range(G):
                    toks = slice(j * T, (j + 1) * T)
                    last = halves(nc, in_ps[:, j, 0:W], [lambda dt: x_hi[:, dt, toks], lambda dt: x_lo[:, dt, toks]],
                                  [lambda dt: w_hi[:, dt, :], lambda dt: w_lo[:, dt, :]], DT)
                last.then_inc(multiplied, 1)
                pe.wait_ge(low_done, g + 1)
                for j in range(G):
                    last = nc.tensor.transpose(lowT_ps[:, j * T:(j + 1) * T], low[:, j, :], ident[:, :])
                last.then_inc(turned, 1)
                pe.wait_ge(low_lo_done, g + 1)
                for j in range(G):
                    toks = slice(j * T, (j + 1) * T)
                    last = halves(nc, delta_ps[:, j, :], [lambda n: low_hi[:, toks], lambda n: low_lo[:, toks]],
                                  [lambda n: b_hi[:, :], lambda n: b_lo[:, :]], 1)
                last.then_inc(delta_done, 1)
                pe.wait_ge(delta_added, g + 1)
                hold(pe)


def stage_context(nc, env, inp):
    with ExitStack() as ctx:
        ctx_in = Mem(nc, ctx).sem("ctx_in")
        block = ctx.enter_context(nc.Block())

        @block.sync
        def _(sp):
            sp.dma_start(env["C"][:, :, :, :].rearrange("p m t b -> p (m t b)"), inp["c0_ctx"]).then_inc(ctx_in, 16)
            sp.wait_ge(ctx_in, 16)
            hold(sp)


def program(nc, inp, out):
    with ExitStack() as ctx:
        m = Mem(nc, ctx)
        env = {
            "X": m.sb("X", [P, B, D]),
            "XTh": m.sb("XTh", [P, DT, B * T], F32R),
            "XTl": m.sb("XTl", [P, DT, B * T], F32R),
            "ident": m.sb("ident", [P, P]),
            "ones": m.sb("ones", [P, P]),
            "minus_half": m.sb("minus_half", [P, 16]),
        }
        with ExitStack() as c0:
            env["OT"] = Mem(nc, c0).sb("OT", [P, B, REP0 * T])
            with ExitStack() as c1:
                a0 = Mem(nc, c1)
                env["Q"] = a0.sb("Q", [P, B, REP0, T])
                env["K"] = a0.sb("K", [P, B * T])
                env["V"] = a0.sb("V", [P, B, P])
                env["sign"] = a0.sb("sign", [P, KV0, 2])
                env["ident_b"] = a0.sb("ident_b", [P, P], BF16)
                env["causal"] = a0.sb("causal", [P, 4, T], BF16)
                env["row_mask"] = a0.sb("row_mask", [P, 2 * KV0])
                stage_attn0_project(nc, env, inp)
                stage_attn0_heads(nc, env, inp)
            stage_attn0_out(nc, env, inp)
        with ExitStack() as c0:
            env["XTf"] = Mem(nc, c0).sb("XTf", [P, DT, B * T])
            stage_norm(nc, env, "ln0", "whole")
            env["C"] = Mem(nc, c0).sb("C", [P, DT, T, B])
            env["Z"] = Mem(nc, c0).sb("Z", [P, DT, B, T])
            stage_context(nc, env, inp)
            stage_conv0(nc, env, inp)
            stage_conv0_out(nc, env)
        stage_norm(nc, env, "ln1", "halves")
        stage_moe0(nc, env, inp)
        stage_norm(nc, env, "ln2", "halves")
        stage_attn1(nc, env, inp)
        with ExitStack() as c1:
            env["XTk"] = Mem(nc, c1).sb("XTk", [P, DT, B, T + 1])
            stage_norm(nc, env, "ln3", "spaced")
            stage_wkv1(nc, env, inp)
        stage_norm(nc, env, "ln4", "halves")
        stage_ffn1(nc, env, inp)
        stage_norm(nc, env, "ln5", None, out=out)


def rope_rows(w, kv, rep):
    import numpy as np
    c = w.reshape(D, kv, rep, 2, DH0)
    partner = c[..., np.arange(DH0) ^ 1]
    tiles = []
    for j in range(rep):
        tiles += [c[:, :, j].reshape(D, P), partner[:, :, j].reshape(D, P)]
    return tiles


def head_rows(w):
    return w.reshape(KV0, REP0, 2 * DH0, -1).swapaxes(0, 1).reshape(w.shape)


def per_head(w):
    return w.reshape(2, D, -1, P).transpose(2, 1, 0, 3)


def kernel(**inputs):
    import numpy as np
    import concourse.bacc as bacc
    from concourse.bass_utils import run_bass_kernel_spmd
    a = {k: np.asarray(v) for k, v in inputs.items()}
    wq = rope_rows(a["L0_attn_Wq"], KV0, REP0)
    wk = rope_rows(a["L0_attn_Wk"], KV0, 1)
    inv = (1.0 / np.float32(10000.0) ** (np.arange(0, DH0, 2, dtype=np.float32) / np.float32(DH0))).astype(np.float32)
    freqs = (np.arange(T, dtype=np.float32)[:, None] * inv[None, :]).astype(np.float32)
    d = np.arange(P) % DH0
    sign = np.where(d % 2 == 0, -1.0, 1.0).astype(np.float32)
    rows = np.arange(P) // (2 * DH0)
    arrays = {
        "x": a["x"],
        "xT": a["x"].reshape(B * T, DT, P).transpose(1, 2, 0),
        "a0_w": np.concatenate(wk + [a["L0_attn_Wv"]] + wq, axis=1).reshape(DT, P, -1),
        "a0_wo": head_rows(a["L0_attn_Wo"]),
        "cos": np.cos(freqs).T[d // 2],
        "sin": np.sin(freqs).T[d // 2] * sign[:, None],
        "row_mask": (np.arange(P)[:, None] // DH0 == np.arange(2 * KV0)).astype(np.float32) * np.float32(DH0 ** -0.5),
        "share": (rows[:, None] == rows[None, :]).astype(np.float32) / np.float32(2 * DH0),
        "lambdas": np.concatenate([a[f"L0_attn_lambda_{n}"] for n in ("q1", "k1", "q2", "k2")]),
        "gn_w": head_rows(a["L0_attn_gn_w"]).reshape(-1, P).T,
        "gn_b": head_rows(a["L0_attn_gn_b"]).reshape(-1, P).T,
        "ident": np.eye(P, dtype=np.float32),
        "anti": np.eye(P, dtype=np.float32)[::-1],
        "c0_ctx": a["ctx_2048"].reshape(B, T, DT, P)[..., ::-1].transpose(3, 2, 1, 0).reshape(P, -1),
        "c0_D": a["L0_xattn_D"],
        "m0_router": np.pad(a["L0_ffn_router_logits"], ((0, 0), (0, P - 8))),
        "m0_router_scale": a["L0_ffn_router_scale"].reshape(DT, P).T,
        "m0_rank": np.arange(8, 0, -1).astype(np.float32),
        "m0_per_expert": a["L0_ffn_per_expert_scale"],
        "a1_w": np.stack([per_head(np.stack([a[f"L1_attn_w{n}_codes"], a[f"L1_attn_w{n}_scales"].repeat(32, axis=0)]))
                          for n in "qk"], axis=3).reshape(16, D, 2 * 2 * P),
        "a1_wv": np.stack([a["L1_attn_wv_codes"], a["L1_attn_wv_scales"].repeat(32, axis=0)])
                   .reshape(2, D, 8, 2 * P).transpose(2, 1, 0, 3).reshape(8, D, 2 * 2 * P),
        "a1_bias": np.stack([a[f"L1_attn_b{n}"].reshape(16, P) for n in "qkv"], axis=2),
        "a1_wo": np.stack([a["L1_attn_wo_codes"], a["L1_attn_wo_scales"].repeat(32, axis=0)], axis=1).reshape(16, P, 2 * D),
        "a1_bo": a["L1_attn_bo"],
        "m0_w": np.concatenate([a["L0_ffn_gating_einsum"].transpose(0, 3, 1, 2).reshape(8, D, 2 * D),
                                a["L0_ffn_linear"]], axis=2),
        "ctxT": a["ctx_2048"].reshape(B * T, DT, P).transpose(1, 2, 0),
        "k1_decay": a["L1_xattn_time_decay"].reshape(DT, P).T,
        "k1_first": a["L1_xattn_time_first"].reshape(DT, P).T,
        "f1_w": np.concatenate([a["L1_ffn_W_base"].T, a["L1_ffn_router_W"].T,
                                a["L1_ffn_A"].reshape(8 * 16, D).T], axis=1),
        "f1_b": a["L1_ffn_Bw"].transpose(0, 2, 1).reshape(8 * 16, D),
        "f1_bias": a["L1_ffn_b_base"],
        "toeplitz": np.pad(a["L0_xattn_ssm_kernel"], ((0, 0), (P - 1, 0)))[:, np.arange(P)[:, None] + np.arange(D)],
    }
    arrays = {k: np.ascontiguousarray(v) for k, v in arrays.items()}
    nc = bacc.Bacc("TRN2", target_bir_lowering=False, num_devices=1)
    inp = {k: nc.dram_tensor(f"in_{k}", v.shape, mybir.dt.from_np(v.dtype), kind="ExternalInput").ap() for k, v in arrays.items()}
    out = nc.dram_tensor("out", (B, T, D), F32, kind="ExternalOutput").ap()
    program(nc, inp, out)
    r = run_bass_kernel_spmd(nc, [{f"in_{k}": v for k, v in arrays.items()}], core_ids=[0])
    return r.results[0]["out"]
```

```python
import math
from contextlib import ExitStack

import concourse.bass as bass
from concourse import mybir
from concourse.alu_op_type import AluOpType as ALU

F32 = mybir.dt.float32
F32R = mybir.dt.float32r
BF16 = mybir.dt.bfloat16
ACT = mybir.ActivationFunctionType
AX_X = mybir.AxisListType.X

P = 128
B = 16
T = 128
D = 256
DT = D // P
G = 4
NG = B // G
GT = G * T
BANK = 512
LN_EPS = 1e-5

H0, KV0, DH0 = 16, 4, 16
REP0 = H0 // KV0
LAMBDA_INIT = 0.8 - 0.6 * math.exp(-0.3 * 0)


def one(ap_3d, i):
    return ap_3d[:, bass.ds(i, 1), :].rearrange("p o n -> p (o n)")


def batch(ap_4d, i, b):
    if isinstance(i, int):
        return ap_4d[:, 2 * i + b, :, :]
    return ap_4d[:, bass.ds(i * 2 + b, 1), :, :].rearrange("p o j t -> p (o j) t")


def flat_batch(ap_3d, i, b):
    return ap_3d[:, 2 * i + b, :] if isinstance(i, int) else one(ap_3d, i * 2 + b)


def hold(eng):
    eng.nop(nofuse=True)


class Mem:

    def __init__(self, nc, ctx):
        self.nc, self.ctx, self.sems = nc, ctx, []

    def recycle(self):
        self.nc.clear_and_free_semaphores(self.sems)
        self.nc.all_engine_barrier()

    def sb(self, name, shape, dt=F32):
        return self.ctx.enter_context(self.nc.sbuf_tensor(name, shape, dt))

    def ps(self, name, shape, dt=F32):
        return self.ctx.enter_context(self.nc.psum_tensor(name, shape, dt))

    def sem(self, name):
        if not self.sems:
            self.ctx.callback(self.recycle)
        self.sems.append(self.nc.alloc_semaphore(name=name))
        return self.sems[-1]


def stage_norm(nc, env, tag, turn=None, out=None, loads=()):
    X, XTh, XTl, ident = env["X"], env["XTh"], env["XTl"], env["ident"]
    split = turn == "halves"
    with ExitStack() as ctx:
        m = Mem(nc, ctx)
        stats = m.sb(f"{tag}_stats", [P, B, 6])
        moments = m.sb(f"{tag}_moments", [P, B, 2])
        var_eps = m.sb(f"{tag}_var_eps", [P, B])
        rstd = m.sb(f"{tag}_rstd", [P, B])
        scaled = m.sb(f"{tag}_scaled", [P, B])
        shift = m.sb(f"{tag}_shift", [P, B])
        xT_ps = [m.ps(f"{tag}_xT_ps{i}", [P, DT, GT]) for i in range(2)]
        stats_done = m.sem(f"{tag}_stats_done")
        moments_done = m.sem(f"{tag}_moments_done")
        eps_done = m.sem(f"{tag}_eps_done")
        rstd_done = m.sem(f"{tag}_rstd_done")
        shift_done = m.sem(f"{tag}_shift_done")
        normed_dve = m.sem(f"{tag}_normed_dve")
        normed_act = m.sem(f"{tag}_normed_act")
        turned = m.sem(f"{tag}_turned")
        hi_done = m.sem(f"{tag}_hi_done")
        lo_done = m.sem(f"{tag}_lo_done")
        out_done = m.sem(f"{tag}_out_done")
        loaded = m.sem(f"{tag}_loaded")
        block = ctx.enter_context(nc.Block())
        half = G // 2

        @block.vector
        def _(dve):
            def normalise(g):
                dve.wait_ge(rstd_done, g + 1)
                for b in range(g * G, g * G + half):
                    last = nc.vector.tensor_scalar(X[:, b, :], X[:, b, :], moments[:, b, 0:1], rstd[:, b:b + 1],
                                                   ALU.subtract, ALU.mult)
                last.then_inc(normed_dve, 1)

            def low(g):
                for dt in range(DT):
                    cols = slice(g * GT, (g + 1) * GT)
                    dve.wait_ge(hi_done, g * DT + (dt + 1))
                    nc.vector.tensor_tensor(XTl[:, dt, cols], xT_ps[g % 2][:, dt, :],
                                            XTh[:, dt, cols].bitcast(F32), ALU.subtract).then_inc(lo_done, 1)

            for g in range(NG):
                for b in range(g * G, (g + 1) * G):
                    nc.vector.bn_stats(stats[:, b, :], X[:, b, :]).then_inc(stats_done, 1)
                for b in range(g * G, (g + 1) * G):
                    dve.wait_ge(stats_done, b + 1)
                    nc.vector.bn_aggr(moments[:, b, :], stats[:, b, :]).then_inc(moments_done, 1)
                if g >= 1:
                    normalise(g - 1)
                if g >= 2 and split:
                    low(g - 2)
            if split:
                low(NG - 2)
            normalise(NG - 1)
            if split:
                low(NG - 1)

        @block.gpsimd
        def _(pool):
            for g in range(NG):
                bs = slice(g * G, (g + 1) * G)
                pool.wait_ge(moments_done, g * G + G)
                nc.gpsimd.tensor_scalar(var_eps[:, bs], moments[:, bs, 1], 1.0, LN_EPS, ALU.mult, ALU.add).then_inc(eps_done, 1)
                pool.wait_ge(eps_done, 2 * g + 1)
                nc.gpsimd.tensor_tensor(rstd[:, bs], var_eps[:, bs], env["minus_half"][:, 0:G], ALU.pow).then_inc(rstd_done, 1)
                pool.wait_ge(rstd_done, g + 1)
                nc.gpsimd.tensor_tensor(scaled[:, bs], moments[:, bs, 0], rstd[:, bs], ALU.mult).then_inc(eps_done, 1)
                pool.wait_ge(eps_done, 2 * g + 2)
                nc.gpsimd.tensor_scalar(shift[:, bs], scaled[:, bs], -1.0, None, ALU.mult).then_inc(shift_done, 1)

        @block.scalar
        def _(act):
            for g in range(NG + 1):
                if g < NG:
                    act.wait_ge(shift_done, g + 1)
                    for b in range(g * G + half, (g + 1) * G):
                        last = nc.scalar.activation(X[:, b, :], X[:, b, :], ACT.Identity, scale=rstd[:, b:b + 1],
                                                    bias=shift[:, b:b + 1])
                    last.then_inc(normed_act, 1)
                if g >= 1 and turn is not None:
                    act.wait_ge(turned, g)
                    for dt in range(DT):
                        src = xT_ps[(g - 1) % 2][:, dt, :]
                        if turn == "spaced":
                            src = src.rearrange("p (b t) -> p b t", b=G)
                            dst = env["XTk"][:, dt, (g - 1) * G:g * G, 1:T + 1]
                        else:
                            dst = (XTh if split else env["XTf"])[:, dt, (g - 1) * GT:g * GT]
                        nc.scalar.activation(dst, src, ACT.Copy).then_inc(hi_done, 1)

        if turn is not None:
            @block.tensor
            def _(pe):
                for g in range(NG):
                    pe.wait_ge(normed_dve, g + 1)
                    pe.wait_ge(normed_act, g + 1)
                    if g >= 2:
                        pe.wait_ge(lo_done if split else hi_done, (g - 1) * DT)
                    for dt in range(DT):
                        for j in range(G):
                            last = nc.tensor.transpose(xT_ps[g % 2][:, dt, j * T:(j + 1) * T],
                                                       X[:, g * G + j, dt * P:(dt + 1) * P], ident[:, :])
                    last.then_inc(turned, 1)

        if loads:
            @block.sync
            def _(sp):
                for dst, src in loads:
                    sp.dma_start(dst, src).then_inc(loaded, 16)
                sp.wait_ge(loaded, 16 * len(loads))

        if out is not None:
            @block.sync
            def _(sp):
                for g in range(NG):
                    sp.wait_ge(normed_dve, g + 1)
                    sp.wait_ge(normed_act, g + 1)
                    sp.dma_start(out[g * G:(g + 1) * G, :, :].rearrange("b t d -> t b d"), X[:, g * G:(g + 1) * G, :])\
                        .then_inc(out_done, 16)
                sp.wait_ge(out_done, 16 * NG)


def halves(nc, out, lhs, rhs, tiles):
    terms = [(lhs[i], rhs[k], n) for n in range(tiles) for i, k in ((0, 0), (0, 1), (1, 0))]
    for at, (lh, rh, n) in enumerate(terms):
        last = nc.tensor.matmul(out, lh(n), rh(n), start=(at == 0), stop=(at == len(terms) - 1))
    return last


def stage_attn0_project(nc, env, inp):
    X, XTh, XTl, Q, K, V = (env[n] for n in ("X", "XTh", "XTl", "Q", "K", "V"))
    NT = REP0
    NPAIR = NT + 1
    first, rest = slice(0, GT), slice(GT, B * T)
    with ExitStack() as ctx:
        m = Mem(nc, ctx)
        x_raw = m.sb("p0_x_raw", [P, DT, B * T])
        w_raw = m.sb("p0_w_raw", [P, DT, NPAIR * 2 * P + P])
        w_hi = m.sb("p0_w_hi", [P, DT, NPAIR * 2 * P + P], F32R)
        w_lo = m.sb("p0_w_lo", [P, DT, NPAIR * 2 * P + P], F32R)
        cos = m.sb("p0_cos", [P, T])
        sin = m.sb("p0_sin", [P, T])
        lam_in = m.sb("p0_lam_in", [P, 4, DH0])
        lam_prod = m.sb("p0_lam_prod", [P, 2, DH0])
        lam_sum = m.sb("p0_lam_sum", [P, 2])
        lam_exp = m.sb("p0_lam_exp", [P, 2])
        lam_dif = m.sb("p0_lam_dif", [P, 1])
        r_cos = m.sb("p0_r_cos", [P, 3, GT])
        r_sin = m.sb("p0_r_sin", [P, 3, GT])
        vT = m.sb("p0_vT", [P, GT])
        proj_ps = [[m.ps(f"p0_proj_ps{i}{k}", [P, BANK]) for k in range(2)] for i in range(3)]
        vT_ps = m.ps("p0_vT_ps", [P, BANK])
        v_ps = m.ps("p0_v_ps", [P, BANK])
        w_in = [m.sem(f"p0_w_in{i}") for i in range(NPAIR)]
        x_in = [m.sem(f"p0_x_in{i}") for i in range(2)]
        const_in = m.sem("p0_const_in")
        X_in = m.sem("p0_X_in")
        ident_in = m.sem("p0_ident_in")
        whi_done = m.sem("p0_whi_done")
        wlo_done = m.sem("p0_wlo_done")
        xhi_done = m.sem("p0_xhi_done")
        xlo_done = m.sem("p0_xlo_done")
        lam = m.sem("p0_lam")
        lam_exped = m.sem("p0_lam_exped")
        const = m.sem("p0_const")
        projected = m.sem("p0_projected")
        v_projected = m.sem("p0_v_projected")
        vT_done = m.sem("p0_vT_done")
        v_turned = m.sem("p0_v_turned")
        v_done = m.sem("p0_v_done")
        roped = m.sem("p0_roped")
        added = m.sem("p0_added")
        block = ctx.enter_context(nc.Block())

        def columns(n):
            return slice(0, 3 * P) if n == 0 else slice((2 * n + 1) * P, (2 * n + 3) * P)

        @block.sync
        def _(sp):
            x_src = inp["xT"].rearrange("k p n -> p k n")
            w_src = inp["a0_w"].rearrange("k p n -> p k n")
            sp.dma_start(w_raw[:, :, columns(0)], w_src[:, :, columns(0)]).then_inc(w_in[0], 16)
            sp.dma_start(x_raw[:, :, first], x_src[:, :, first]).then_inc(x_in[0], 16)
            sp.dma_start(w_raw[:, :, columns(1)], w_src[:, :, columns(1)]).then_inc(w_in[1], 16)
            sp.dma_start(cos[:, :], inp["cos"]).then_inc(const_in, 16)
            sp.dma_start(sin[:, :], inp["sin"]).then_inc(const_in, 16)
            sp.dma_start(lam_in[:, :, :].rearrange("p a d -> p (a d)"),
                         inp["lambdas"].partition_broadcast(P)).then_inc(const_in, 16)
            sp.dma_start(env["ident"][:, :], inp["ident"]).then_inc(ident_in, 16)
            for n in range(2, NPAIR):
                sp.dma_start(w_raw[:, :, columns(n)], w_src[:, :, columns(n)]).then_inc(w_in[n], 16)
            sp.dma_start(x_raw[:, :, rest], x_src[:, :, rest]).then_inc(x_in[1], 16)
            sp.dma_start(env["row_mask"][:, :], inp["row_mask"]).then_inc(X_in, 16)
            sp.dma_start(X[:, :, :], inp["x"].rearrange("b t d -> t b d")).then_inc(X_in, 16)
            sp.wait_ge(X_in, 32)

        @block.gpsimd
        def _(pool):
            causal, ident_b = env["causal"], env["ident_b"]
            nc.gpsimd.memset(env["minus_half"][:, :], -0.5).then_inc(const, 1)
            nc.gpsimd.memset(env["ones"][:, :], 1.0).then_inc(const, 1)
            nc.gpsimd.memset(causal[:, :, :], 0.0).then_inc(const, 1)
            nc.gpsimd.memset(ident_b[:, :], 0.0).then_inc(const, 1)
            pool.wait_ge(const, 4)
            nc.gpsimd.affine_select(out=causal[:, :, :], in_=causal[:, :, :], compare_op=ALU.is_ge, fill=-1e38,
                                    base=0, pattern=[[0, 4], [-1, T]], channel_multiplier=1).then_inc(const, 1)
            nc.gpsimd.affine_select(out=ident_b[:, :], in_=ident_b[:, :], compare_op=ALU.not_equal, fill=1.0,
                                    base=0, pattern=[[-1, P]], channel_multiplier=1).then_inc(const, 1)
            pool.sem_inc(added, 2)
            with pool.Fori(0, NG) as g:
                for n in range(NPAIR):
                    pool.wait_ge(roped, g * NPAIR + (n + 1))
                    hold(pool)
                    if n == 0:
                        nc.gpsimd.tensor_tensor(K[:, bass.ds(g * GT, GT)], r_cos[:, n % 3, :], r_sin[:, n % 3, :], ALU.add)\
                            .then_inc(added, 1)
                    else:
                        nc.gpsimd.tensor_tensor(Q[:, bass.ds(g * G, G), n - 1, :],
                                                r_cos[:, n % 3, :].rearrange("p (b t) -> p b t", b=G),
                                                r_sin[:, n % 3, :].rearrange("p (b t) -> p b t", b=G), ALU.add)\
                            .then_inc(added, 1)

        @block.scalar
        def _(act):
            def w_high(n):
                act.wait_ge(w_in[n], 16)
                nc.scalar.activation(w_hi[:, :, columns(n)], w_raw[:, :, columns(n)], ACT.Copy).then_inc(whi_done, 1)

            def x_high(n, toks):
                act.wait_ge(x_in[n], 16)
                nc.scalar.activation(XTh[:, :, toks], x_raw[:, :, toks], ACT.Copy).then_inc(xhi_done, 1)

            w_high(0)
            x_high(0, first)
            for n in range(1, NPAIR):
                w_high(n)
            x_high(1, rest)
            with act.Fori(0, NG) as g:
                act.wait_ge(v_projected, g + 1)
                nc.scalar.activation(vT[:, :], vT_ps[:, :], ACT.Copy).then_inc(vT_done, 1)
                act.wait_ge(v_turned, g + 1)
                hold(act)
                nc.scalar.activation(V[:, bass.ds(g * G, G), :], v_ps[:, :].rearrange("p (b c) -> p b c", b=G), ACT.Copy)\
                    .then_inc(v_done, 1)
            act.wait_ge(lam, 2)
            nc.scalar.activation(lam_exp[:, :], lam_sum[:, :], ACT.Exp).then_inc(lam_exped, 1)

        @block.vector
        def _(dve):
            def w_low(n):
                dve.wait_ge(whi_done, n + 1)
                nc.vector.tensor_tensor(w_lo[:, :, columns(n)], w_raw[:, :, columns(n)],
                                        w_hi[:, :, columns(n)].bitcast(F32), ALU.subtract).then_inc(wlo_done, 1)

            def x_low(n, toks):
                dve.wait_ge(xhi_done, n + 1)
                nc.vector.tensor_tensor(XTl[:, :, toks], x_raw[:, :, toks], XTh[:, :, toks].bitcast(F32),
                                        ALU.subtract).then_inc(xlo_done, 1)

            def rotate(g, n):
                dve.wait_ge(projected, g * NPAIR + (n + 1))
                dve.wait_ge(added, g * NPAIR + (n + 1))
                v3 = "p (b t) -> p b t"
                for dst, src, table in ((r_cos, proj_ps[n % 3][0], cos), (r_sin, proj_ps[n % 3][1], sin)):
                    last = nc.vector.tensor_tensor(dst[:, n % 3, :].rearrange(v3, b=G), src[:, :].rearrange(v3, b=G),
                                                   table[:, :].unsqueeze(1).broadcast_to([P, G, T]), ALU.mult)
                last.then_inc(roped, 1)

            w_low(0)
            x_low(0, first)
            dve.wait_ge(const_in, 48)
            for n in range(NPAIR):
                if n + 1 < NPAIR:
                    w_low(n + 1)
                rotate(0, n)
            x_low(1, rest)
            sign = env["sign"]
            nc.vector.tensor_tensor(lam_prod[:, :, :], lam_in[:, 0:4:2, :], lam_in[:, 1:4:2, :], ALU.mult).then_inc(lam, 1)
            dve.wait_ge(lam, 1)
            nc.vector.tensor_reduce(lam_sum[:, :], lam_prod[:, :, :], AX_X, ALU.add).then_inc(lam, 1)
            with dve.Fori(1, NG) as g:
                for n in range(NPAIR):
                    rotate(g, n)
            dve.wait_ge(lam_exped, 1)
            nc.vector.memset(sign[:, :, 0:1], 1.0).then_inc(lam, 1)
            nc.vector.tensor_tensor(lam_dif[:, :], lam_exp[:, 1:2], lam_exp[:, 0:1], ALU.subtract).then_inc(lam, 1)
            dve.wait_ge(lam, 4)
            nc.vector.tensor_scalar(sign[:, :, 1], lam_dif[:, 0:1].broadcast_to([P, KV0]), 1.0, -LAMBDA_INIT,
                                    ALU.mult, ALU.add).then_inc(lam, 1)

        @block.tensor
        def _(pe):
            w_halves = [lambda c: lambda dt: w_hi[:, dt, c], lambda c: lambda dt: w_lo[:, dt, c]]

            def project(g):
                toks = first if isinstance(g, int) else bass.ds(g * GT, GT)
                x_halves = [lambda dt: XTh[:, dt, toks], lambda dt: XTl[:, dt, toks]]
                for n in range(NPAIR):
                    if isinstance(g, int):
                        pe.wait_ge(wlo_done, n + 1)
                    if n >= 2 or not isinstance(g, int):
                        pe.wait_ge(roped, g * NPAIR + (n - 1))
                    at = 0 if n == 0 else 2 * n + 1
                    for pr in range(2):
                        c = slice((at + pr) * P, (at + pr + 1) * P)
                        last = halves(nc, proj_ps[n % 3][pr][:, :], [w(c) for w in w_halves], x_halves, DT)
                    last.then_inc(projected, 1)
                    if n == 0:
                        c = slice(2 * P, 3 * P)
                        halves(nc, vT_ps[:, :], [w(c) for w in w_halves], x_halves, DT).then_inc(v_projected, 1)
                    if n == 1:
                        pe.wait_ge(vT_done, g + 1)
                        if isinstance(g, int):
                            pe.wait_ge(ident_in, 16)
                        else:
                            pe.wait_ge(v_done, g)
                        for b in range(G):
                            last = nc.tensor.transpose(v_ps[:, b * T:(b + 1) * T], vT[:, b * T:(b + 1) * T],
                                                       env["ident"][:, :])
                        last.then_inc(v_turned, 1)

            pe.wait_ge(xlo_done, 1)
            project(0)
            pe.wait_ge(xlo_done, 2)
            hold(pe)
            with pe.Fori(1, NG) as g:
                project(g)


def stage_attn0_heads(nc, env, inp):
    Q, K, V, OT, ident = env["Q"], env["K"], env["V"], env["OT"], env["ident"]
    causal, ident_b, sign, row_mask = env["causal"], env["ident_b"], env["sign"], env["row_mask"]
    N = B * REP0
    BODY = 2 * REP0
    FIRST = BODY + 2
    TURNS = (N - FIRST) // BODY
    R = 2 * KV0
    VW = 2 * DH0
    with ExitStack() as ctx:
        m = Mem(nc, ctx)
        q_hi = m.sb("a0_q_hi", [P, 2, REP0, T], F32R)
        q_lo = m.sb("a0_q_lo", [P, 2, REP0, T], F32R)
        k_hi = m.sb("a0_k_hi", [P, 2, T], F32R)
        k_lo = m.sb("a0_k_lo", [P, 2, T], F32R)
        kz_hi = m.sb("a0_kz_hi", [P, 2, R, T], F32R)
        kz_lo = m.sb("a0_kz_lo", [P, 2, R, T], F32R)
        v = m.sb("a0_v", [P, 2, P])
        negmax = m.sb("a0_negmax", [P, 2, R])
        sums = m.sb("a0_sums", [P, 2, R])
        recip = m.sb("a0_recip", [P, 2, R])
        factor = m.sb("a0_factor", [P, 2, KV0, 2])
        probs = m.sb("a0_probs", [P, 4, KV0, 2, T])
        second = m.sb("a0_second", [P, 2, KV0, T])
        diff = m.sb("a0_diff", [P, 2, KV0, T])
        diffT = m.sb("a0_diffT", [P, 2, KV0, REP0, T])
        s_ps = [m.ps(f"a0_s_ps{i}", [P, 2 * BANK]) for i in range(2)]
        dT_ps = [m.ps(f"a0_dT_ps{i}", [P, BANK]) for i in range(2)]
        oT_ps = m.ps("a0_oT_ps", [P, BANK])
        next_in = m.sem("a0_next_in")
        khi_done = m.sem("a0_khi_done")
        klo_done = m.sem("a0_klo_done")
        qhi_done = m.sem("a0_qhi_done")
        qlo_done = m.sem("a0_qlo_done")
        kz_done = m.sem("a0_kz_done")
        v_done = m.sem("a0_v_done")
        scored = m.sem("a0_scored")
        maxed = m.sem("a0_maxed")
        exped = m.sem("a0_exped")
        recip_done = m.sem("a0_recip_done")
        factor_done = m.sem("a0_factor_done")
        second_done = m.sem("a0_second_done")
        diff_done = m.sem("a0_diff_done")
        turned = m.sem("a0_turned")
        dT_done = m.sem("a0_dT_done")
        pv_done = m.sem("a0_pv_done")
        oT_done = m.sem("a0_oT_done")
        block = ctx.enter_context(nc.Block())

        def run(eng, step):
            for k in range(FIRST):
                step(0, k)
            with eng.Fori(0, TURNS) as i:
                for k in range(FIRST, FIRST + BODY):
                    step(i, k)
            for k in range(FIRST, N + 6 - TURNS * BODY):
                step(TURNS, k)

        def inside(i, k):
            return not isinstance(i, int) or 0 <= i * BODY + k < N

        def early(i, k, n):
            return isinstance(i, int) and i * BODY + k < n

        @block.sync
        def _(sp):
            sp.dma_start(env["wo_raw"][:, :, :], inp["a0_wo"].rearrange("(k p) n -> p k n", p=P)).then_inc(next_in, 16)
            sp.dma_start(env["gn_w"][:, :], inp["gn_w"]).then_inc(next_in, 16)
            sp.dma_start(env["gn_b"][:, :], inp["gn_b"]).then_inc(next_in, 16)
            sp.dma_start(env["share"][:, :], inp["share"]).then_inc(next_in, 16)
            sp.wait_ge(next_in, 64)

        @block.gpsimd
        def _(pool):
            def mask_keys(i, k, half):
                src, dst, ready = ((k_hi, kz_hi, khi_done), (k_lo, kz_lo, klo_done))[half]
                p = (k // REP0 + 1) % 2
                pool.wait_ge(ready, i * 2 + (k // REP0 + 2))
                if not early(i, k, REP0):
                    pool.wait_ge(scored, i * BODY + k // REP0 * REP0)
                nc.gpsimd.tensor_tensor(dst[:, p, :, :], src[:, p, :].bitcast(F32).unsqueeze(1).broadcast_to([P, R, T]),
                                        row_mask[:, :].unsqueeze(2).broadcast_to([P, R, T]), ALU.mult).then_inc(kz_done, 1)

            def low_queries(i, k):
                b = k // REP0 + 1
                pool.wait_ge(qhi_done, i * 2 + (b + 1))
                hold(pool)
                nc.gpsimd.tensor_tensor(q_lo[:, b % 2, :, :], batch(Q, i, b), q_hi[:, b % 2, :, :].bitcast(F32),
                                        ALU.subtract).then_inc(qlo_done, 1)

            def step(i, k):
                if inside(i, k - 1):
                    pool.wait_ge(factor_done, i * BODY + k)
                    nc.gpsimd.tensor_tensor(second[:, (k - 1) % 2, :, :], probs[:, (k - 1) % 4, :, 1, :],
                                            factor[:, (k - 1) % 2, :, 1:2].broadcast_to([P, KV0, T]), ALU.mult)\
                        .then_inc(second_done, 1)
                if k % REP0 < 2 and inside(i, k // REP0 * REP0 + REP0):
                    mask_keys(i, k, k % REP0)
                if k % REP0 == 2 and inside(i, k - 2 + REP0):
                    low_queries(i, k - 2)

            mask_keys(0, -REP0, 0)
            mask_keys(0, -REP0, 1)
            low_queries(0, -REP0)
            run(pool, step)

        @block.scalar
        def _(act):
            def high_halves(i, k):
                b, p = k // REP0 + 1, (k // REP0 + 1) % 2
                if not early(i, k, REP0):
                    act.wait_ge(scored, i * BODY + k)
                hold(act)
                toks = bass.ds(i * (2 * T) + b * T, T) if not isinstance(i, int) else slice((2 * i + b) * T, (2 * i + b + 1) * T)
                nc.scalar.activation(k_hi[:, p, :], K[:, toks], ACT.Copy).then_inc(khi_done, 1)
                nc.scalar.activation(q_hi[:, p, :, :], batch(Q, i, b), ACT.Copy).then_inc(qhi_done, 1)

            def step(i, k):
                if k % REP0 == 0 and inside(i, k + REP0):
                    high_halves(i, k)
                if inside(i, k):
                    act.wait_ge(maxed, i * BODY + (k + 1))
                    for r in range(R):
                        nc.scalar.activation(probs[:, k % 4, r // 2, r % 2, :], s_ps[k % 2][:, r * T:(r + 1) * T],
                                             ACT.Exp, bias=negmax[:, k % 2, r:r + 1],
                                             accum_out=sums[:, k % 2, r:r + 1]).then_inc(exped, 1)
                if k % REP0 == 0 and inside(i, k - REP0):
                    b = k // REP0 - 1
                    if not early(i, k, 3 * REP0):
                        act.wait_ge(pv_done, i * 2 + (b - 1))
                        hold(act)
                    nc.scalar.activation(v[:, b % 2, :], flat_batch(V, i, b), ACT.Copy).then_inc(v_done, 1)
                if k % REP0 == 1 and inside(i, k - 9):
                    b = (k - 9) // REP0
                    act.wait_ge(pv_done, i * 2 + (b + 1))
                    hold(act)
                    nc.scalar.activation(flat_batch(OT, i, b), oT_ps[:, :], ACT.Copy).then_inc(oT_done, 1)

            high_halves(0, -REP0)
            run(act, step)

        @block.vector
        def _(dve):
            def low_halves(i, k):
                b, p = k // REP0 + 1, (k // REP0 + 1) % 2
                toks = bass.ds(i * (2 * T) + b * T, T) if not isinstance(i, int) else slice((2 * i + b) * T, (2 * i + b + 1) * T)
                dve.wait_ge(khi_done, i * 2 + (b + 1))
                hold(dve)
                nc.vector.tensor_tensor(k_lo[:, p, :], K[:, toks], k_hi[:, p, :].bitcast(F32), ALU.subtract)\
                    .then_inc(klo_done, 1)

            def step(i, k):
                if inside(i, k):
                    dve.wait_ge(scored, i * BODY + (k + 1))
                    nc.vector.tensor_reduce(negmax[:, k % 2, :], s_ps[k % 2][:, :].rearrange("p (r s) -> p r s", r=R),
                                            AX_X, ALU.max, negate=True).then_inc(maxed, 1)
                if inside(i, k - 4):
                    u = k - 4
                    dve.wait_ge(turned, i * BODY + (u + 1))
                    nc.vector.tensor_copy(diffT[:, u // REP0 % 2, :, u % REP0, :],
                                          dT_ps[u % 2][:, :].rearrange("p (k t) -> p k t", k=KV0)).then_inc(dT_done, 1)
                if k % REP0 == 0 and inside(i, k + REP0):
                    low_halves(i, k)
                if inside(i, k - 1):
                    p = (k - 1) % 2
                    dve.wait_ge(exped, i * (R * BODY) + R * k)
                    nc.vector.reciprocal(recip[:, p, :], sums[:, p, :]).then_inc(recip_done, 1)
                    dve.wait_ge(recip_done, i * BODY + k)
                    nc.vector.tensor_tensor(factor[:, p, :, :].rearrange("p k h -> p (k h)"), recip[:, p, :],
                                            sign[:, :, :].rearrange("p k h -> p (k h)"), ALU.mult).then_inc(factor_done, 1)
                if inside(i, k - 2):
                    u = k - 2
                    dve.wait_ge(second_done, i * BODY + (u + 1))
                    if not early(i, u, 2):
                        dve.wait_ge(turned, i * BODY + (u - 1))
                    for kv in range(KV0):
                        last = nc.vector.scalar_tensor_tensor(diff[:, u % 2, kv, :], probs[:, u % 4, kv, 0, :],
                                                              factor[:, u % 2, kv, 0:1], second[:, u % 2, kv, :],
                                                              ALU.mult, ALU.add)
                    last.then_inc(diff_done, 1)

            low_halves(0, -REP0)
            run(dve, step)

        @block.tensor
        def _(pe):
            def step(i, k):
                if inside(i, k):
                    p, j = k // REP0 % 2, k % REP0
                    if j == 0:
                        pe.wait_ge(kz_done, i * 4 + (2 * (k // REP0) + 2))
                        pe.wait_ge(qlo_done, i * 2 + (k // REP0 + 1))
                    if not early(i, k, 2):
                        pe.wait_ge(exped, i * (R * BODY) + R * (k - 1))
                    for h in range(2):
                        bank = s_ps[k % 2][:, h * BANK:(h + 1) * BANK]
                        nc.tensor.matmul(bank, ident_b[:, :], causal[:, :, :].rearrange("p a s -> p (a s)"),
                                         start=True, stop=False)
                        for q, kz in ((q_hi, kz_hi), (q_hi, kz_lo), (q_lo, kz_hi)):
                            last = nc.tensor.matmul(bank, q[:, p, j, :],
                                                    kz[:, p, 4 * h:4 * h + 4, :].rearrange("p r s -> p (r s)"),
                                                    start=False, stop=q is q_lo)
                    last.then_inc(scored, 1)
                if inside(i, k - 3):
                    u = k - 3
                    if not early(i, u, 2):
                        pe.wait_ge(dT_done, i * BODY + (u - 1))
                    pe.wait_ge(diff_done, i * BODY + (u + 1))
                    for kv in range(KV0):
                        last = nc.tensor.transpose(dT_ps[u % 2][:, kv * T:(kv + 1) * T], diff[:, u % 2, kv, :], ident[:, :])
                    last.then_inc(turned, 1)
                if k % REP0 == 0 and inside(i, k - 2 * REP0):
                    b = k // REP0 - 2
                    pe.wait_ge(dT_done, i * BODY + (REP0 * b + REP0))
                    pe.wait_ge(v_done, i * 2 + (b + 1))
                    if not early(i, b * REP0, REP0):
                        pe.wait_ge(oT_done, i * 2 + b)
                    for kv in range(KV0):
                        last = nc.tensor.matmul(oT_ps[kv * VW:(kv + 1) * VW, :], v[:, b % 2, kv * VW:(kv + 1) * VW],
                                                diffT[:, b % 2, kv, :, :].rearrange("p j t -> p (j t)"),
                                                start=True, stop=True)
                    last.then_inc(pv_done, 1)

            run(pe, step)


def stage_attn0_out(nc, env, inp):
    X, OT = env["X"], env["OT"]
    NJ = REP0
    N = B // 2
    BODY, FIRST = 2, 2
    TURNS = (N - FIRST - 1) // BODY
    with ExitStack() as ctx:
        m = Mem(nc, ctx)
        wo_raw, gn_w, gn_b, share = (env[n] for n in ("wo_raw", "gn_w", "gn_b", "share"))
        wo_b = m.sb("n0_wo_b", [P, NJ, D])
        wo = m.sb("n0_wo", [P, NJ, D])
        bias = m.sb("n0_bias", [P, D])
        stats = m.sb("n0_stats", [P, 2, 2, NJ, 6])
        moments = m.sb("n0_moments", [P, 2, 2, NJ, 2])
        square = m.sb("n0_square", [P, 2, 2, NJ])
        avg = m.sb("n0_avg", [P, 2, 2, NJ, 2])
        avg2 = m.sb("n0_avg2", [P, 2, 2, NJ])
        var = m.sb("n0_var", [P, 2, 2, NJ])
        rstd = m.sb("n0_rstd", [P, 2, 2, NJ])
        scaled = m.sb("n0_scaled", [P, 2, 2, NJ])
        shift = m.sb("n0_shift", [P, 2, 2, NJ])
        yT = m.sb("n0_yT", [P, 2, 2, NJ, T])
        avg_ps = [m.ps(f"n0_avg_ps{i}", [P, BANK]) for i in range(2)]
        out_ps = [m.ps(f"n0_out_ps{i}", [P, BANK]) for i in range(2)]
        bias_ps = m.ps("n0_bias_ps", [P, BANK])
        wb_done = m.sem("n0_wb_done")
        wo_done = m.sem("n0_wo_done")
        bias_ready = m.sem("n0_bias_ready")
        bias_done = m.sem("n0_bias_done")
        bias_added = m.sem("n0_bias_added")
        stats_done = m.sem("n0_stats_done")
        moments_done = m.sem("n0_moments_done")
        squared = m.sem("n0_squared")
        power_done = m.sem("n0_power_done")
        averaged = m.sem("n0_averaged")
        avg_done = m.sem("n0_avg_done")
        avg2_done = m.sem("n0_avg2_done")
        var_done = m.sem("n0_var_done")
        rstd_done = m.sem("n0_rstd_done")
        scaled_done = m.sem("n0_scaled_done")
        shift_done = m.sem("n0_shift_done")
        y_done = m.sem("n0_y_done")
        multiplied = m.sem("n0_multiplied")
        added = m.sem("n0_added")
        block = ctx.enter_context(nc.Block())

        def run(eng, step):
            for k in range(FIRST):
                step(0, k)
            with eng.Fori(0, TURNS) as i:
                for k in range(FIRST, FIRST + BODY):
                    step(i, k)
            for k in range(FIRST, N + 1 - TURNS * BODY):
                step(TURNS, k)

        def inside(i, k):
            return not isinstance(i, int) or 0 <= i * BODY + k < N

        def tokens(ap_3d, i, b):
            return ap_3d[:, 2 * BODY * i + b, :] if isinstance(i, int) else one(ap_3d, i * (2 * BODY) + b)

        def batches(i, k):
            return slice(2 * (i * BODY + k), 2 * (i * BODY + k) + 2) if isinstance(i, int) else \
                bass.ds(i * (2 * BODY) + 2 * k, 2)

        def early(i, k):
            return isinstance(i, int) and i * BODY + k < 2

        @block.gpsimd
        def _(pool):
            for k in range(NJ):
                nc.gpsimd.tensor_scalar(wo_b[:, k, :], wo_raw[:, k, :], gn_b[:, k:k + 1], 1.0 - LAMBDA_INIT,
                                        ALU.mult, ALU.mult).then_inc(wb_done, 1)
                nc.gpsimd.tensor_scalar(wo[:, k, :], wo_raw[:, k, :], gn_w[:, k:k + 1], 1.0 - LAMBDA_INIT,
                                        ALU.mult, ALU.mult).then_inc(wo_done, 1)
            def step(i, k):
                if inside(i, k):
                    pool.wait_ge(var_done, i * BODY + (k + 1))
                    nc.gpsimd.tensor_tensor(rstd[:, k % 2, :, :], var[:, k % 2, :, :],
                                            env["minus_half"][:, 0:2 * NJ].rearrange("p (b j) -> p b j", b=2), ALU.pow)\
                        .then_inc(rstd_done, 1)
                    pool.wait_ge(rstd_done, i * BODY + (k + 1))
                    nc.gpsimd.tensor_tensor(scaled[:, k % 2, :, :], avg[:, k % 2, :, :, 0], rstd[:, k % 2, :, :], ALU.mult)\
                        .then_inc(scaled_done, 1)
                    pool.wait_ge(scaled_done, i * BODY + (k + 1))
                    hold(pool)
                    nc.gpsimd.tensor_scalar(shift[:, k % 2, :, :], scaled[:, k % 2, :, :], -1.0, None, ALU.mult)\
                        .then_inc(shift_done, 1)
                    if isinstance(i, int) and i * BODY + k == 0:
                        pool.wait_ge(bias_done, 1)
                    bs = batches(i, k)
                    nc.gpsimd.tensor_tensor(X[:, bs, :], X[:, bs, :], bias[:, :].unsqueeze(1).broadcast_to([P, 2, D]),
                                            ALU.add).then_inc(bias_added, 1)

            run(pool, step)

        @block.scalar
        def _(act):
            def step(i, k):
                if inside(i, k):
                    p = k % 2
                    act.wait_ge(shift_done, i * BODY + (k + 1))
                    if not early(i, k):
                        act.wait_ge(multiplied, i * BODY + (k - 1))
                    hold(act)
                    for r in range(2):
                        for j in range(NJ):
                            last = nc.scalar.activation(yT[:, p, r, j, :], tokens(OT, i, 2 * k + r)[:, j * T:(j + 1) * T],
                                                        ACT.Identity, scale=rstd[:, p, r, j:j + 1],
                                                        bias=shift[:, p, r, j:j + 1])
                    last.then_inc(y_done, 1)

            run(act, step)

        @block.vector
        def _(dve):
            def statistics(i, k):
                p = k % 2
                if not isinstance(i, int):
                    hold(dve)
                for r in range(2):
                    for j in range(NJ):
                        last = nc.vector.bn_stats(stats[:, p, r, j, :], tokens(OT, i, 2 * k + r)[:, j * T:(j + 1) * T])
                last.then_inc(stats_done, 1)
                dve.wait_ge(stats_done, i * BODY + (k + 1))
                hold(dve)
                for r in range(2):
                    for j in range(NJ):
                        last = nc.vector.bn_aggr(moments[:, p, r, j, :], stats[:, p, r, j, :])
                last.then_inc(moments_done, 1)
                mean, power = moments[:, p, :, :, 0], moments[:, p, :, :, 1]
                dve.wait_ge(moments_done, i * BODY + (k + 1))
                nc.vector.tensor_tensor(square[:, p, :, :], mean, mean, ALU.mult).then_inc(squared, 1)
                dve.wait_ge(squared, i * BODY + (k + 1))
                nc.vector.tensor_tensor(power, power, square[:, p, :, :], ALU.add).then_inc(power_done, 1)

            def step(i, k):
                p = k % 2
                if inside(i, k):
                    dve.wait_ge(averaged, i * BODY + (k + 1))
                    if not early(i, k):
                        dve.wait_ge(y_done, i * BODY + (k - 1))
                    nc.vector.tensor_copy(avg[:, p, :, :, :].rearrange("p b j a -> p (b j a)"), avg_ps[p][:, 0:4 * NJ])\
                        .then_inc(avg_done, 1)
                    dve.wait_ge(avg_done, i * BODY + (k + 1))
                    nc.vector.tensor_tensor(avg2[:, p, :, :], avg[:, p, :, :, 0], avg[:, p, :, :, 0], ALU.mult)\
                        .then_inc(avg2_done, 1)
                    dve.wait_ge(avg2_done, i * BODY + (k + 1))
                    nc.vector.scalar_tensor_tensor(var[:, p, :, :], avg[:, p, :, :, 1], LN_EPS, avg2[:, p, :, :],
                                                   ALU.add, ALU.subtract).then_inc(var_done, 1)
                if inside(i, k + 1):
                    statistics(i, k + 1)
                if inside(i, k - 1):
                    dve.wait_ge(bias_added, i * BODY + k)
                    dve.wait_ge(multiplied, i * BODY + k)
                    hold(dve)
                    bs = batches(i, k - 1)
                    nc.vector.tensor_tensor(X[:, bs, :], X[:, bs, :],
                                            out_ps[(k - 1) % 2][:, :].rearrange("p (b d) -> p b d", b=2), ALU.add)\
                        .then_inc(added, 1)

            statistics(0, 0)
            dve.wait_ge(bias_ready, 1)
            nc.vector.tensor_copy(bias[:, :], bias_ps[:, 0:D]).then_inc(bias_done, 1)
            run(dve, step)

        @block.tensor
        def _(pe):
            pe.wait_ge(wb_done, NJ)
            for k in range(NJ):
                last = nc.tensor.matmul(bias_ps[:, 0:D], env["ones"][:, :], wo_b[:, k, :], start=(k == 0), stop=(k == NJ - 1))
            last.then_inc(bias_ready, 1)
            pe.wait_ge(wo_done, NJ)

            def average(i, k):
                pe.wait_ge(power_done, i * BODY + (k + 1))
                nc.tensor.matmul(avg_ps[k % 2][:, 0:4 * NJ], share[:, :],
                                 moments[:, k % 2, :, :, :].rearrange("p b j a -> p (b j a)"), start=True, stop=True)\
                    .then_inc(averaged, 1)

            def step(i, k):
                if inside(i, k + 1):
                    average(i, k + 1)
                if inside(i, k):
                    pe.wait_ge(y_done, i * BODY + (k + 1))
                    if not early(i, k):
                        pe.wait_ge(added, i * BODY + (k - 1))
                    for r in range(2):
                        for j in range(NJ):
                            last = nc.tensor.matmul(out_ps[k % 2][:, r * D:(r + 1) * D], yT[:, k % 2, r, j, :], wo[:, j, :],
                                                    start=(j == 0), stop=(j == NJ - 1))
                    last.then_inc(multiplied, 1)

            average(0, 0)
            run(pe, step)


def stage_conv0(nc, env, inp):
    XTf, Z, C = env["XTf"], env["Z"], env["C"]
    HD = 8
    H = T // HD
    LB = D // P
    with ExitStack() as ctx:
        m = Mem(nc, ctx)
        toep = [m.sb(f"c0_toep{i}", [P, LB * P]) for i in range(2)]
        toep_d = [m.sb(f"c0_toep_d{i}", [P, P]) for i in range(2)]
        d_all = m.sb("c0_d_all", [P, H])
        anti = m.sb("c0_anti", [P, P])
        d_diag = m.sb("c0_d_diag", [P, H, P])
        pairs = m.sb("c0_pairs", [P, 2, LB, HD, HD, B])
        weighted = m.sb("c0_weighted", [P, 2, HD, HD, B])
        y_ps = [[m.ps(f"c0_y_ps{r}{lb}", [P, 2 * BANK]) for lb in range(LB)] for r in range(2)]
        d_in = m.sem("c0_d_in")
        toep_in = [m.sem(f"c0_toep_in{r}") for r in range(2)]
        diag_done = m.sem("c0_diag_done")
        toep_done = m.sem("c0_toep_done")
        paired = m.sem("c0_paired")
        convolved = m.sem("c0_convolved")
        weighted_done = m.sem("c0_weighted_done")
        summed = m.sem("c0_summed")
        block = ctx.enter_context(nc.Block())

        @block.sync
        def _(sp):
            sp.dma_start(d_all[:, :], inp["c0_D"].partition_broadcast(P)).then_inc(d_in, 16)
            sp.dma_start(anti[:, :], inp["anti"]).then_inc(d_in, 16)
            sp.sem_inc(convolved, 4)
            with sp.Fori(0, H // 2) as i:
                for r in range(2):
                    sp.wait_ge(convolved, i * 4 + (2 * r + 2))
                    hold(sp)
                    sp.dma_start(toep[r][:, :], inp["toeplitz"][bass.ds(i * 2 + r, 1), :, :]
                                 .rearrange("o p l -> p (o l)")).then_inc(toep_in[r], 16)

        @block.gpsimd
        def _(pool):
            with pool.Fori(0, H // 2) as i:
                for r in range(2):
                    pool.wait_ge(convolved, i * 4 + (2 * r + 2))
                    for mb in range(LB):
                        hold(pool)
                        c = C[:, mb, bass.ds((i * 2 + r) * HD, HD), :]
                        nc.gpsimd.tensor_tensor(pairs[:, r, mb, :, :, :],
                                                c.unsqueeze(2).broadcast_to([P, HD, HD, B]),
                                                c.unsqueeze(1).broadcast_to([P, HD, HD, B]), ALU.mult).then_inc(paired, 1)

        @block.vector
        def _(dve):
            dve.sem_inc(weighted_done, 4)
            dve.wait_ge(d_in, 32)
            nc.vector.tensor_tensor(d_diag[:, :, :], anti[:, :].unsqueeze(1).broadcast_to([P, H, P]),
                                    d_all[:, :].unsqueeze(2).broadcast_to([P, H, P]), ALU.mult).then_inc(diag_done, 1)
            dve.wait_ge(diag_done, 1)
            hold(dve)

            def diagonal(i, r):
                dve.wait_ge(toep_in[r], i * 16 + 16)
                dve.wait_ge(convolved, i * 4 + (2 * r + 2))
                d = d_diag[:, r, :] if isinstance(i, int) else one(d_diag, i * 2 + r)
                nc.vector.tensor_tensor(toep_d[r][:, :], toep[r][:, 0:P], d, ALU.add)\
                    .then_inc(toep_done, 1)

            def weigh(i, r):
                for lb in range(LB):
                    n = 2 * r + lb
                    dve.wait_ge(convolved, i * 4 + (n + 5))
                    heads = bass.ds((i * 2 + r) * HD, HD) if not isinstance(i, int) else \
                        slice((2 * i + r) * HD, (2 * i + r + 1) * HD)
                    q = XTf[:, lb, :].rearrange("p (b t) -> p t b", b=B)[:, heads, :]
                    nc.vector.tensor_tensor(weighted[:, lb, :, :, :],
                                            y_ps[r][lb][:, :].rearrange("p (i j b) -> p i j b", i=HD, j=HD),
                                            q.unsqueeze(2).broadcast_to([P, HD, HD, B]), ALU.mult)\
                        .then_inc(weighted_done, 1)
                    dve.wait_ge(weighted_done, i * 4 + (n + 5))
                    nc.vector.tensor_reduce(Z[:, lb, :, :].rearrange("p b t -> p t b")[:, heads, :],
                                            weighted[:, lb, :, :, :].rearrange("p i j b -> p j b i"),
                                            AX_X, ALU.add).then_inc(summed, 1)

            for r in range(2):
                diagonal(0, r)
            with dve.Fori(0, H // 2 - 1) as i:
                for r in range(2):
                    weigh(i, r)
                    diagonal(i + 1, r)
            for r in range(2):
                weigh(H // 2 - 1, r)

        @block.tensor
        def _(pe):
            with pe.Fori(0, H // 2) as i:
                for r in range(2):
                    halves2 = [slice(0, HD // 2), slice(HD // 2, HD)]

                    def product(lb, mb, weights, start, stop):
                        for k, half in enumerate(halves2):
                            last = nc.tensor.matmul(y_ps[r][lb][:, k * BANK:(k + 1) * BANK], weights,
                                                    pairs[:, r, mb, half, :, :].rearrange("p i j b -> p (i j b)"),
                                                    start=start, stop=stop)
                        return last

                    pe.wait_ge(weighted_done, i * 4 + (2 * r + 2))
                    pe.wait_ge(toep_done, i * 2 + (r + 1))
                    pe.wait_ge(paired, i * 4 + (2 * r + 1))
                    product(0, 0, toep_d[r][:, :], True, True).then_inc(convolved, 1)
                    product(1, 0, toep[r][:, P:2 * P], True, False)
                    pe.wait_ge(paired, i * 4 + (2 * r + 2))
                    product(1, 1, toep_d[r][:, :], False, True).then_inc(convolved, 1)


def stage_conv0_out(nc, env):
    X, Z = env["X"], env["Z"]
    with ExitStack() as ctx:
        m = Mem(nc, ctx)
        z = m.sb("z0_z", [P, 2, D // P, T])
        z_ps = [m.ps(f"z0_z_ps{i}", [P, BANK]) for i in range(2)]
        copied = m.sem("z0_copied")
        turned = m.sem("z0_turned")
        added = m.sem("z0_added")
        block = ctx.enter_context(nc.Block())

        @block.scalar
        def _(act):
            with act.Fori(0, B // 2) as i:
                for r in range(2):
                    act.wait_ge(turned, i * 2 + (r + 1))
                    hold(act)
                    nc.scalar.activation(z[:, r, :, :], Z[:, :, bass.ds(i * 2 + r, 1), :].rearrange("p l o t -> p l (o t)"),
                                         ACT.Copy).then_inc(copied, 1)

        @block.tensor
        def _(pe):
            pe.sem_inc(turned, 2)
            with pe.Fori(0, B // 2) as i:
                for r in range(2):
                    pe.wait_ge(copied, i * 2 + (r + 1))
                    pe.wait_ge(added, i * 2 + (r + 1))
                    for lb in range(D // P):
                        last = nc.tensor.transpose(z_ps[r][:, lb * P:(lb + 1) * P], z[:, r, lb, :], env["ident"][:, :])
                    last.then_inc(turned, 1)

        @block.vector
        def _(dve):
            dve.sem_inc(added, 2)
            with dve.Fori(0, B // 2) as i:
                for r in range(2):
                    dve.wait_ge(turned, i * 2 + (r + 3))
                    hold(dve)
                    nc.vector.tensor_tensor(one(X, i * 2 + r), one(X, i * 2 + r), z_ps[r][:, 0:D], ALU.add)\
                        .then_inc(added, 1)


def stage_moe0(nc, env, inp):
    X, XTh, XTl, ident = env["X"], env["XTh"], env["XTl"], env["ident"]
    E = 8
    HT = D // P
    WG = 2 * D
    WE = WG + D
    NU = E * HT
    with ExitStack() as ctx:
        m = Mem(nc, ctx)
        w_raw, r_raw, r_scale, rank, per_expert = (env[n] for n in ("w_raw", "r_raw", "r_scale", "rank", "per_expert"))
        w_hi = m.sb("m0_w_hi", [P, E, DT, WE], F32R)
        w_lo = m.sb("m0_w_lo", [P, E, DT, WE], F32R)
        r_scaled = m.sb("m0_r_scaled", [P, DT, P])
        r_hi = m.sb("m0_r_hi", [P, DT, P], F32R)
        r_lo = m.sb("m0_r_lo", [P, DT, P], F32R)
        square = m.sb("m0_square", [P, D])
        power = m.sb("m0_power", [P, B])
        power_eps = m.sb("m0_power_eps", [P, B])
        x_rstd = m.sb("m0_x_rstd", [P, B])
        lgT = m.sb("m0_lgT", [P, 2, GT])
        small = {n: m.sb(f"m0_{n}", [P, B, E]) for n in
                 ("logit", "tie", "order", "first", "rest", "tie2", "order2", "second", "chosen", "less", "exp",
                  "picked", "share", "weight")}
        top = {n: m.sb(f"m0_{n}", [P, B]) for n in ("max1", "rank1", "max2", "rank2", "total", "inverse")}
        w_grp = m.sb("m0_w_grp", [P, G, E])
        act_g = m.sb("m0_act_g", [P, 2, GT])
        hid = m.sb("m0_hid", [P, 2, GT])
        hid_hi = m.sb("m0_hid_hi", [P, 2, HT, GT], F32R)
        hid_lo = m.sb("m0_hid_lo", [P, 2, HT, GT], F32R)
        acc = m.sb("m0_acc", [P, G, D])
        gate_ps = [m.ps(f"m0_gate_ps{i}", [P, BANK]) for i in range(2)]
        up_ps = [m.ps(f"m0_up_ps{i}", [P, BANK]) for i in range(2)]
        out_ps = [[m.ps(f"m0_out_ps{i}{k}", [P, BANK]) for k in range(2)] for i in range(2)]
        w_in = [m.sem(f"m0_w_in{i}") for i in range(2)]
        whi_done = m.sem("m0_whi_done")
        wlo_done = m.sem("m0_wlo_done")
        power_done = m.sem("m0_power_done")
        eps_done = m.sem("m0_eps_done")
        x_rstd_done = m.sem("m0_x_rstd_done")
        r_scaled_done = m.sem("m0_r_scaled_done")
        rhi_done = m.sem("m0_rhi_done")
        rlo_done = m.sem("m0_rlo_done")
        lgT_ready = m.sem("m0_lgT_ready")
        lgT_done = m.sem("m0_lgT_done")
        lg_ready = m.sem("m0_lg_ready")
        logit_done = m.sem("m0_logit_done")
        routed = m.sem("m0_routed")
        exp_done = m.sem("m0_exp_done")
        grp_done = m.sem("m0_grp_done")
        gated = m.sem("m0_gated")
        gelu_done = m.sem("m0_gelu_done")
        hid_done = m.sem("m0_hid_done")
        hid_hi_done = m.sem("m0_hid_hi_done")
        hid_lo_done = m.sem("m0_hid_lo_done")
        down_done = m.sem("m0_down_done")
        acc_done = m.sem("m0_acc_done")
        block = ctx.enter_context(nc.Block())

        @block.sync
        def _(sp):
            for e in range(2, E):
                sp.wait_ge(wlo_done, e - 1)
                sp.dma_start(w_raw[:, e % 2, :, :], inp["m0_w"][e].rearrange("(k p) n -> p k n", p=P))\
                    .then_inc(w_in[e % 2], 16)

        @block.gpsimd
        def _(pool):
            def w_low(e):
                pool.wait_ge(whi_done, e + 1)
                nc.gpsimd.tensor_tensor(w_lo[:, e, :, :], w_raw[:, e % 2, :, :], w_hi[:, e, :, :].bitcast(F32),
                                        ALU.subtract).then_inc(wlo_done, 1)

            def hidden_low(g, u):
                pool.wait_ge(hid_hi_done, g * NU + (u + 1))
                nc.gpsimd.tensor_tensor(hid_lo[:, u // HT % 2, u % HT, :], hid[:, u % 2, :],
                                        hid_hi[:, u // HT % 2, u % HT, :].bitcast(F32), ALU.subtract)\
                    .then_inc(hid_lo_done, 1)

            w_low(0)
            w_low(1)
            pool.wait_ge(power_done, B)
            nc.gpsimd.tensor_scalar(power_eps[:, :], power[:, :], 1.0 / D, 1e-6, ALU.mult, ALU.add).then_inc(eps_done, 1)
            pool.wait_ge(eps_done, 1)
            nc.gpsimd.tensor_tensor(x_rstd[:, :], power_eps[:, :], env["minus_half"][:, 0:B], ALU.pow)\
                .then_inc(x_rstd_done, 1)
            for u in range(NU):
                hidden_low(0, u)
                if u % HT == HT - 1 and u // HT + 2 < E:
                    w_low(u // HT + 2)
            with pool.Fori(1, NG) as g:
                for u in range(NU):
                    hidden_low(g, u)

        def high(act, g, u):
            act.wait_ge(hid_done, g * NU + (u + 3))
            nc.scalar.activation(hid_hi[:, u // HT % 2, u % HT, :], hid[:, u % 2, :], ACT.Copy).then_inc(hid_hi_done, 1)

        @block.scalar
        def _(act):
            def w_high(e):
                if e >= 2:
                    act.wait_ge(w_in[e % 2], 16 * (e // 2))
                nc.scalar.activation(w_hi[:, e, :, :], w_raw[:, e % 2, :, :], ACT.Copy).then_inc(whi_done, 1)

            def group(g):
                for u in range(NU):
                    act.wait_ge(gated, g * NU + (u + 1))
                    nc.scalar.activation(act_g[:, u % 2, :], gate_ps[u % 2][:, :], ACT.Gelu_apprx_tanh)\
                        .then_inc(gelu_done, 1)
                    if isinstance(g, int) and u % HT == HT - 1 and u // HT + 2 < E:
                        w_high(u // HT + 2)
                    if u >= 1:
                        high(act, g, u - 1)
                    if isinstance(g, int) and u == 1:
                        act.wait_ge(routed, 11)
                        nc.scalar.activation(small["exp"][:, :, :], small["less"][:, :, :], ACT.Exp).then_inc(exp_done, 1)
                high(act, g, NU - 1)

            act.wait_ge(r_scaled_done, DT)
            nc.scalar.activation(r_hi[:, :, :], r_scaled[:, :, :], ACT.Copy).then_inc(rhi_done, 1)
            w_high(0)
            w_high(1)
            for g in range(NG):
                act.wait_ge(lgT_ready, g + 1)
                if g >= 2:
                    act.wait_ge(lg_ready, g - 1)
                nc.scalar.activation(lgT[:, g % 2, :], gate_ps[g % 2][:, :], ACT.Copy).then_inc(lgT_done, 1)
                for b in range(g * G, (g + 1) * G):
                    if b:
                        act.wait_ge(power_done, b)
                    nc.scalar.activation(square[:, :], X[:, b, :], ACT.Square, accum_out=power[:, b:b + 1])\
                        .then_inc(power_done, 1)
            group(0)
            with act.Fori(1, NG) as g:
                group(g)

        @block.vector
        def _(dve):
            for dt in range(DT):
                nc.vector.tensor_scalar(r_scaled[:, dt, :], r_raw[:, dt, :], r_scale[:, dt:dt + 1], D ** -0.5,
                                        ALU.mult, ALU.mult).then_inc(r_scaled_done, 1)
            dve.wait_ge(rhi_done, 1)
            nc.vector.tensor_tensor(r_lo[:, :, :], r_scaled[:, :, :], r_hi[:, :, :].bitcast(F32), ALU.subtract)\
                .then_inc(rlo_done, 1)
            dve.wait_ge(x_rstd_done, 1)
            for g in range(NG):
                dve.wait_ge(lg_ready, g + 1)
                nc.vector.tensor_tensor(small["logit"][:, g * G:(g + 1) * G, :],
                                        out_ps[g // 2][g % 2][:, :].rearrange("p (b t) -> p b t", b=G)[:, :, 0:E],
                                        x_rstd[:, g * G:(g + 1) * G].unsqueeze(2).broadcast_to([P, G, E]),
                                        ALU.mult).then_inc(logit_done, 1)

            def wide(name):
                return top[name][:, :].unsqueeze(2).broadcast_to([P, B, E])

            def expert_row(ap):
                return ap[:, :].unsqueeze(1).broadcast_to([P, B, E])

            s = {n: ap[:, :, :] for n, ap in small.items()}
            step = [0]

            def chained(ins):
                step[0] += 1
                ins.then_inc(routed, 1)
                dve.wait_ge(routed, step[0])

            tt = nc.vector.tensor_tensor

            def choose():
                dve.wait_ge(logit_done, NG)
                chained(nc.vector.tensor_reduce(top["max1"][:, :], s["logit"], AX_X, ALU.max))
                chained(tt(s["tie"], s["logit"], wide("max1"), ALU.is_equal))
                chained(tt(s["order"], s["tie"], expert_row(rank), ALU.mult))
                chained(nc.vector.tensor_reduce(top["rank1"][:, :], s["order"], AX_X, ALU.max))
                chained(tt(s["first"], s["order"], wide("rank1"), ALU.is_equal))
                chained(nc.vector.scalar_tensor_tensor(s["rest"].rearrange("p b e -> p (b e)"),
                                                       s["first"].rearrange("p b e -> p (b e)"), -1e38,
                                                       s["logit"].rearrange("p b e -> p (b e)"), ALU.mult, ALU.add))
                chained(nc.vector.tensor_reduce(top["max2"][:, :], s["rest"], AX_X, ALU.max))
                chained(tt(s["tie2"], s["rest"], wide("max2"), ALU.is_equal))
                chained(tt(s["order2"], s["tie2"], expert_row(rank), ALU.mult))
                chained(nc.vector.tensor_reduce(top["rank2"][:, :], s["order2"], AX_X, ALU.max))
                chained(tt(s["less"], s["logit"], wide("max1"), ALU.subtract))
                chained(tt(s["second"], s["order2"], wide("rank2"), ALU.is_equal))
                chained(tt(s["chosen"], s["first"], s["second"], ALU.add))
                dve.wait_ge(exp_done, 1)
                chained(tt(s["picked"], s["exp"], s["chosen"], ALU.mult))
                chained(nc.vector.tensor_reduce(top["total"][:, :], s["picked"], AX_X, ALU.add))
                chained(nc.vector.reciprocal(top["inverse"][:, :], top["total"][:, :]))
                chained(tt(s["share"], s["picked"], wide("inverse"), ALU.mult))
                chained(tt(s["weight"], s["share"], expert_row(per_expert), ALU.mult))

            def accumulate(g, e):
                for j in range(G):
                    dve.wait_ge(down_done, g * E * G + (e * G + j // 2 * 2 + 2))
                    if e:
                        dve.wait_ge(acc_done, g * E * G + ((e + 1) * G + j + 1))
                    hold(dve)
                    x = X[:, g * G + j, :] if isinstance(g, int) else one(X, g * G + j)
                    src = acc[:, j, :] if e else x
                    dst = acc[:, j, :] if e < E - 1 else x
                    nc.vector.scalar_tensor_tensor(dst, out_ps[e % 2][j // 2][:, (j % 2) * D:(j % 2 + 1) * D],
                                                   w_grp[:, j, e:e + 1], src, ALU.mult, ALU.add).then_inc(acc_done, 1)

            dve.sem_inc(hid_done, 2)
            dve.sem_inc(acc_done, 2 * G)

            def group(g):
                for u in range(NU):
                    if u == 2:
                        if isinstance(g, int):
                            choose()
                        dve.wait_ge(acc_done, g * E * G + 2 * G)
                        hold(dve)
                        bs = slice(g * G, (g + 1) * G) if isinstance(g, int) else bass.ds(g * G, G)
                        nc.vector.tensor_copy(w_grp[:, :, :], small["weight"][:, bs, :]).then_inc(grp_done, 1)
                        dve.wait_ge(grp_done, g + 1)
                        hold(dve)
                    dve.wait_ge(gelu_done, g * NU + (u + 1))
                    if u >= 2:
                        dve.wait_ge(hid_lo_done, g * NU + (u - 1))
                    nc.vector.tensor_tensor(hid[:, u % 2, :], act_g[:, u % 2, :], up_ps[u % 2][:, :], ALU.mult)\
                        .then_inc(hid_done, 1)
                    if u % HT == HT - 1 and u >= 2 * HT - 1:
                        accumulate(g, u // HT - 1)
                accumulate(g, E - 1)

            group(0)
            with dve.Fori(1, NG) as g:
                group(g)

        @block.tensor
        def _(pe):
            def logits(g):
                toks = slice(g * GT, (g + 1) * GT)
                if g >= 2:
                    pe.wait_ge(lgT_done, g - 1)
                halves(nc, gate_ps[g % 2][:, :], [lambda dt: r_hi[:, dt, :], lambda dt: r_lo[:, dt, :]],
                       [lambda dt: XTh[:, dt, toks], lambda dt: XTl[:, dt, toks]], DT).then_inc(lgT_ready, 1)

            pe.wait_ge(rlo_done, 1)
            logits(0)
            for g in range(NG):
                if g + 1 < NG:
                    logits(g + 1)
                pe.wait_ge(lgT_done, g + 1)
                for b in range(G):
                    last = nc.tensor.transpose(out_ps[g // 2][g % 2][:, b * P:(b + 1) * P], lgT[:, g % 2, b * T:(b + 1) * T],
                                               ident[:, :])
                last.then_inc(lg_ready, 1)

            def gates(g, e):
                toks = bass.ds(g * GT, GT)
                x_halves = [lambda dt: XTh[:, dt, toks], lambda dt: XTl[:, dt, toks]]
                pe.wait_ge(wlo_done, e + 1)
                for ht in range(HT):
                    u = e * HT + ht
                    pe.wait_ge(hid_done, g * NU + (u + 1))
                    for ps, c0 in ((gate_ps[u % 2], ht * P), (up_ps[u % 2], D + ht * P)):
                        c = slice(c0, c0 + P)
                        last = halves(nc, ps[:, :], [lambda dt: w_hi[:, e, dt, c], lambda dt: w_lo[:, e, dt, c]],
                                      x_halves, DT)
                    last.then_inc(gated, 1)

            def down(g, e):
                pe.wait_ge(hid_lo_done, g * NU + (e * HT + HT))
                pe.wait_ge(logit_done, NG)
                pe.wait_ge(acc_done, g * E * G + (e * G + G))
                for j in range(G):
                    toks = slice(j * T, (j + 1) * T)
                    halves(nc, out_ps[e % 2][j // 2][:, (j % 2) * D:(j % 2 + 1) * D],
                           [lambda n: hid_hi[:, e % 2, n, toks], lambda n: hid_lo[:, e % 2, n, toks]],
                           [lambda n: w_hi[:, e, n, WG:WE], lambda n: w_lo[:, e, n, WG:WE]], HT).then_inc(down_done, 1)

            with pe.Fori(0, NG) as g:
                gates(g, 0)
                for e in range(E):
                    if e + 1 < E:
                        gates(g, e + 1)
                    down(g, e)


def stage_attn1(nc, env, inp):
    X, XTh, XTl, ident = env["X"], env["XTh"], env["XTl"], env["ident"]
    H, DH = 16, P
    SCALE = 1.0 / math.sqrt(DH)
    N = H * NG
    BODY = 2 * NG
    FIRST = 3
    TURNS = (N - FIRST - NG - 2) // BODY
    QK = 2 * DH
    V2 = 2 * DH
    with ExitStack() as ctx:
        m = Mem(nc, ctx)
        w_raw, wv_raw, w_bias, o_raw = (env[n] for n in ("w_raw", "wv_raw", "w_bias", "o_raw"))
        w_full = m.sb("a1_w_full", [P, DT, QK])
        wv_full = m.sb("a1_wv_full", [P, DT, V2])
        wv_hi = m.sb("a1_wv_hi", [P, DT, V2], F32R)
        wv_lo = m.sb("a1_wv_lo", [P, DT, V2], F32R)
        w_hi = m.sb("a1_w_hi", [P, 2, DT, QK], F32R)
        w_lo = m.sb("a1_w_lo", [P, 2, DT, QK], F32R)
        o_full = m.sb("a1_o_full", [P, D])
        o_hi = m.sb("a1_o_hi", [P, 2, D], F32R)
        o_lo = m.sb("a1_o_lo", [P, 2, D], F32R)
        bo = m.sb("a1_bo", [P, D])
        qT = m.sb("a1_qT", [P, 4, GT])
        kT = m.sb("a1_kT", [P, 4, GT])
        v = m.sb("a1_v", [P, NG, G, V2])
        negmax = m.sb("a1_negmax", [P, 2, G])
        shift = m.sb("a1_shift", [P, 2, G])
        sums = m.sb("a1_sums", [P, 2, G])
        recip = m.sb("a1_recip", [P, 2, G])
        probs = m.sb("a1_probs", [P, 2, G, T])
        normed = m.sb("a1_normed", [P, 2, G, T])
        normedT = m.sb("a1_normedT", [P, 2, GT])
        head_hi = m.sb("a1_head_hi", [P, 2, GT], F32R)
        head_lo = m.sb("a1_head_lo", [P, 2, GT], F32R)
        proj_ps = [m.ps(f"a1_proj_ps{i}", [P, BANK]) for i in range(2)]
        s_ps = m.ps("a1_s_ps", [P, BANK])
        nT_ps = m.ps("a1_nT_ps", [P, BANK])
        v_ps = m.ps("a1_v_ps", [P, BANK])
        head_ps = m.ps("a1_head_ps", [P, BANK])
        out_ps = [m.ps(f"a1_out_ps{i}", [P, BANK]) for i in range(2)]
        w_in = [m.sem(f"a1_w_in{i}") for i in range(2)]
        o_in = [m.sem(f"a1_o_in{i}") for i in range(2)]
        b_in = [m.sem(f"a1_b_in{i}") for i in range(2)]
        bo_in = m.sem("a1_bo_in")
        wv_in = m.sem("a1_wv_in")
        wvfull_done = m.sem("a1_wvfull_done")
        wvhi_done = m.sem("a1_wvhi_done")
        wvlo_done = m.sem("a1_wvlo_done")
        bo_done = m.sem("a1_bo_done")
        wfull_done = m.sem("a1_wfull_done")
        whi_done = m.sem("a1_whi_done")
        wlo_done = m.sem("a1_wlo_done")
        ofull_done = m.sem("a1_ofull_done")
        ohi_done = m.sem("a1_ohi_done")
        olo_done = m.sem("a1_olo_done")
        projected = m.sem("a1_projected")
        proj_read = m.sem("a1_proj_read")
        v_projected = m.sem("a1_v_projected")
        v_done = m.sem("a1_v_done")
        scored = m.sem("a1_scored")
        maxed = m.sem("a1_maxed")
        shifted = m.sem("a1_shifted")
        exped = m.sem("a1_exped")
        recip_done = m.sem("a1_recip_done")
        normed_done = m.sem("a1_normed_done")
        turned = m.sem("a1_turned")
        nT_done = m.sem("a1_nT_done")
        valued = m.sem("a1_valued")
        hi_done = m.sem("a1_hi_done")
        lo_done = m.sem("a1_lo_done")
        multiplied = m.sem("a1_multiplied")
        added = m.sem("a1_added")
        block = ctx.enter_context(nc.Block())

        def run(eng, step):
            for k in range(FIRST):
                step(0, k)
            with eng.Fori(0, TURNS) as i:
                for k in range(FIRST, FIRST + BODY):
                    step(i, k)
            for k in range(FIRST, N + 3 - TURNS * BODY):
                step(TURNS, k)

        def inside(i, k):
            return not isinstance(i, int) or 0 <= i * BODY + k < N

        def has_values(k):
            return k // NG % 2 == 0

        def rounds(i, k):
            return i * (2 * NG) + 2 * (k // BODY * NG + k % NG)

        def w_low(pool, i, h):
            pool.wait_ge(whi_done, i * 2 + (h + 1))
            nc.gpsimd.tensor_tensor(w_lo[:, h % 2, :, :], w_full[:, :, :], w_hi[:, h % 2, :, :].bitcast(F32),
                                    ALU.subtract).then_inc(wlo_done, 1)
            if h % 2 == 0:
                pool.wait_ge(wvhi_done, i + (h // 2 + 1))
                nc.gpsimd.tensor_tensor(wv_lo[:, :, :], wv_full[:, :, :], wv_hi[:, :, :].bitcast(F32),
                                        ALU.subtract).then_inc(wvlo_done, 1)

        def w_high(act, i, h):
            act.wait_ge(wfull_done, i * 2 + (h + 1))
            nc.scalar.activation(w_hi[:, h % 2, :, :], w_full[:, :, :], ACT.Copy).then_inc(whi_done, 1)
            if h % 2 == 0:
                act.wait_ge(wvfull_done, i + (h // 2 + 1))
                nc.scalar.activation(wv_hi[:, :, :], wv_full[:, :, :], ACT.Copy).then_inc(wvhi_done, 1)

        def w_multiply(dve, i, h):
            dve.wait_ge(w_in[h % 2], i * 16 + (h // 2 + 1) * 16)
            if not (isinstance(i, int) and i * BODY + h == 0):
                dve.wait_ge(wlo_done, i * 2 + h)
            nc.vector.tensor_tensor(w_full[:, :, :], w_raw[:, h % 2, :, 0, :], w_raw[:, h % 2, :, 1, :], ALU.mult)\
                .then_inc(wfull_done, 1)
            if h % 2 == 0:
                dve.wait_ge(wv_in, i * 16 + (h // 2 + 1) * 16)
                if not (isinstance(i, int) and i * BODY + h == 0):
                    dve.wait_ge(wvlo_done, i + h // 2)
                nc.vector.tensor_tensor(wv_full[:, :, :], wv_raw[:, :, 0, :], wv_raw[:, :, 1, :], ALU.mult)\
                    .then_inc(wvfull_done, 1)

        def project_read(act, i, k):
            par = k // NG % 2
            if k % NG == 0:
                act.wait_ge(b_in[par], i * 16 + (k // BODY + 1) * 16)
            for a, dst in enumerate((qT, kT)):
                act.wait_ge(projected, i * (2 * BODY) + (2 * k + a + 1))
                nc.scalar.activation(dst[:, k % 4, :], proj_ps[a][:, :], ACT.Identity, bias=w_bias[:, par, a:a + 1])\
                    .then_inc(proj_read, 1)

        def values_read(act, i, k, half):
            act.wait_ge(v_projected, rounds(i, k) + (half + 1))
            nc.scalar.activation(v[:, k % NG, 2 * half:2 * half + 2, :], v_ps[:, :].rearrange("p (b n) -> p b n", b=2),
                                 ACT.Copy).then_inc(v_done, 1)

        @block.sync
        def _(sp):
            sp.dma_start(bo[:, :], inp["a1_bo"].partition_broadcast(P)).then_inc(bo_in, 16)

            sp.sem_inc(wv_in, 16)
            for par in range(2):
                for first in (w_in, o_in, b_in):
                    sp.sem_inc(first[par], 16)
            with sp.Fori(1, H // 2) as i:
                sp.wait_ge(wvlo_done, i)
                hold(sp)
                sp.dma_start(wv_raw[:, :, :, :].rearrange("p k a n -> p k (a n)"),
                             inp["a1_wv"][bass.ds(i, 1)].rearrange("o (k p) n -> p (o k) n", p=P)).then_inc(wv_in, 16)
                for par in range(2):
                    head = bass.ds(i * 2 + par, 1)
                    sp.wait_ge(wlo_done, i * 2 + (par - 1))
                    sp.wait_ge(olo_done, i * 2 + (par - 1))
                    hold(sp)
                    sp.dma_start(w_raw[:, par, :, :, :].rearrange("p k a n -> p k (a n)"),
                                 inp["a1_w"][head].rearrange("o (k p) n -> p (o k) n", p=P)).then_inc(w_in[par], 16)
                    sp.dma_start(o_raw[:, par, :, :].rearrange("p a n -> p (a n)"),
                                 inp["a1_wo"][head].rearrange("o r c -> r (o c)")).then_inc(o_in[par], 16)
                    sp.wait_ge(lo_done, i * (2 * NG) + (par - 1) * NG)
                    hold(sp)
                    sp.dma_start(w_bias[:, par, :], inp["a1_bias"][head].rearrange("o r c -> r (o c)"))\
                        .then_inc(b_in[par], 16)

        @block.gpsimd
        def _(pool):
            w_low(pool, 0, 0)
            w_low(pool, 0, 1)
            pool.wait_ge(bo_in, 16)
            nc.gpsimd.tensor_tensor(X[:, :, :], X[:, :, :], bo[:, :].unsqueeze(1).broadcast_to([P, B, D]), ALU.add)\
                .then_inc(bo_done, 1)

            def step(i, k):
                if inside(i, k):
                    pool.wait_ge(recip_done, i * BODY + (k + 1))
                    nc.gpsimd.tensor_tensor(normed[:, k % 2, :, :], probs[:, k % 2, :, :],
                                            recip[:, k % 2, :].unsqueeze(2).broadcast_to([P, G, T]), ALU.mult)\
                        .then_inc(normed_done, 1)
                if k % NG == 2 and inside(i, k + 6):
                    w_low(pool, i, (k + 6) // NG)
                if k % NG == 0 and inside(i, k):
                    hq = k // NG
                    pool.wait_ge(ohi_done, i * 2 + (hq + 1))
                    nc.gpsimd.tensor_tensor(o_lo[:, hq % 2, :], o_full[:, :], o_hi[:, hq % 2, :].bitcast(F32),
                                            ALU.subtract).then_inc(olo_done, 1)

            run(pool, step)

        @block.scalar
        def _(act):
            w_high(act, 0, 0)
            w_high(act, 0, 1)
            for k in range(2):
                project_read(act, 0, k)
                for half in range(2):
                    values_read(act, 0, k, half)

            def step(i, k):
                if inside(i, k):
                    act.wait_ge(shifted, i * BODY + (k + 1))
                    for j in range(G):
                        nc.scalar.activation(probs[:, k % 2, j, :], s_ps[:, j * T:(j + 1) * T], ACT.Exp, scale=SCALE,
                                             bias=shift[:, k % 2, j:j + 1], accum_out=sums[:, k % 2, j:j + 1])\
                            .then_inc(exped, 1)
                if inside(i, k - 1):
                    act.wait_ge(turned, i * BODY + k)
                    nc.scalar.activation(normedT[:, (k - 1) % 2, :], nT_ps[:, :], ACT.Copy).then_inc(nT_done, 1)
                if inside(i, k + 2):
                    project_read(act, i, k + 2)
                    if has_values(k + 2):
                        values_read(act, i, k + 2, 0)
                if inside(i, k - 1):
                    act.wait_ge(valued, i * BODY + k)
                    nc.scalar.activation(head_hi[:, (k - 1) % 2, :], head_ps[:, :], ACT.Identity,
                                         bias=w_bias[:, (k - 1) // NG % 2, 2:3]).then_inc(hi_done, 1)
                if inside(i, k + 2) and has_values(k + 2):
                    values_read(act, i, k + 2, 1)
                if k % NG == 2 and inside(i, k + 6):
                    w_high(act, i, (k + 6) // NG)
                if k % NG == 0 and inside(i, k):
                    hq = k // NG
                    act.wait_ge(ofull_done, i * 2 + (hq + 1))
                    nc.scalar.activation(o_hi[:, hq % 2, :], o_full[:, :], ACT.Copy).then_inc(ohi_done, 1)

            run(act, step)

        @block.vector
        def _(dve):
            w_multiply(dve, 0, 0)
            w_multiply(dve, 0, 1)

            def step(i, k):
                if inside(i, k):
                    dve.wait_ge(scored, i * BODY + (k + 1))
                    nc.vector.tensor_reduce(negmax[:, k % 2, :], s_ps[:, :].rearrange("p (b s) -> p b s", b=G),
                                            AX_X, ALU.max, negate=True).then_inc(maxed, 1)
                    dve.wait_ge(maxed, i * BODY + (k + 1))
                    nc.vector.tensor_scalar(shift[:, k % 2, :], negmax[:, k % 2, :], SCALE, None, ALU.mult)\
                        .then_inc(shifted, 1)
                if inside(i, k - 3):
                    g = (k - 3) % NG
                    if isinstance(i, int) and i * BODY + k == 3:
                        dve.wait_ge(bo_done, 1)
                    dve.wait_ge(multiplied, i * BODY + (k - 2))
                    for c in range(2):
                        xs = X[:, g * G + 2 * c:g * G + 2 * c + 2, :].rearrange("p b d -> p (b d)")
                        last = nc.vector.tensor_tensor(xs, xs, out_ps[c][:, :], ALU.add)
                    last.then_inc(added, 1)
                if k % NG == 2 and inside(i, k + 6):
                    w_multiply(dve, i, (k + 6) // NG)
                if k % NG == 0 and inside(i, k):
                    hq = k // NG
                    dve.wait_ge(o_in[hq % 2], i * 16 + (hq // 2 + 1) * 16)
                    if hq or not isinstance(i, int) or i:
                        dve.wait_ge(olo_done, i * 2 + hq)
                    nc.vector.tensor_tensor(o_full[:, :], o_raw[:, hq % 2, 0, :], o_raw[:, hq % 2, 1, :], ALU.mult)\
                        .then_inc(ofull_done, 1)
                if inside(i, k):
                    dve.wait_ge(exped, i * (G * BODY) + (G * k + G))
                    nc.vector.reciprocal(recip[:, k % 2, :], sums[:, k % 2, :]).then_inc(recip_done, 1)
                if inside(i, k - 1):
                    dve.wait_ge(hi_done, i * BODY + k)
                    nc.vector.scalar_tensor_tensor(head_lo[:, (k - 1) % 2, :], head_ps[:, :],
                                                   w_bias[:, (k - 1) // NG % 2, 2:3],
                                                   head_hi[:, (k - 1) % 2, :].bitcast(F32),
                                                   ALU.add, ALU.subtract).then_inc(lo_done, 1)

            run(dve, step)

        @block.tensor
        def _(pe):
            def project(i, k):
                g, par = k % NG, k // NG % 2
                toks = slice(g * GT, (g + 1) * GT)
                if g == 0:
                    pe.wait_ge(wlo_done, i * 2 + (k // NG + 1))
                for a in range(2):
                    if not (isinstance(i, int) and i * BODY + k < 1):
                        pe.wait_ge(proj_read, i * (2 * BODY) + (2 * k + a - 1))
                    c = slice(a * DH, (a + 1) * DH)
                    halves(nc, proj_ps[a][:, :],
                           [lambda dt: w_hi[:, par, dt, c], lambda dt: w_lo[:, par, dt, c]],
                           [lambda dt: XTh[:, dt, toks], lambda dt: XTl[:, dt, toks]], DT).then_inc(projected, 1)

            def project_values(i, k, half):
                if k % BODY == 0 and half == 0:
                    pe.wait_ge(wvlo_done, i + (k // BODY + 1))
                if not (isinstance(i, int) and i * BODY + k + half < 1):
                    pe.wait_ge(v_done, rounds(i, k) + half)
                for j in range(2):
                    at = (k % NG * G + 2 * half + j) * T
                    toks = slice(at, at + T)
                    last = halves(nc, v_ps[:, j * V2:(j + 1) * V2],
                                  [lambda dt: XTh[:, dt, toks], lambda dt: XTl[:, dt, toks]],
                                  [lambda dt: wv_hi[:, dt, :], lambda dt: wv_lo[:, dt, :]], DT)
                last.then_inc(v_projected, 1)

            for k in range(2):
                project(0, k)
                for half in range(2):
                    project_values(0, k, half)

            def step(i, k):
                if inside(i, k):
                    if not (isinstance(i, int) and i * BODY + k < 1):
                        pe.wait_ge(exped, i * (G * BODY) + G * k)
                    pe.wait_ge(proj_read, i * (2 * BODY) + (2 * k + 2))
                    for j in range(G):
                        toks = slice(j * T, (j + 1) * T)
                        last = nc.tensor.matmul(s_ps[:, toks], qT[:, k % 4, toks], kT[:, k % 4, toks],
                                                start=True, stop=True)
                    last.then_inc(scored, 1)
                if inside(i, k - 1):
                    pe.wait_ge(normed_done, i * BODY + k)
                    for j in range(G):
                        last = nc.tensor.transpose(nT_ps[:, j * T:(j + 1) * T], normed[:, (k - 1) % 2, j, :], ident[:, :])
                    last.then_inc(turned, 1)
                if inside(i, k + 2):
                    project(i, k + 2)
                    if has_values(k + 2):
                        project_values(i, k + 2, 0)
                if inside(i, k - 1):
                    pe.wait_ge(nT_done, i * BODY + k)
                    if inside(i, k - 2):
                        pe.wait_ge(lo_done, i * BODY + (k - 1))
                    pe.wait_ge(v_done, rounds(i, k - 1) + 2)
                    pair = slice((k - 1) // NG % 2 * DH, ((k - 1) // NG % 2 + 1) * DH)
                    for j in range(G):
                        toks = slice(j * T, (j + 1) * T)
                        last = nc.tensor.matmul(head_ps[:, toks], v[:, (k - 1) % NG, j, pair], normedT[:, (k - 1) % 2, toks],
                                                start=True, stop=True)
                    last.then_inc(valued, 1)
                if inside(i, k + 2) and has_values(k + 2):
                    project_values(i, k + 2, 1)
                if inside(i, k - 2):
                    q, hq = (k - 2) % 2, (k - 2) // NG
                    pe.wait_ge(lo_done, i * BODY + (k - 1))
                    pe.wait_ge(olo_done, i * 2 + (hq + 1))
                    if inside(i, k - 3):
                        pe.wait_ge(added, i * BODY + (k - 2))
                    for j in range(G):
                        toks = slice(j * T, (j + 1) * T)
                        last = halves(nc, out_ps[j // 2][:, (j % 2) * D:(j % 2 + 1) * D],
                                      [lambda n: head_hi[:, q, toks], lambda n: head_lo[:, q, toks]],
                                      [lambda n: o_hi[:, hq % 2, :], lambda n: o_lo[:, hq % 2, :]], 1)
                    last.then_inc(multiplied, 1)

            run(pe, step)


def stage_wkv1(nc, env, inp):
    X, XTk, ident = env["X"], env["XTk"], env["ident"]
    LOW = -1e38
    with ExitStack() as ctx:
        m = Mem(nc, ctx)
        values, decay, first = env["values"], env["decay"], env["first"]
        exp_decay = m.sb("k1_exp_decay", [P, DT])
        w = m.sb("k1_w", [P, DT])
        w_row = m.sb("k1_w_row", [P, DT, G, T + 1])
        pp = m.sb("k1_pp", [P, 2, G, T + 1])
        aa = m.sb("k1_aa", [P, G, T + 1])
        bb = m.sb("k1_bb", [P, G, T + 1])
        q = m.sb("k1_q", [P, G, T])
        d_out = m.sb("k1_d_out", [P, 2, 2, G, T])
        d_next = m.sb("k1_d_next", [P, 2, 2, G, T])
        e_out = m.sb("k1_e_out", [P, 2, 2, G, T])
        e_next = m.sb("k1_e_next", [P, 2, 2, G, T + 1])
        ev_next = m.sb("k1_ev_next", [P, 2, G, T + 1])
        ev_out = m.sb("k1_ev_out", [P, 2, G, T])
        num = m.sb("k1_num", [P, G, T])
        den = m.sb("k1_den", [P, G, T])
        num_sum = m.sb("k1_num_sum", [P, G, T])
        den_sum = m.sb("k1_den_sum", [P, G, T])
        den_inv = m.sb("k1_den_inv", [P, G, T])
        y = m.sb("k1_y", [P, 2, G, T])
        y_ps = [m.ps(f"k1_y_ps{i}", [P, BANK]) for i in range(2)]
        exp_decay_done = m.sem("k1_exp_decay_done")
        w_done = m.sem("k1_w_done")
        row_done = m.sem("k1_row_done")
        starts = m.sem("k1_starts")
        pp_done = m.sem("k1_pp_done")
        q_done = m.sem("k1_q_done")
        dve_exponents = m.sem("k1_dve_exponents")
        pool_exponents = m.sem("k1_pool_exponents")
        next_done = m.sem("k1_next_done")
        out_done = m.sem("k1_out_done")
        ev_next_done = m.sem("k1_ev_next_done")
        ev_out_done = m.sem("k1_ev_out_done")
        scanned = m.sem("k1_scanned")
        weighted = m.sem("k1_weighted")
        summed = m.sem("k1_summed")
        inverted = m.sem("k1_inverted")
        num_weighted = m.sem("k1_num_weighted")
        num_done = m.sem("k1_num_done")
        y_done = m.sem("k1_y_done")
        turned = m.sem("k1_turned")
        added = m.sem("k1_added")
        block = ctx.enter_context(nc.Block())

        def group(g, n):
            return slice(g * n, (g + 1) * n) if isinstance(g, int) else bass.ds(g * n, n)

        def k_of(g, ct):
            return XTk[:, ct, group(g, G), 1:T + 1]

        def v_of(g, ct):
            return values[:, ct, group(g, GT)].rearrange("p (b t) -> p b t", b=G)

        def flat(ap):
            return ap.rearrange("p b t -> p (b t)")

        @block.scalar
        def _(act):
            nc.scalar.activation(exp_decay[:, :], decay[:, :], ACT.Exp).then_inc(exp_decay_done, 1)
            with act.Fori(0, NG) as g:
                for ct in range(DT):
                    act.wait_ge(dve_exponents, g * (2 * DT) + (2 * ct + 2))
                    act.wait_ge(pool_exponents, g * (2 * DT) + (2 * ct + 3))
                    act.wait_ge(y_done, g * DT + (ct + 1))
                    nc.scalar.activation(e_next[:, ct, :, :, 1:T + 1].rearrange("p k b t -> p (k b) t"),
                                         d_next[:, ct, :, :, :].rearrange("p k b t -> p (k b) t"), ACT.Exp)\
                        .then_inc(next_done, 1)
                    nc.scalar.activation(e_out[:, ct, :, :, :], d_out[:, ct, :, :, :], ACT.Exp).then_inc(out_done, 1)

        @block.gpsimd
        def _(pool):
            pool.wait_ge(exp_decay_done, 1)
            nc.gpsimd.tensor_scalar(w[:, :], exp_decay[:, :], -1.0, None, ALU.mult).then_inc(w_done, 1)
            pool.wait_ge(w_done, 1)
            for ct in range(DT):
                nc.gpsimd.tensor_copy(w_row[:, ct, :, 1:T + 1], w[:, ct:ct + 1].unsqueeze(2).broadcast_to([P, G, T]))\
                    .then_inc(row_done, 1)
                nc.gpsimd.memset(w_row[:, ct, :, 0:1], LOW).then_inc(row_done, 1)
                nc.gpsimd.memset(XTk[:, ct, :, 0:1], LOW).then_inc(starts, 1)
                nc.gpsimd.memset(ev_next[:, ct, :, 0:1], 0.0).then_inc(starts, 1)
                for k in range(2):
                    nc.gpsimd.memset(e_next[:, ct, k, :, 0:1], 0.0).then_inc(starts, 1)

            def exponents(g, ct):
                pool.wait_ge(q_done, g * DT + (ct + 1))
                pool.wait_ge(next_done, g * DT + (ct + 1))
                hold(pool)
                nc.gpsimd.tensor_tensor(d_next[:, ct, 1, :, :], k_of(g, ct), pp[:, ct, :, 1:T + 1], ALU.subtract)\
                    .then_inc(pool_exponents, 1)
                pool.wait_ge(out_done, g * DT + (ct + 1))
                nc.gpsimd.tensor_tensor(d_out[:, ct, 0, :, :], pp[:, ct, :, 0:T], q[:, :, :], ALU.subtract)\
                    .then_inc(pool_exponents, 1)

            def weigh(g, ct):
                pool.wait_ge(next_done, g * DT + (ct + 3))
                pool.wait_ge(y_done, g * DT + (ct + 1))
                hold(pool)
                nc.gpsimd.tensor_tensor(ev_next[:, ct, :, 1:T + 1], e_next[:, ct, 1, :, 1:T + 1], v_of(g, ct), ALU.mult)\
                    .then_inc(ev_next_done, 1)
                pool.wait_ge(out_done, g * DT + (ct + 3))
                hold(pool)
                nc.gpsimd.tensor_tensor(ev_out[:, ct, :, :], e_out[:, ct, 1, :, :], v_of(g, ct), ALU.mult)\
                    .then_inc(ev_out_done, 1)

            def numerate(g, ct):
                n = g * DT + ct
                pool.wait_ge(scanned, n * 2 + 2)
                nc.gpsimd.tensor_tensor(num[:, :, :], e_out[:, ct, 0, :, :], aa[:, :, 0:T], ALU.mult).then_inc(num_weighted, 1)
                pool.wait_ge(num_weighted, n + 1)
                pool.wait_ge(ev_out_done, n + 1)
                pool.wait_ge(y_done, n + 2)
                nc.gpsimd.tensor_tensor(num_sum[:, :, :], num[:, :, :], ev_out[:, ct, :, :], ALU.add).then_inc(num_done, 1)

            pool.sem_inc(next_done, 2)
            pool.sem_inc(out_done, 2)
            exponents(0, 0)
            with pool.Fori(0, NG - 1) as g:
                exponents(g, 1)
                weigh(g, 0)
                numerate(g, 0)
                exponents(g + 1, 0)
                weigh(g, 1)
                numerate(g, 1)
            exponents(NG - 1, 1)
            for ct in range(DT):
                weigh(NG - 1, ct)
                numerate(NG - 1, ct)

        @block.vector
        def _(dve):
            def exponents(g, ct):
                dve.wait_ge(pool_exponents, g * (2 * DT) + (2 * ct + 1))
                hold(dve)
                nc.vector.tensor_tensor_scan(flat(pp[:, ct, :, :]), flat(w_row[:, ct, :, :]),
                                             flat(XTk[:, ct, group(g, G), :]), LOW,
                                             ALU.add, ALU.max).then_inc(pp_done, 1)
                dve.wait_ge(pp_done, g * DT + (ct + 1))
                hold(dve)
                nc.vector.scalar_tensor_tensor(q[:, :, :], k_of(g, ct), first[:, ct:ct + 1], pp[:, ct, :, 0:T],
                                               ALU.add, ALU.max).then_inc(q_done, 1)
                nc.vector.scalar_tensor_tensor(d_next[:, ct, 0, :, :], pp[:, ct, :, 0:T], w[:, ct:ct + 1],
                                               pp[:, ct, :, 1:T + 1], ALU.add, ALU.subtract).then_inc(dve_exponents, 1)
                dve.wait_ge(q_done, g * DT + (ct + 1))
                hold(dve)
                nc.vector.scalar_tensor_tensor(d_out[:, ct, 1, :, :], k_of(g, ct), first[:, ct:ct + 1], q[:, :, :],
                                               ALU.add, ALU.subtract).then_inc(dve_exponents, 1)

            def output(g, ct):
                n = g * DT + ct
                tt = nc.vector.tensor_tensor
                dve.wait_ge(next_done, n + 3)
                nc.vector.tensor_tensor_scan(flat(bb[:, :, :]), flat(e_next[:, ct, 0, :, :]), flat(e_next[:, ct, 1, :, :]), 0.0,
                                             ALU.mult, ALU.add).then_inc(scanned, 1)
                dve.wait_ge(out_done, n + 3)
                dve.wait_ge(scanned, n * 2 + 1)
                tt(den[:, :, :], e_out[:, ct, 0, :, :], bb[:, :, 0:T], ALU.mult).then_inc(weighted, 1)
                dve.wait_ge(ev_next_done, n + 1)
                nc.vector.tensor_tensor_scan(flat(aa[:, :, :]), flat(e_next[:, ct, 0, :, :]), flat(ev_next[:, ct, :, :]), 0.0,
                                             ALU.mult, ALU.add).then_inc(scanned, 1)
                dve.wait_ge(weighted, n + 1)
                tt(den_sum[:, :, :], den[:, :, :], e_out[:, ct, 1, :, :], ALU.add).then_inc(summed, 1)
                dve.wait_ge(summed, n + 1)
                nc.vector.reciprocal(den_inv[:, :, :], den_sum[:, :, :]).then_inc(inverted, 1)
                dve.wait_ge(num_done, n + 1)
                dve.wait_ge(inverted, n + 1)
                dve.wait_ge(turned, n + 1)
                tt(y[:, ct, :, :], num_sum[:, :, :], den_inv[:, :, :], ALU.mult).then_inc(y_done, 1)

            def add(g, ct):
                n = g * DT + ct
                dve.wait_ge(turned, n + 3)
                hold(dve)
                xs = X[:, group(g, G), ct * P:(ct + 1) * P]
                nc.vector.tensor_tensor(xs, xs, y_ps[ct][:, :].rearrange("p (b c) -> p b c", b=G), ALU.add)\
                    .then_inc(added, 1)

            dve.sem_inc(pool_exponents, 1)
            dve.sem_inc(y_done, 2)
            dve.wait_ge(row_done, 2 * DT)
            dve.wait_ge(starts, 4 * DT)
            hold(dve)
            exponents(0, 0)
            exponents(0, 1)
            with dve.Fori(0, NG - 1) as g:
                for ct in range(DT):
                    output(g, ct)
                    exponents(g + 1, ct)
                    add(g, ct)
            for ct in range(DT):
                output(NG - 1, ct)
            for ct in range(DT):
                add(NG - 1, ct)

        @block.tensor
        def _(pe):
            pe.sem_inc(turned, 2)
            pe.sem_inc(added, 2)
            with pe.Fori(0, NG) as g:
                for ct in range(DT):
                    pe.wait_ge(y_done, g * DT + (ct + 3))
                    pe.wait_ge(added, g * DT + (ct + 1))
                    for j in range(G):
                        last = nc.tensor.transpose(y_ps[ct][:, j * P:(j + 1) * P], y[:, ct, j, :], ident[:, :])
                    last.then_inc(turned, 1)


def stage_ffn1(nc, env, inp):
    X, XTh, XTl, ident = env["X"], env["XTh"], env["XTl"], env["ident"]
    E, R = 8, 16
    SCALING = 32.0 / R
    LG = slice(D, D + E)
    LR = slice(D + E, D + E + E * R)
    W = D + E + E * R
    N = B // 2
    with ExitStack() as ctx:
        m = Mem(nc, ctx)
        w_raw, b_raw, bias, rank = env["w_raw"], env["b_raw"], env["bias"], env["rank"]
        w_hi = m.sb("f1_w_hi", [P, DT, W], F32R)
        w_lo = m.sb("f1_w_lo", [P, DT, W], F32R)
        b_hi = m.sb("f1_b_hi", [P, D], F32R)
        b_lo = m.sb("f1_b_lo", [P, D], F32R)
        best = m.sb("f1_best", [P, 2])
        tie = m.sb("f1_tie", [P, 2, E])
        order = m.sb("f1_order", [P, 2, E])
        best_rank = m.sb("f1_best_rank", [P, 2])
        chosen = m.sb("f1_chosen", [P, 2, E])
        low = m.sb("f1_low", [P, 2, 2, E * R])
        low_hi = m.sb("f1_low_hi", [P, 2, 2 * T], F32R)
        low_lo = m.sb("f1_low_lo", [P, 2, 2 * T], F32R)
        in_ps = [m.ps(f"f1_in_ps{i}", [P, 2, BANK]) for i in range(2)]
        lowT_ps = [m.ps(f"f1_lowT_ps{i}", [P, BANK]) for i in range(2)]
        delta_ps = [m.ps(f"f1_delta_ps{i}", [P, 2, D]) for i in range(2)]
        whi_done = m.sem("f1_whi_done")
        wlo_done = m.sem("f1_wlo_done")
        bhi_done = m.sem("f1_bhi_done")
        blo_done = m.sem("f1_blo_done")
        bias_done = m.sem("f1_bias_done")
        multiplied = m.sem("f1_multiplied")
        routed = m.sem("f1_routed")
        low_done = m.sem("f1_low_done")
        turned = m.sem("f1_turned")
        low_hi_done = m.sem("f1_low_hi_done")
        low_lo_done = m.sem("f1_low_lo_done")
        base_added = m.sem("f1_base_added")
        delta_done = m.sem("f1_delta_done")
        delta_added = m.sem("f1_delta_added")
        block = ctx.enter_context(nc.Block())

        @block.gpsimd
        def _(pool):
            nc.gpsimd.tensor_tensor(X[:, :, :], X[:, :, :], bias[:, :].unsqueeze(1).broadcast_to([P, B, D]), ALU.add)\
                .then_inc(bias_done, 1)

        @block.scalar
        def _(act):
            nc.scalar.activation(w_hi[:, :, :], w_raw[:, :, :], ACT.Copy).then_inc(whi_done, 1)
            nc.scalar.activation(b_hi[:, :], b_raw[:, :], ACT.Copy, scale=SCALING).then_inc(bhi_done, 1)
            for u in range(N):
                act.wait_ge(turned, u + 1)
                if u >= 2:
                    act.wait_ge(delta_done, u - 1)
                nc.scalar.activation(low_hi[:, u % 2, :], lowT_ps[u % 2][:, 0:2 * T], ACT.Copy).then_inc(low_hi_done, 1)

        @block.vector
        def _(dve):
            dve.wait_ge(whi_done, 1)
            nc.vector.tensor_tensor(w_lo[:, :, :], w_raw[:, :, :], w_hi[:, :, :].bitcast(F32), ALU.subtract)\
                .then_inc(wlo_done, 1)
            dve.wait_ge(bhi_done, 1)
            nc.vector.scalar_tensor_tensor(b_lo[:, :], b_raw[:, :], SCALING, b_hi[:, :].bitcast(F32), ALU.mult, ALU.subtract)\
                .then_inc(blo_done, 1)
            dve.wait_ge(bias_done, 1)
            tt = nc.vector.tensor_tensor

            def route(u):
                logits = in_ps[u % 2][:, :, LG]
                dve.wait_ge(multiplied, u + 1)
                nc.vector.tensor_reduce(best[:, :], logits, AX_X, ALU.max).then_inc(routed, 1)
                dve.wait_ge(routed, u * 5 + 1)
                tt(tie[:, :, :], logits, best[:, :].unsqueeze(2).broadcast_to([P, 2, E]), ALU.is_equal).then_inc(routed, 1)
                dve.wait_ge(routed, u * 5 + 2)
                tt(order[:, :, :], tie[:, :, :], rank[:, :].unsqueeze(1).broadcast_to([P, 2, E]), ALU.mult)\
                    .then_inc(routed, 1)
                dve.wait_ge(routed, u * 5 + 3)
                nc.vector.tensor_reduce(best_rank[:, :], order[:, :, :], AX_X, ALU.max).then_inc(routed, 1)
                dve.wait_ge(routed, u * 5 + 4)
                tt(chosen[:, :, :], order[:, :, :], best_rank[:, :].unsqueeze(2).broadcast_to([P, 2, E]), ALU.is_equal)\
                    .then_inc(routed, 1)
                dve.wait_ge(routed, u * 5 + 5)
                if u >= 2:
                    dve.wait_ge(turned, u - 1)
                tt(low[:, u % 2, :, :].rearrange("p b (e r) -> p b e r", e=E),
                   in_ps[u % 2][:, :, LR].rearrange("p b (e r) -> p b e r", e=E),
                   chosen[:, :, :].unsqueeze(3).broadcast_to([P, 2, E, R]), ALU.mult).then_inc(low_done, 1)

            for u in range(N + 2):
                if u < N:
                    xs = X[:, 2 * u:2 * u + 2, :]
                    route(u)
                    tt(xs, xs, in_ps[u % 2][:, :, 0:D], ALU.add).then_inc(base_added, 1)
                if 1 <= u <= N:
                    p = (u - 1) % 2
                    dve.wait_ge(low_hi_done, u)
                    tt(low_lo[:, p, :], lowT_ps[p][:, 0:2 * T], low_hi[:, p, :].bitcast(F32), ALU.subtract)\
                        .then_inc(low_lo_done, 1)
                if u >= 2:
                    xs = X[:, 2 * u - 4:2 * u - 2, :]
                    dve.wait_ge(delta_done, u - 1)
                    tt(xs, xs, delta_ps[u % 2][:, :, :], ALU.add).then_inc(delta_added, 1)

        @block.tensor
        def _(pe):
            def multiply(u):
                if u >= 2:
                    pe.wait_ge(base_added, u - 1)
                for r in range(2):
                    toks = slice((2 * u + r) * T, (2 * u + r + 1) * T)
                    last = halves(nc, in_ps[u % 2][:, r, 0:W], [lambda dt: XTh[:, dt, toks], lambda dt: XTl[:, dt, toks]],
                                  [lambda dt: w_hi[:, dt, :], lambda dt: w_lo[:, dt, :]], DT)
                last.then_inc(multiplied, 1)

            pe.wait_ge(wlo_done, 1)
            multiply(0)
            pe.wait_ge(blo_done, 1)
            for u in range(N + 1):
                if u + 1 < N:
                    multiply(u + 1)
                if u < N:
                    pe.wait_ge(low_done, u + 1)
                    if u >= 2:
                        pe.wait_ge(low_lo_done, u - 1)
                    for r in range(2):
                        last = nc.tensor.transpose(lowT_ps[u % 2][:, r * T:(r + 1) * T], low[:, u % 2, r, :], ident[:, :])
                    last.then_inc(turned, 1)
                if u >= 1:
                    p = (u - 1) % 2
                    pe.wait_ge(low_lo_done, u)
                    if u >= 3:
                        pe.wait_ge(delta_added, u - 2)
                    for r in range(2):
                        toks = slice(r * T, (r + 1) * T)
                        last = halves(nc, delta_ps[p][:, r, :], [lambda n: low_hi[:, p, toks], lambda n: low_lo[:, p, toks]],
                                      [lambda n: b_hi[:, :], lambda n: b_lo[:, :]], 1)
                    last.then_inc(delta_done, 1)


def program(nc, inp, out):
    with ExitStack() as ctx:
        m = Mem(nc, ctx)
        env = {
            "X": m.sb("X", [P, B, D]),
            "XTh": m.sb("XTh", [P, DT, B * T], F32R),
            "XTl": m.sb("XTl", [P, DT, B * T], F32R),
            "ident": m.sb("ident", [P, P]),
            "ones": m.sb("ones", [P, P]),
            "minus_half": m.sb("minus_half", [P, 16]),
        }
        with ExitStack() as c0:
            env["OT"] = Mem(nc, c0).sb("OT", [P, B, REP0 * T])
            n0 = Mem(nc, c0)
            env["wo_raw"] = n0.sb("n0_wo_raw", [P, REP0, D])
            env["gn_w"] = n0.sb("n0_gn_w", [P, REP0])
            env["gn_b"] = n0.sb("n0_gn_b", [P, REP0])
            env["share"] = n0.sb("n0_share", [P, P])
            with ExitStack() as c1:
                a0 = Mem(nc, c1)
                env["Q"] = a0.sb("Q", [P, B, REP0, T])
                env["K"] = a0.sb("K", [P, B * T])
                env["V"] = a0.sb("V", [P, B, P])
                env["sign"] = a0.sb("sign", [P, KV0, 2])
                env["ident_b"] = a0.sb("ident_b", [P, P], BF16)
                env["causal"] = a0.sb("causal", [P, 4, T], BF16)
                env["row_mask"] = a0.sb("row_mask", [P, 2 * KV0])
                stage_attn0_project(nc, env, inp)
                stage_attn0_heads(nc, env, inp)
            stage_attn0_out(nc, env, inp)
        with ExitStack() as c0:
            env["XTf"] = Mem(nc, c0).sb("XTf", [P, DT, B * T])
            env["C"] = Mem(nc, c0).sb("C", [P, DT, T, B])
            env["Z"] = Mem(nc, c0).sb("Z", [P, DT, B, T])
            stage_norm(nc, env, "ln0", "whole",
                       loads=[(env["C"][:, :, :, :].rearrange("p m t b -> p (m t b)"), inp["c0_ctx"])])
            stage_conv0(nc, env, inp)
            stage_conv0_out(nc, env)
        with ExitStack() as c0:
            m0 = Mem(nc, c0)
            env["w_raw"] = m0.sb("m0_w_raw", [P, 2, DT, 3 * D])
            env["r_raw"] = m0.sb("m0_r_raw", [P, DT, P])
            env["r_scale"] = m0.sb("m0_r_scale", [P, DT])
            env["rank"] = m0.sb("m0_rank", [P, 8])
            env["per_expert"] = m0.sb("m0_per_expert", [P, 8])
            stage_norm(nc, env, "ln1", "halves", loads=[
                (env["r_raw"][:, :, :], inp["m0_router"].rearrange("(k p) e -> p k e", p=P)),
                (env["r_scale"][:, :], inp["m0_router_scale"]),
                (env["rank"][:, :], inp["m0_rank"].partition_broadcast(P)),
                (env["per_expert"][:, :], inp["m0_per_expert"].partition_broadcast(P))]
                + [(env["w_raw"][:, e, :, :], inp["m0_w"][e].rearrange("(k p) n -> p k n", p=P)) for e in range(2)])
            stage_moe0(nc, env, inp)
        with ExitStack() as c1:
            a1 = Mem(nc, c1)
            env["w_raw"] = a1.sb("a1_w_raw", [P, 2, DT, 2, 2 * P])
            env["wv_raw"] = a1.sb("a1_wv_raw", [P, DT, 2, 2 * P])
            env["w_bias"] = a1.sb("a1_w_bias", [P, 2, 3])
            env["o_raw"] = a1.sb("a1_o_raw", [P, 2, 2, D])
            loads = [(env["w_raw"][:, h, :, :, :].rearrange("p k a n -> p k (a n)"),
                      inp["a1_w"][h].rearrange("(k p) n -> p k n", p=P)) for h in range(2)]
            loads += [(env["w_bias"][:, h, :], inp["a1_bias"][h]) for h in range(2)]
            loads += [(env["o_raw"][:, h, :, :].rearrange("p a n -> p (a n)"), inp["a1_wo"][h]) for h in range(2)]
            loads += [(env["wv_raw"][:, :, :, :].rearrange("p k a n -> p k (a n)"),
                       inp["a1_wv"][0].rearrange("(k p) n -> p k n", p=P))]
            stage_norm(nc, env, "ln2", "halves", loads=loads)
            stage_attn1(nc, env, inp)
        with ExitStack() as c1:
            env["XTk"] = Mem(nc, c1).sb("XTk", [P, DT, B, T + 1])
            k1 = Mem(nc, c1)
            env["values"] = k1.sb("k1_values", [P, DT, B * T])
            env["decay"] = k1.sb("k1_decay", [P, DT])
            env["first"] = k1.sb("k1_first", [P, DT])
            stage_norm(nc, env, "ln3", "spaced", loads=[
                (env["decay"][:, :], inp["k1_decay"]),
                (env["first"][:, :], inp["k1_first"]),
                (env["values"][:, :, :], inp["ctxT"].rearrange("k p n -> p k n"))])
            stage_wkv1(nc, env, inp)
        with ExitStack() as c1:
            f1 = Mem(nc, c1)
            env["w_raw"] = f1.sb("f1_w_raw", [P, DT, D + 8 + P])
            env["b_raw"] = f1.sb("f1_b_raw", [P, D])
            env["bias"] = f1.sb("f1_bias", [P, D])
            env["rank"] = f1.sb("f1_rank", [P, 8])
            stage_norm(nc, env, "ln4", "halves", loads=[
                (env["w_raw"][:, :, :], inp["f1_w"].rearrange("(k p) n -> p k n", p=P)),
                (env["b_raw"][:, :], inp["f1_b"]),
                (env["bias"][:, :], inp["f1_bias"].partition_broadcast(P)),
                (env["rank"][:, :], inp["m0_rank"].partition_broadcast(P))])
            stage_ffn1(nc, env, inp)
        stage_norm(nc, env, "ln5", None, out=out)


def rope_rows(w, kv, rep):
    import numpy as np
    c = w.reshape(D, kv, rep, 2, DH0)
    partner = c[..., np.arange(DH0) ^ 1]
    tiles = []
    for j in range(rep):
        tiles += [c[:, :, j].reshape(D, P), partner[:, :, j].reshape(D, P)]
    return tiles


def head_rows(w):
    return w.reshape(KV0, REP0, 2 * DH0, -1).swapaxes(0, 1).reshape(w.shape)


def per_head(w):
    return w.reshape(2, D, -1, P).transpose(2, 1, 0, 3)


def kernel(**inputs):
    import numpy as np
    import concourse.bacc as bacc
    from concourse.bass_utils import run_bass_kernel_spmd
    a = {k: np.asarray(v) for k, v in inputs.items()}
    wq = rope_rows(a["L0_attn_Wq"], KV0, REP0)
    wk = rope_rows(a["L0_attn_Wk"], KV0, 1)
    inv = (1.0 / np.float32(10000.0) ** (np.arange(0, DH0, 2, dtype=np.float32) / np.float32(DH0))).astype(np.float32)
    freqs = (np.arange(T, dtype=np.float32)[:, None] * inv[None, :]).astype(np.float32)
    d = np.arange(P) % DH0
    sign = np.where(d % 2 == 0, -1.0, 1.0).astype(np.float32)
    rows = np.arange(P) // (2 * DH0)
    arrays = {
        "x": a["x"],
        "xT": a["x"].reshape(B * T, DT, P).transpose(1, 2, 0),
        "a0_w": np.concatenate(wk + [a["L0_attn_Wv"]] + wq, axis=1).reshape(DT, P, -1),
        "a0_wo": head_rows(a["L0_attn_Wo"]),
        "cos": np.cos(freqs).T[d // 2],
        "sin": np.sin(freqs).T[d // 2] * sign[:, None],
        "row_mask": (np.arange(P)[:, None] // DH0 == np.arange(2 * KV0)).astype(np.float32) * np.float32(DH0 ** -0.5),
        "share": (rows[:, None] == rows[None, :]).astype(np.float32) / np.float32(2 * DH0),
        "lambdas": np.concatenate([a[f"L0_attn_lambda_{n}"] for n in ("q1", "k1", "q2", "k2")]),
        "gn_w": head_rows(a["L0_attn_gn_w"]).reshape(-1, P).T,
        "gn_b": head_rows(a["L0_attn_gn_b"]).reshape(-1, P).T,
        "ident": np.eye(P, dtype=np.float32),
        "anti": np.eye(P, dtype=np.float32)[::-1],
        "c0_ctx": a["ctx_2048"].reshape(B, T, DT, P)[..., ::-1].transpose(3, 2, 1, 0).reshape(P, -1),
        "c0_D": a["L0_xattn_D"],
        "m0_router": np.pad(a["L0_ffn_router_logits"], ((0, 0), (0, P - 8))),
        "m0_router_scale": a["L0_ffn_router_scale"].reshape(DT, P).T,
        "m0_rank": np.arange(8, 0, -1).astype(np.float32),
        "m0_per_expert": a["L0_ffn_per_expert_scale"],
        "a1_w": np.stack([per_head(np.stack([a[f"L1_attn_w{n}_codes"], a[f"L1_attn_w{n}_scales"].repeat(32, axis=0)]))
                          for n in "qk"], axis=3).reshape(16, D, 2 * 2 * P),
        "a1_wv": np.stack([a["L1_attn_wv_codes"], a["L1_attn_wv_scales"].repeat(32, axis=0)])
                   .reshape(2, D, 8, 2 * P).transpose(2, 1, 0, 3).reshape(8, D, 2 * 2 * P),
        "a1_bias": np.stack([a[f"L1_attn_b{n}"].reshape(16, P) for n in "qkv"], axis=2),
        "a1_wo": np.stack([a["L1_attn_wo_codes"], a["L1_attn_wo_scales"].repeat(32, axis=0)], axis=1).reshape(16, P, 2 * D),
        "a1_bo": a["L1_attn_bo"],
        "m0_w": np.concatenate([a["L0_ffn_gating_einsum"].transpose(0, 3, 1, 2).reshape(8, D, 2 * D),
                                a["L0_ffn_linear"]], axis=2),
        "ctxT": a["ctx_2048"].reshape(B * T, DT, P).transpose(1, 2, 0),
        "k1_decay": a["L1_xattn_time_decay"].reshape(DT, P).T,
        "k1_first": a["L1_xattn_time_first"].reshape(DT, P).T,
        "f1_w": np.concatenate([a["L1_ffn_W_base"].T, a["L1_ffn_router_W"].T,
                                a["L1_ffn_A"].reshape(8 * 16, D).T], axis=1),
        "f1_b": a["L1_ffn_Bw"].transpose(0, 2, 1).reshape(8 * 16, D),
        "f1_bias": a["L1_ffn_b_base"],
        "toeplitz": np.pad(a["L0_xattn_ssm_kernel"], ((0, 0), (P - 1, 0)))[:, np.arange(P)[:, None] + np.arange(D)],
    }
    arrays = {k: np.ascontiguousarray(v) for k, v in arrays.items()}
    nc = bacc.Bacc("TRN2", target_bir_lowering=False, num_devices=1)
    inp = {k: nc.dram_tensor(f"in_{k}", v.shape, mybir.dt.from_np(v.dtype), kind="ExternalInput").ap() for k, v in arrays.items()}
    out = nc.dram_tensor("out", (B, T, D), F32, kind="ExternalOutput").ap()
    program(nc, inp, out)
    r = run_bass_kernel_spmd(nc, [{f"in_{k}": v for k, v in arrays.items()}], core_ids=[0])
    return r.results[0]["out"]
```
